# Optimizing a Trainium2 kernel written in Bass

```python
import numpy as np
import jax
import jax.numpy as jnp

def _softmax(x, axis=-1):
    return jax.nn.softmax(x, axis=axis)

def _gelu(x):
    return jax.nn.gelu(x, approximate=True)

def _silu(x):
    return jax.nn.silu(x)

def _sigmoid(x):
    return jax.nn.sigmoid(x)

def _layernorm(x, axis=-1, eps=1e-05):
    m = jnp.mean(x, axis=axis, keepdims=True)
    v = jnp.var(x, axis=axis, keepdims=True)
    return (x - m) / jnp.sqrt(v + eps)

def _scatter_add(tgt, idx, src, axis=0):
    return tgt.at[idx].add(src)

def _segment_sum(src, seg, n):
    return jax.ops.segment_sum(src, seg, n)
kernel_name = 'mk_flamingo_gated_d2_seqx_r4_c39763'

def setup_inputs(seed: int=0):
    np.random.seed(seed)
    _w = jnp.asarray

    def _rec_inputs():
        import jax
        import jax.numpy as jnp
        _rk = jax.random.key(seed)
        x = -0.0003929 + 0.9999 * jax.random.normal(jax.random.fold_in(_rk, 1), (16, 128, 256), jnp.float32)
        _lenS = 128 - jax.random.randint(jax.random.fold_in(_rk, 7), (16,), 0, max(1, 128 // 4) + 1, jnp.int32)
        _lenS2 = 128 - jax.random.randint(jax.random.fold_in(_rk, 8), (16,), 0, max(1, 128 // 4) + 1, jnp.int32)
        _ctx_2048P = jax.random.normal(jax.random.fold_in(_rk, 11), (16, 16, 512), jnp.float32)
        _ctx_2048c = jax.random.dirichlet(jax.random.fold_in(_rk, 511), 0.3 * jnp.ones((16,), jnp.float32), (16, 128))
        _ctx_2048t = jnp.einsum('bsk,bkd->bsd', _ctx_2048c, _ctx_2048P)
        _ctx_2048t = _ctx_2048t * jax.lax.rsqrt(jnp.mean(jnp.square(_ctx_2048t)) + 1e-12) * 0.953939
        ctx_2048 = 4.13588e-05 + 0.999923 * (_ctx_2048t + 0.3 * jax.random.normal(jax.random.fold_in(_rk, 611), (16, 128, 512), jnp.float32))
        _validS = jnp.arange(128)[None, :] < _lenS[:, None]
        _validS2 = jnp.arange(128)[None, :] < _lenS2[:, None]
        _causal = jnp.tril(jnp.ones((128, 128), dtype=bool))
        mask_BxS2_if0 = jnp.where(jnp.ones((16, 128), dtype=bool), 4, 0).astype(jnp.int32)
        _g = jax.random.normal(jax.random.fold_in(_rk, 9001), (2, 2), jnp.float32)
        _g = jnp.sign(_g) * jnp.maximum(jnp.abs(_g), 1.0) + (_g == 0) * 1.0
        g_xattn = _g[0]
        g_ffn = _g[1]
        return (x, ctx_2048, mask_BxS2_if0, g_xattn, g_ffn)
    x, ctx_2048, mask_BxS2_if0, g_xattn, g_ffn = _rec_inputs()

    def _L0_xattn_setup():
        import jax, jax.numpy as jnp
        import numpy as np
        B, L, P = (4, 1024, 256)
        D_MODEL = 256
        D_GLOBAL = 512
        HEADDIM = 32
        EPSILON = 0.001
        RMS_EPS = 1e-05

        def rmsnorm(x, g, eps=RMS_EPS):
            var = jnp.mean(jnp.square(x), axis=-1, keepdims=True)
            return x * jax.lax.rsqrt(var + eps) * g

        def _hnet_depool(h, h_patch_full, patch_lens):
            h_patch = h_patch_full[..., :D_MODEL]
            bsz, plen = (h_patch.shape[0], h_patch.shape[1])
            seqlen = h.shape[1]
            logp = jnp.full((bsz, plen), -EPSILON, dtype=jnp.float32)
            bidx = jnp.cumsum(patch_lens, axis=1) - 1
            boundary_mask = jnp.zeros((bsz, seqlen), dtype=jnp.int32)
            boundary_mask = boundary_mask.at[jnp.arange(bsz)[:, None], bidx].set(1)
            dt = (-jnp.log(-jnp.expm1(logp))).astype(h_patch.dtype)
            x = h_patch / dt[..., None]
            n_heads = D_MODEL // HEADDIM
            A = -jnp.ones((n_heads,), dtype=jnp.float32)
            bcoef = jnp.exp(logp).astype(h_patch.dtype)
            x4 = x.reshape(bsz, plen, n_heads, HEADDIM)
            a = jnp.exp(dt[:, :, None] * A[None, None, :])
            u = (dt * bcoef)[:, :, None, None] * x4
            a_b = jnp.broadcast_to(a[..., None], u.shape)

            def comb(lft, rgt):
                aL, uL = lft
                aR, uR = rgt
                return (aL * aR, uL * aR + uR)
            _, s = jax.lax.associative_scan(comb, (a_b, u), axis=1)
            depool = s.reshape(bsz, plen, D_MODEL)
            plug = jnp.clip(jnp.cumsum(boundary_mask, axis=1) - 1, 0, plen - 1)
            depool_out = depool[jnp.arange(bsz)[:, None], plug]
            return depool_out + h
        key = jax.random.key(seed)
        k1, k2, k3, k4 = jax.random.split(key, 4)
        embeds = jax.random.normal(k1, (B, L, D_MODEL), dtype=jnp.float32)
        patch_embeds = jax.random.normal(k2, (B, P, D_GLOBAL), dtype=jnp.float32)
        patch_lens = jnp.full((B, P), L // P, dtype=jnp.int64)
        W_in = jax.random.normal(k3, (D_MODEL, D_MODEL), dtype=jnp.float32) * 0.02
        b_in = jnp.zeros((D_MODEL,), dtype=jnp.float32)
        g_res = jnp.ones((D_MODEL,), dtype=jnp.float32)
        g_init = jnp.ones((D_GLOBAL,), dtype=jnp.float32)
        return {'embeds': embeds, 'patch_embeds': patch_embeds, 'patch_lens': patch_lens, 'W_in': W_in, 'b_in': b_in, 'g_res': g_res, 'g_init': g_init}
    _L0_xattn_all = _L0_xattn_setup()
    _L0_xattn_in = {k: v for k, v in _L0_xattn_all.items() if k in ('W_in', 'b_in', 'g_res', 'g_init')}
    del _L0_xattn_all

    def _L0_ffn_setup():
        import jax, jax.numpy as jnp
        import numpy as np
        NUM_EXPERTS = 8
        TOP_K = 2
        D_MODEL = 256
        D_HID = 1024
        BATCH, SEQ = (2, 512)
        key = jax.random.key(seed)
        ks = jax.random.split(key, 5)
        s = 0.02
        return {'x': jax.random.normal(ks[0], (BATCH, SEQ, D_MODEL), dtype=jnp.float32), 'Wg': jax.random.normal(ks[1], (D_MODEL, NUM_EXPERTS), dtype=jnp.float32) * s, 'bg': jnp.zeros((NUM_EXPERTS,), dtype=jnp.float32), 'W0': jax.random.normal(ks[2], (NUM_EXPERTS, D_MODEL, D_HID), dtype=jnp.float32) * s, 'b0': jnp.zeros((NUM_EXPERTS, D_HID), dtype=jnp.float32), 'W1': jax.random.normal(ks[3], (NUM_EXPERTS, D_MODEL, D_HID), dtype=jnp.float32) * s, 'b1': jnp.zeros((NUM_EXPERTS, D_HID), dtype=jnp.float32), 'W2': jax.random.normal(ks[4], (NUM_EXPERTS, D_HID, D_MODEL), dtype=jnp.float32) * s, 'b2': jnp.zeros((NUM_EXPERTS, D_MODEL), dtype=jnp.float32)}
    _L0_ffn_all = _L0_ffn_setup()
    _L0_ffn_in = {k: v for k, v in _L0_ffn_all.items() if k in ('Wg', 'bg', 'W0', 'b0', 'W1', 'b1', 'W2', 'b2')}
    del _L0_ffn_all

    def _L1_xattn_setup():
        import jax, jax.numpy as jnp
        import numpy as np
        B, N, DIM = (8, 1024, 256)
        M, CTX = (64, 512)
        HEADS, DH = (16, 64)
        INNER = HEADS * DH
        EPS = 1e-06

        def _split_heads(t):
            b, n, _ = t.shape
            return t.reshape(b, n, HEADS, DH).transpose(0, 2, 1, 3)
        key = jax.random.key(seed)
        ks = jax.random.split(key, 6)
        x = jax.random.normal(ks[0], (B, N, DIM), dtype=jnp.float32)
        context = jax.random.normal(ks[1], (B, M, CTX), dtype=jnp.float32)
        Wq = jax.random.normal(ks[2], (DIM, INNER), dtype=jnp.float32) / np.sqrt(DIM)
        Wkv = jax.random.normal(ks[3], (CTX, 2 * INNER), dtype=jnp.float32) / np.sqrt(CTX)
        null_kv = jax.random.normal(ks[4], (2, DH), dtype=jnp.float32) / np.sqrt(2.0)
        Wout = jax.random.normal(ks[5], (INNER, DIM), dtype=jnp.float32) / np.sqrt(INNER)
        ln_scale = jnp.ones((DIM,), dtype=jnp.float32)
        ln_bias = jnp.zeros((DIM,), dtype=jnp.float32)
        return {'x': x, 'context': context, 'Wq': Wq, 'Wkv': Wkv, 'null_kv': null_kv, 'Wout': Wout, 'ln_scale': ln_scale, 'ln_bias': ln_bias}
    _L1_xattn_all = _L1_xattn_setup()
    _L1_xattn_in = {k: v for k, v in _L1_xattn_all.items() if k in ('Wq', 'Wkv', 'null_kv', 'Wout', 'ln_scale', 'ln_bias')}
    del _L1_xattn_all

    def _L1_ffn_setup():
        import jax, jax.numpy as jnp
        import numpy as np
        import math
        D = 256
        H = 16
        E = 8
        TOPK = 2
        LAT = D // 2
        KPH = LAT // H
        HD = D // H

        def _forward(hs, q_w, q_b, k_w, k_b, v_w, v_b, o_w, o_b, router_w, router_b, w1, b1, w2, b2):
            B, S, _ = hs.shape
            Q = (hs @ q_w + q_b).reshape(B, S, H, HD).transpose(0, 2, 1, 3)
            K = (hs @ k_w + k_b).reshape(B, S, H, KPH).transpose(0, 2, 1, 3)
            V = (hs @ v_w + v_b).reshape(B, S, H, KPH).transpose(0, 2, 1, 3)
            scores = jnp.einsum('bhsk,bhtk->bhst', Q[..., :KPH], K) / math.sqrt(KPH)
            attn = jax.nn.softmax(scores, axis=-1)
            ao = jnp.einsum('bhst,bhtv->bhsv', attn, V)
            ao = ao.transpose(0, 2, 1, 3).reshape(B, S, H * KPH)
            ao = jnp.concatenate([ao, jnp.zeros((B, S, D - LAT), ao.dtype)], axis=-1)
            mla_out = ao @ o_w + o_b
            probs = jax.nn.softmax(mla_out @ router_w + router_b, axis=-1)
            topw, topi = jax.lax.top_k(probs, TOPK)
            topw = topw / (topw.sum(-1, keepdims=True) + 1e-08)
            combine = jnp.sum(jax.nn.one_hot(topi, E, dtype=probs.dtype) * topw[..., None], axis=-2)
            h1 = jnp.einsum('bsd,edf->ebsf', mla_out, w1) + b1[:, None, None, :]
            h1 = jax.nn.gelu(h1, approximate=False)
            h2 = jnp.einsum('ebsf,efd->ebsd', h1, w2) + b2[:, None, None, :]
            moe_out = jnp.einsum('bse,ebsd->bsd', combine, h2)
            return hs + 0.3 * moe_out
        key = jax.random.key(seed)
        ks = jax.random.split(key, 16)
        s = 0.02
        inp = {'hidden_states': jax.random.normal(ks[0], (2, 512, D), jnp.float32), 'q_w': jax.random.normal(ks[1], (D, D), jnp.float32) * s, 'q_b': jnp.zeros((D,), jnp.float32), 'k_w': jax.random.normal(ks[2], (D, LAT), jnp.float32) * s, 'k_b': jnp.zeros((LAT,), jnp.float32), 'v_w': jax.random.normal(ks[3], (D, LAT), jnp.float32) * s, 'v_b': jnp.zeros((LAT,), jnp.float32), 'o_w': jax.random.normal(ks[4], (D, D), jnp.float32) * s, 'o_b': jnp.zeros((D,), jnp.float32), 'router_w': jax.random.normal(ks[5], (D, E), jnp.float32) * s, 'router_b': jnp.zeros((E,), jnp.float32), 'w1': jax.random.normal(ks[6], (E, D, 2 * D), jnp.float32) * s, 'b1': jnp.zeros((E, 2 * D), jnp.float32), 'w2': jax.random.normal(ks[7], (E, 2 * D, D), jnp.float32) * s, 'b2': jnp.zeros((E, D), jnp.float32)}
        return inp
    _L1_ffn_all = _L1_ffn_setup()
    _L1_ffn_in = {k: v for k, v in _L1_ffn_all.items() if k in ('q_w', 'q_b', 'k_w', 'k_b', 'v_w', 'v_b', 'o_w', 'o_b', 'router_w', 'router_b', 'w1', 'b1', 'w2', 'b2')}
    del _L1_ffn_all
    return {'x': x, 'ctx_2048': ctx_2048, 'mask_BxS2_if0': mask_BxS2_if0, 'g_xattn': g_xattn, 'g_ffn': g_ffn, 'L0_xattn_W_in': _L0_xattn_in['W_in'], 'L0_xattn_b_in': _L0_xattn_in['b_in'], 'L0_xattn_g_res': _L0_xattn_in['g_res'], 'L0_xattn_g_init': _L0_xattn_in['g_init'], 'L0_ffn_Wg': _L0_ffn_in['Wg'], 'L0_ffn_bg': _L0_ffn_in['bg'], 'L0_ffn_W0': _L0_ffn_in['W0'], 'L0_ffn_b0': _L0_ffn_in['b0'], 'L0_ffn_W1': _L0_ffn_in['W1'], 'L0_ffn_b1': _L0_ffn_in['b1'], 'L0_ffn_W2': _L0_ffn_in['W2'], 'L0_ffn_b2': _L0_ffn_in['b2'], 'L1_xattn_Wq': _L1_xattn_in['Wq'], 'L1_xattn_Wkv': _L1_xattn_in['Wkv'], 'L1_xattn_null_kv': _L1_xattn_in['null_kv'], 'L1_xattn_Wout': _L1_xattn_in['Wout'], 'L1_xattn_ln_scale': _L1_xattn_in['ln_scale'], 'L1_xattn_ln_bias': _L1_xattn_in['ln_bias'], 'L1_ffn_q_w': _L1_ffn_in['q_w'], 'L1_ffn_q_b': _L1_ffn_in['q_b'], 'L1_ffn_k_w': _L1_ffn_in['k_w'], 'L1_ffn_k_b': _L1_ffn_in['k_b'], 'L1_ffn_v_w': _L1_ffn_in['v_w'], 'L1_ffn_v_b': _L1_ffn_in['v_b'], 'L1_ffn_o_w': _L1_ffn_in['o_w'], 'L1_ffn_o_b': _L1_ffn_in['o_b'], 'L1_ffn_router_w': _L1_ffn_in['router_w'], 'L1_ffn_router_b': _L1_ffn_in['router_b'], 'L1_ffn_w1': _L1_ffn_in['w1'], 'L1_ffn_b1': _L1_ffn_in['b1'], 'L1_ffn_w2': _L1_ffn_in['w2'], 'L1_ffn_b2': _L1_ffn_in['b2']}

def reference(x, ctx_2048, mask_BxS2_if0, g_xattn, g_ffn, L0_xattn_W_in, L0_xattn_b_in, L0_xattn_g_res, L0_xattn_g_init, L0_ffn_Wg, L0_ffn_bg, L0_ffn_W0, L0_ffn_b0, L0_ffn_W1, L0_ffn_b1, L0_ffn_W2, L0_ffn_b2, L1_xattn_Wq, L1_xattn_Wkv, L1_xattn_null_kv, L1_xattn_Wout, L1_xattn_ln_scale, L1_xattn_ln_bias, L1_ffn_q_w, L1_ffn_q_b, L1_ffn_k_w, L1_ffn_k_b, L1_ffn_v_w, L1_ffn_v_b, L1_ffn_o_w, L1_ffn_o_b, L1_ffn_router_w, L1_ffn_router_b, L1_ffn_w1, L1_ffn_b1, L1_ffn_w2, L1_ffn_b2):
    import jax
    import jax.numpy as jnp

    def _L0_xattn_ref(embeds, patch_embeds, patch_lens, W_in, b_in, g_res, g_init):
        import jax, jax.numpy as jnp
        import numpy as np
        B, L, P = (4, 1024, 256)
        D_MODEL = 256
        D_GLOBAL = 512
        HEADDIM = 32
        EPSILON = 0.001
        RMS_EPS = 1e-05

        def rmsnorm(x, g, eps=RMS_EPS):
            var = jnp.mean(jnp.square(x), axis=-1, keepdims=True)
            return x * jax.lax.rsqrt(var + eps) * g

        def _hnet_depool(h, h_patch_full, patch_lens):
            h_patch = h_patch_full[..., :D_MODEL]
            bsz, plen = (h_patch.shape[0], h_patch.shape[1])
            seqlen = h.shape[1]
            logp = jnp.full((bsz, plen), -EPSILON, dtype=jnp.float32)
            bidx = jnp.cumsum(patch_lens, axis=1) - 1
            boundary_mask = jnp.zeros((bsz, seqlen), dtype=jnp.int32)
            boundary_mask = boundary_mask.at[jnp.arange(bsz)[:, None], bidx].set(1)
            dt = (-jnp.log(-jnp.expm1(logp))).astype(h_patch.dtype)
            x = h_patch / dt[..., None]
            n_heads = D_MODEL // HEADDIM
            A = -jnp.ones((n_heads,), dtype=jnp.float32)
            bcoef = jnp.exp(logp).astype(h_patch.dtype)
            x4 = x.reshape(bsz, plen, n_heads, HEADDIM)
            a = jnp.exp(dt[:, :, None] * A[None, None, :])
            u = (dt * bcoef)[:, :, None, None] * x4
            a_b = jnp.broadcast_to(a[..., None], u.shape)

            def comb(lft, rgt):
                aL, uL = lft
                aR, uR = rgt
                return (aL * aR, uL * aR + uR)
            _, s = jax.lax.associative_scan(comb, (a_b, u), axis=1)
            depool = s.reshape(bsz, plen, D_MODEL)
            plug = jnp.clip(jnp.cumsum(boundary_mask, axis=1) - 1, 0, plen - 1)
            depool_out = depool[jnp.arange(bsz)[:, None], plug]
            return depool_out + h
        h = rmsnorm(embeds, g_res)
        h = jnp.einsum('bld,ed->ble', h, W_in) + b_in
        h_patch = rmsnorm(patch_embeds, g_init)
        return _hnet_depool(h, h_patch, patch_lens)

    def _L0_ffn_ref(x, Wg, bg, W0, b0, W1, b1, W2, b2):
        import jax, jax.numpy as jnp
        import numpy as np
        NUM_EXPERTS = 8
        TOP_K = 2
        D_MODEL = 256
        D_HID = 1024
        BATCH, SEQ = (2, 512)
        n, s, d = x.shape
        gate_logits = x @ Wg + bg
        top_vals, top_idx = jax.lax.top_k(gate_logits, TOP_K)
        w = jax.nn.softmax(top_vals, axis=-1)
        combine = jnp.sum(jax.nn.one_hot(top_idx, NUM_EXPERTS, dtype=x.dtype) * w[..., None], axis=-2)
        xf = x.reshape(n * s, d)
        h = jnp.einsum('td,edh->eth', xf, W0) + b0[:, None, :]
        g = jax.nn.silu(jnp.einsum('td,edh->eth', xf, W1) + b1[:, None, :])
        y = jnp.einsum('eth,ehd->etd', h * g, W2) + b2[:, None, :]
        out = jnp.einsum('te,etd->td', combine.reshape(n * s, NUM_EXPERTS), y)
        return out.reshape(n, s, d)

    def _L1_xattn_ref(x, context, Wq, Wkv, null_kv, Wout, ln_scale, ln_bias):
        import jax, jax.numpy as jnp
        import numpy as np
        B, N, DIM = (8, 1024, 256)
        M, CTX = (64, 512)
        HEADS, DH = (16, 64)
        INNER = HEADS * DH
        EPS = 1e-06

        def _split_heads(t):
            b, n, _ = t.shape
            return t.reshape(b, n, HEADS, DH).transpose(0, 2, 1, 3)
        scale = DH ** (-0.5)
        b = x.shape[0]
        q = _split_heads(jnp.einsum('bnd,df->bnf', x, Wq))
        kv = jnp.einsum('bmc,cf->bmf', context, Wkv)
        k, v = jnp.split(kv, 2, axis=-1)
        k, v = (_split_heads(k), _split_heads(v))
        nk = jnp.broadcast_to(null_kv[0], (b, HEADS, 1, DH))
        nv = jnp.broadcast_to(null_kv[1], (b, HEADS, 1, DH))
        k = jnp.concatenate((nk, k), axis=-2)
        v = jnp.concatenate((nv, v), axis=-2)
        q = q * scale
        sim = jnp.einsum('bhid,bhjd->bhij', q, k)
        attn = jax.nn.softmax(sim, axis=-1)
        out = jnp.einsum('bhij,bhjd->bhid', attn, v)
        out = out.transpose(0, 2, 1, 3).reshape(b, -1, INNER)
        out = jnp.einsum('bnf,fd->bnd', out, Wout)
        mu = jnp.mean(out, axis=-1, keepdims=True)
        var = jnp.var(out, axis=-1, keepdims=True)
        out = (out - mu) * jax.lax.rsqrt(var + EPS) * ln_scale + ln_bias
        return out

    def _L1_ffn_ref(hidden_states, q_w, q_b, k_w, k_b, v_w, v_b, o_w, o_b, router_w, router_b, w1, b1, w2, b2):
        import jax, jax.numpy as jnp
        import numpy as np
        import math
        D = 256
        H = 16
        E = 8
        TOPK = 2
        LAT = D // 2
        KPH = LAT // H
        HD = D // H

        def _forward(hs, q_w, q_b, k_w, k_b, v_w, v_b, o_w, o_b, router_w, router_b, w1, b1, w2, b2):
            B, S, _ = hs.shape
            Q = (hs @ q_w + q_b).reshape(B, S, H, HD).transpose(0, 2, 1, 3)
            K = (hs @ k_w + k_b).reshape(B, S, H, KPH).transpose(0, 2, 1, 3)
            V = (hs @ v_w + v_b).reshape(B, S, H, KPH).transpose(0, 2, 1, 3)
            scores = jnp.einsum('bhsk,bhtk->bhst', Q[..., :KPH], K) / math.sqrt(KPH)
            attn = jax.nn.softmax(scores, axis=-1)
            ao = jnp.einsum('bhst,bhtv->bhsv', attn, V)
            ao = ao.transpose(0, 2, 1, 3).reshape(B, S, H * KPH)
            ao = jnp.concatenate([ao, jnp.zeros((B, S, D - LAT), ao.dtype)], axis=-1)
            mla_out = ao @ o_w + o_b
            probs = jax.nn.softmax(mla_out @ router_w + router_b, axis=-1)
            topw, topi = jax.lax.top_k(probs, TOPK)
            topw = topw / (topw.sum(-1, keepdims=True) + 1e-08)
            combine = jnp.sum(jax.nn.one_hot(topi, E, dtype=probs.dtype) * topw[..., None], axis=-2)
            h1 = jnp.einsum('bsd,edf->ebsf', mla_out, w1) + b1[:, None, None, :]
            h1 = jax.nn.gelu(h1, approximate=False)
            h2 = jnp.einsum('ebsf,efd->ebsd', h1, w2) + b2[:, None, None, :]
            moe_out = jnp.einsum('bse,ebsd->bsd', combine, h2)
            return hs + 0.3 * moe_out
        return _forward(hidden_states, q_w, q_b, k_w, k_b, v_w, v_b, o_w, o_b, router_w, router_b, w1, b1, w2, b2)
    x = x + jnp.tanh(g_xattn[0]) * _L0_xattn_ref(_layernorm(x, axis=-1), ctx_2048, mask_BxS2_if0, L0_xattn_W_in, L0_xattn_b_in, L0_xattn_g_res, L0_xattn_g_init)
    x = x + jnp.tanh(g_ffn[0]) * _L0_ffn_ref(_layernorm(x, axis=-1), L0_ffn_Wg, L0_ffn_bg, L0_ffn_W0, L0_ffn_b0, L0_ffn_W1, L0_ffn_b1, L0_ffn_W2, L0_ffn_b2)
    x = x + jnp.tanh(g_xattn[1]) * _L1_xattn_ref(_layernorm(x, axis=-1), ctx_2048, L1_xattn_Wq, L1_xattn_Wkv, L1_xattn_null_kv, L1_xattn_Wout, L1_xattn_ln_scale, L1_xattn_ln_bias)
    x = x + jnp.tanh(g_ffn[1]) * _L1_ffn_ref(_layernorm(x, axis=-1), L1_ffn_q_w, L1_ffn_q_b, L1_ffn_k_w, L1_ffn_k_b, L1_ffn_v_w, L1_ffn_v_b, L1_ffn_o_w, L1_ffn_o_b, L1_ffn_router_w, L1_ffn_router_b, L1_ffn_w1, L1_ffn_b1, L1_ffn_w2, L1_ffn_b2)
    return x

_drawn_inputs = setup_inputs


def setup_inputs(seed=0):
    import zlib

    import numpy as np

    out = dict(_drawn_inputs(seed))
    spreads = {'g_ffn': (-1.0, 0.2),
     'L0_xattn_b_in': (0.0, 0.1),
     'L0_xattn_g_res': (1.0, 0.2),
     'L0_xattn_g_init': (1.0, 0.2),
     'L0_ffn_bg': (0.0, 0.457),
     'L0_ffn_b0': (0.0, 0.8),
     'L0_ffn_b1': (0.0, 0.8),
     'L0_ffn_b2': (0.0, 0.1),
     'L1_xattn_ln_scale': (1.0, 0.2),
     'L1_xattn_ln_bias': (0.0, 0.1),
     'L1_ffn_q_b': (0.0, 0.8),
     'L1_ffn_k_b': (0.0, 2.0),
     'L1_ffn_v_b': (0.0, 0.8),
     'L1_ffn_o_b': (0.0, 0.8),
     'L1_ffn_router_b': (0.0, 0.1),
     'L1_ffn_b1': (0.0, 0.8),
     'L1_ffn_b2': (0.0, 2.0)}
    factors = {'L0_ffn_W0': 4.54,
     'L0_ffn_W1': 4.588,
     'L0_ffn_W2': 4.328,
     'L1_xattn_null_kv': 5.388,
     'L1_ffn_q_w': 8.0,
     'L1_ffn_k_w': 8.0,
     'L1_ffn_v_w': 8.0,
     'L1_ffn_o_w': 8.0,
     'L1_ffn_router_w': 8.0,
     'L1_ffn_w1': 8.0,
     'L1_ffn_w2': 8.0}
    for name, (base, spread) in spreads.items():
        noise = np.random.default_rng([zlib.crc32(name.encode()), seed]).standard_normal(out[name].shape)
        drawn = base * np.exp(spread * noise) if base else spread * noise
        out[name] = jnp.asarray(drawn.astype(out[name].dtype))
    for name, factor in factors.items():
        out[name] = (out[name] * factor).astype(out[name].dtype)
    return out
```

```python
import math
from contextlib import ExitStack

import concourse.bass as bass
from concourse import mybir

F32 = mybir.dt.float32
BF16 = mybir.dt.bfloat16
I32 = mybir.dt.int32
ACT = mybir.ActivationFunctionType
ALU = mybir.AluOpType
AX = mybir.AxisListType

P = 128
NT = 16
T = NT * P
D = 256
KD = D // P
CTX = 512
KC = CTX // P
E = 8
PASSES = ((0, 0), (0, 1), (1, 0))
LN_EPS = 1e-5
RMS_EPS = 1e-5
DECAY_EPS = 0.001
DECAY_DT = -math.log(-math.expm1(-DECAY_EPS))
XHEADS, XDH = 16, 64
LHEADS, LDH = 16, 8
XW = P + 1


def ts(start, size):
    return bass.ds(start, size)


AHEAD = 1


def start_ahead(sp, *sems):
    for sem in sems:
        sp.sem_inc(sem, AHEAD)


class Chain:

    def __init__(self, eng, sem):
        self.eng, self.sem, self.n = eng, sem, 0

    def link(self, ins):
        self.n += 1
        ins.then_inc(self.sem, 1)
        self.eng.wait_ge(self.sem, self.n)


class Scope(ExitStack):

    def __init__(self, nc, stage):
        super().__init__()
        self.nc, self.stage, self.sems = nc, stage, []
        self.callback(self.clear)

    def sb(self, name, shape, dt=F32):
        return self.enter_context(self.nc.sbuf_tensor(f"{self.stage}_{name}", shape, dt))

    def sem(self, name):
        self.sems.append(self.nc.alloc_semaphore(f"{self.stage}_{name}"))
        return self.sems[-1]

    def clear(self):
        if self.sems:
            self.nc.clear_and_free_semaphores(self.sems)
            self.nc.all_engine_barrier()

    def block(self):
        return self.enter_context(self.nc.Block())


class Shared:

    def __init__(self, nc, scope):
        self.ps = scope.enter_context(nc.psum_tensor("banks", [P, 8, 512], F32))
        self.x = scope.sb("x_res", [P, NT, D])
        self.zt = scope.sb("zt", [P, 2, KD, T], BF16)
        self.ident = scope.sb("ident", [P, P])
        self.gates = scope.sb("gates", [P, 4])
        self.cw = scope.sb("cw", [P, NT, E])
        self.mean = scope.sb("mean", [P, NT])
        self.rstd = scope.sb("rstd", [P, NT])


def stats_loop(eng, src, raw, done):
    with eng.Fori(0, NT) as b:
        eng.bn_stats(raw[:, ts(b, 1), :].squeeze(1), src[:, ts(b, 1), :].squeeze(1)).then_inc(done, 1)


def combine_stats(eng, chain, raw, mean, var, tmp, width):
    half = width // 2
    me, mo, ve, vo = raw[:, :, 1], raw[:, :, 4], raw[:, :, 2], raw[:, :, 5]
    chain.link(eng.tensor_tensor(mean, me, mo, ALU.add))
    chain.link(eng.tensor_scalar(mean, mean, 0.5, None, ALU.mult))
    chain.link(eng.tensor_tensor(tmp, me, mo, ALU.subtract))
    chain.link(eng.tensor_tensor(tmp, tmp, tmp, ALU.mult))
    chain.link(eng.tensor_tensor(var, ve, vo, ALU.add))
    chain.link(eng.tensor_scalar(var, var, 1.0 / width, None, ALU.mult))
    chain.link(eng.scalar_tensor_tensor(out=var, in0=tmp, scalar=0.25, in1=var, op0=ALU.mult, op1=ALU.add))


def depool_stage(nc, S, A):
    with Scope(nc, "dp") as c:
        ctx = c.sb("ctx", [P, NT, CTX])
        lens = c.sb("lens", [NT, 2, P], I32)
        bidx = c.sb("bidx", [NT, 3, P])
        idxT = c.sb("idxT", [P, NT])
        iota_i = c.sb("iota_i", [P, P], I32)
        iota_s = c.sb("iota_s", [P, P])
        part_i = c.sb("part_i", [P, 1], I32)
        part = c.sb("part", [P, 1])
        ones = c.sb("ones", [P, P], BF16)
        tri = c.sb("tri", [P, P], BF16)
        hot = c.sb("hot", [P, NT, P], BF16)
        hit = c.sb("hit", [P, NT])
        diff = c.sb("diff", [P, NT, P])
        decay = c.sb("decay", [P, NT, P])
        win = c.sb("win", [P, KD, D])
        winT = c.sb("winT", [P, KD, D])
        gres = c.sb("gres", [P, KD])
        ginit = c.sb("ginit", [P, D])
        bin_row = c.sb("bin_row", [P, D])
        graw = c.sb("graw", [P, 4])
        raw = c.sb("raw", [P, NT, 6])
        var = c.sb("var", [P, 2, NT])
        tmp = c.sb("tmp", [P, NT])
        ssq = c.sb("ssq", [P, NT])
        rctx = c.sb("rctx", [P, NT])
        sq = c.sb("sq", [P, 2, CTX])
        z = c.sb("z", [P, 2, D])
        zT = c.sb("zT", [P, 2, D])
        pick = c.sb("pick", [P, 2, P])
        cg = c.sb("cg", [P, 2, D])
        xb = c.sb("xb", [P, 2, D])

        s_len, s_win, s_rows, s_x, s_ctx = (c.sem(n) for n in ("len", "win", "rows", "x", "ctx"))
        s_pool = c.sem("pool")
        s_dve = c.sem("dve")
        s_idx, s_idxT, s_hot, s_hits, s_step, s_cum, s_diff = (
            c.sem(n) for n in ("idx", "idxT", "hot", "hits", "step", "cum", "diff"))
        s_decay, s_wT, s_wTs, s_stats, s_var, s_root, s_ssq, s_act = (
            c.sem(n) for n in ("decay", "wT", "wTs", "stats", "var", "root", "ssq", "act"))
        s_rstd, s_gate, s_bias = c.sem("rstd"), c.sem("gate"), c.sem("bias")
        s_z, s_zt, s_ztc, s_pick, s_out, s_xb, s_res = (
            c.sem(n) for n in ("z", "zt", "ztc", "pick", "out", "xb", "res"))
        ps = S.ps
        block = c.block()
        CONSTS = 7

        @block.sync
        def _(sp):
            start_ahead(sp, s_act, s_out, s_ztc, s_zt)
            sp.dma_start(lens[:, 0, :], A["mask_BxS2_if0"]).then_inc(s_len, 16)
            for q in range(4):
                sp.dma_start(S.x[:, 4 * q:4 * q + 4, :],
                             A["x"][4 * q:4 * q + 4].rearrange("b p d -> p b d")).then_inc(s_x, 16)
            sp.dma_start(win[:, :, :], A["L0_xattn_W_in"].rearrange("(c p) d -> p c d", p=P)).then_inc(s_win, 16)
            for q in range(4):
                sp.dma_start(ctx[:, 4 * q:4 * q + 4, :],
                             A["ctx_2048"][4 * q:4 * q + 4].rearrange("b p d -> p b d")).then_inc(s_ctx, 16)

        @block.gpsimd
        def _(pool):
            chain = Chain(pool, s_pool)
            chain.link(pool.memset(S.ident[:, :], 0.0))
            chain.link(pool.affine_select(out=S.ident[:, :], in_=S.ident[:, :], compare_op=ALU.not_equal, fill=1.0,
                                          base=0, pattern=[[-1, P]], channel_multiplier=1))
            chain.link(pool.iota(iota_i[:, :], pattern=[[1, P]], base=0, channel_multiplier=0))
            chain.link(pool.iota(part_i[:, :], pattern=[[0, 1]], base=0, channel_multiplier=1))
            chain.link(pool.memset(ones[:, :], 1.0))
            chain.link(pool.memset(tri[:, :], 1.0))
            chain.link(pool.affine_select(out=tri[:, :], in_=tri[:, :], compare_op=ALU.is_ge, fill=0.0,
                                          base=0, pattern=[[1, P]], channel_multiplier=-1))
            assert chain.n == CONSTS
            pool.wait_ge(s_bias, 1)
            pool.wait_ge(s_x, 64)
            with pool.Fori(0, NT // 2) as i:
                for j in range(2):
                    b = 2 * i + j
                    pool.wait_ge(s_res, b + 1)
                    pool.tensor_tensor(xb[:, j, :], S.x[:, ts(b, 1), :].squeeze(1), bin_row[:, :],
                                       ALU.add).then_inc(s_xb, 1)

        @block.scalar
        def _(act):
            act.dma_start(graw[:, 0:2], A["g_xattn"].partition_broadcast(P)).then_inc(s_rows, 16)
            act.dma_start(graw[:, 2:4], A["g_ffn"].partition_broadcast(P)).then_inc(s_rows, 16)
            act.dma_start(ginit[:, :], A["L0_xattn_g_init"][0:D].partition_broadcast(P)).then_inc(s_rows, 16)
            act.dma_start(bin_row[:, :], A["L0_xattn_b_in"].partition_broadcast(P)).then_inc(s_rows, 16)
            for k in range(KD):
                act.dma_start(gres[:, k:k + 1],
                              A["L0_xattn_g_res"][k * P:(k + 1) * P].rearrange("(p a) -> p a", a=1)).then_inc(s_rows, 16)
            act.wait_ge(s_rows, 96)
            act.activation(S.gates[:, :], graw[:, :], ACT.Tanh).then_inc(s_gate, 1)
            act.wait_ge(s_ctx, 64)
            with act.Fori(0, NT // 2) as i:
                for j in range(2):
                    b = 2 * i + j
                    act.wait_ge(s_act, b + AHEAD)
                    act.activation(sq[:, j, :], ctx[:, ts(b, 1), :].squeeze(1), ACT.Square,
                                   accum_out=ssq[:, ts(b, 1)]).then_inc(s_act, 1)
            act.wait_ge(s_var, 1)
            act.activation(S.rstd[:, :], var[:, 0, :], ACT.Sqrt).then_inc(s_root, 1)
            act.activation(rctx[:, :], var[:, 1, :], ACT.Sqrt).then_inc(s_root, 1)
            act.wait_ge(s_diff, 1)
            act.activation(decay[:, :, :], decay[:, :, :], ACT.Exp, scale=-DECAY_DT).then_inc(s_decay, 1)
            with act.Fori(0, NT // 2) as i:
                for j in range(2):
                    b = 2 * i + j
                    act.wait_ge(s_zt, b + 1 + AHEAD)
                    act.wait_ge(s_out, b + AHEAD)
                    act.activation(zT[:, j, :], ps[:, j, 0:D], ACT.Copy).then_inc(s_ztc, 1)

        @block.tensor
        def _(pe):
            pe.wait_ge(s_pool, CONSTS)
            pe.wait_ge(s_win, 16)
            for k in range(KD):
                for e in range(KD):
                    mm = pe.transpose(ps[:, 7, k * D + e * P:k * D + e * P + P], win[:, e, k * P:k * P + P], S.ident[:, :])
            mm.then_inc(s_wT, 1)
            pe.wait_ge(s_idx, 1)
            pe.transpose(ps[:, 6, 0:NT], bidx[:, 2, :], S.ident[0:NT, 0:NT]).then_inc(s_idxT, 1)
            pe.wait_ge(s_hot, 1)
            for b in range(NT):
                mm = pe.matmul(ps[:, 5, b:b + 1], hot[:, b, :], ones[:, 0:1], start=True, stop=True)
            mm.then_inc(s_hits, 1)
            pe.wait_ge(s_step, 1)
            for q in range(4):
                mm = pe.matmul(ps[:, q, :], ones[:, :], hot[:, 4 * q:4 * q + 4, :].rearrange("p b s -> p (b s)"),
                               start=True, stop=True)
            mm.then_inc(s_cum, 1)
            pe.wait_ge(s_diff, 1)
            pe.wait_ge(s_wTs, 1)
            with pe.Fori(0, NT // 2) as i:
                for j in range(2):
                    b = 2 * i + j
                    pe.wait_ge(s_z, b + 1)
                    if j == 0:
                        pe.wait_ge(s_ztc, b + AHEAD)
                    else:
                        pe.wait_ge(s_ztc, b + AHEAD)
                    for k in range(KD):
                        mm = pe.transpose(ps[:, j, k * P:k * P + P], z[:, j, k * P:k * P + P], S.ident[:, :])
                    mm.then_inc(s_zt, 1)
                    pe.wait_ge(s_pick, b + 1)
                    pe.wait_ge(s_res, b + 1)
                    pe.matmul(ps[:, 2 + j, 0:D], pick[:, j, :], cg[:, j, :], start=True, stop=False)
                    pe.wait_ge(s_ztc, b + 1 + AHEAD)
                    for k in range(KD):
                        mm = pe.matmul(ps[:, 2 + j, 0:D], zT[:, j, k * P:k * P + P], winT[:, k, :],
                                       start=False, stop=(k == KD - 1))
                    mm.then_inc(s_out, 1)

        @block.vector
        def _(dve):
            chain = Chain(dve, s_dve)
            dve.wait_ge(s_len, 16)
            src = 0
            for step in (1, 2, 4, 8, 16, 32, 64):
                a, b = lens[:, src, :], lens[:, 1 - src, :]
                chain.link(dve.tensor_copy(b[:, 0:step], a[:, 0:step]))
                chain.link(dve.tensor_tensor(b[:, step:P], a[:, step:P], a[:, 0:P - step], ALU.add))
                src = 1 - src
            chain.link(dve.tensor_copy(bidx[:, 0, :], lens[:, src, :]))
            chain.link(dve.tensor_scalar(bidx[:, 0, :], bidx[:, 0, :], -1.0, None, ALU.add))
            chain.link(dve.tensor_scalar(bidx[:, 1, :], bidx[:, 0, :], 0.0, float(P), ALU.is_lt, ALU.mult))
            dve.tensor_tensor(bidx[:, 2, :], bidx[:, 0, :], bidx[:, 1, :], ALU.add).then_inc(s_idx, 1)
            dve.wait_ge(s_pool, CONSTS)
            chain.link(dve.tensor_copy(iota_s[:, :], iota_i[:, :]))
            chain.link(dve.tensor_copy(part[:, :], part_i[:, :]))
            dve.wait_ge(s_idxT, 1)
            chain.link(dve.tensor_copy(idxT[:, :], ps[:, 6, 0:NT]))
            dve.tensor_tensor(hot[:, :, :], iota_s[:, :].unsqueeze(1).broadcast_to([P, NT, P]),
                              idxT[:, :].unsqueeze(2).broadcast_to([P, NT, P]), ALU.is_equal).then_inc(s_hot, 1)
            dve.wait_ge(s_wT, 1)
            dve.wait_ge(s_rows, 96)
            for k in range(KD):
                w = dve.tensor_scalar(winT[:, k, :], ps[:, 7, k * D:k * D + D], gres[:, k:k + 1], None, ALU.mult)
            w.then_inc(s_wTs, 1)
            dve.wait_ge(s_hits, 1)
            chain.link(dve.tensor_scalar(hit[:, :], ps[:, 5, 0:NT], 1.0, None, ALU.min))
            dve.tensor_tensor(hot[:, :, :], tri[:, :].unsqueeze(1).broadcast_to([P, NT, P]),
                              hit[:, :].unsqueeze(2).broadcast_to([P, NT, P]), ALU.mult).then_inc(s_step, 1)
            dve.wait_ge(s_x, 64)
            stats_loop(dve, S.x, raw, s_stats)
            dve.wait_ge(s_stats, NT)
            combine_stats(dve, chain, raw, S.mean[:, :], var[:, 0, :], tmp[:, :], D)
            chain.link(dve.tensor_scalar(var[:, 0, :], var[:, 0, :], 1.0 + RMS_EPS, RMS_EPS * LN_EPS, ALU.mult, ALU.add))
            dve.wait_ge(s_act, NT + AHEAD)
            dve.tensor_scalar(var[:, 1, :], ssq[:, :], 1.0 / CTX, RMS_EPS, ALU.mult, ALU.add).then_inc(s_var, 1)
            dve.wait_ge(s_cum, 1)
            for q in range(4):
                chain.link(dve.tensor_scalar(diff[:, 4 * q:4 * q + 4, :].rearrange("p b s -> p (b s)"), ps[:, q, :],
                                             -1.0, 0.0, ALU.add, ALU.max))
            chain.link(dve.tensor_scalar(diff[:, :, :], diff[:, :, :], float(P - 1), part[:, :], ALU.min, ALU.subtract))
            dve.tensor_scalar(decay[:, :, :], diff[:, :, :], 0.0, None, ALU.max).then_inc(s_diff, 1)
            dve.wait_ge(s_root, 2)
            chain.link(dve.reciprocal(S.rstd[:, :], S.rstd[:, :]))
            chain.link(dve.reciprocal(rctx[:, :], rctx[:, :]))
            chain.link(dve.tensor_scalar(rctx[:, :], rctx[:, :], math.exp(-DECAY_EPS), None, ALU.mult))
            dve.wait_ge(s_gate, 1)
            dve.tensor_scalar(bin_row[:, :], bin_row[:, :], S.gates[:, 0:1], None, ALU.mult).then_inc(s_bias, 1)
            dve.wait_ge(s_bias, 1)
            dve.tensor_copy(tmp[:, 0:1], part[:, :]).then_inc(s_res, 1)
            dve.tensor_copy(tmp[:, 1:2], part[:, :]).then_inc(s_res, 1)
            dve.wait_ge(s_decay, 1)

            def finish(b, j):
                dve.wait_ge(s_out, b + 1 + AHEAD)
                dve.wait_ge(s_xb, b + 1)
                dve.scalar_tensor_tensor(out=S.x[:, ts(b, 1), :].squeeze(1), in0=ps[:, 2 + j, 0:D],
                                         scalar=S.gates[:, 0:1], in1=xb[:, j, :],
                                         op0=ALU.mult, op1=ALU.add).then_inc(s_res, 1)

            with dve.Fori(0, NT // 2) as i:
                for j in range(2):
                    b = 2 * i + j
                    dve.wait_ge(s_zt, b + AHEAD)
                    dve.tensor_scalar(z[:, j, :], S.x[:, ts(b, 1), :].squeeze(1), S.mean[:, ts(b, 1)],
                                      S.rstd[:, ts(b, 1)], ALU.subtract, ALU.mult).then_inc(s_z, 1)
                    dve.wait_ge(s_out, b + AHEAD)
                    dve.scalar_tensor_tensor(out=cg[:, j, :], in0=ctx[:, ts(b, 1), 0:D].squeeze(1),
                                             scalar=rctx[:, ts(b, 1)], in1=ginit[:, :], op0=ALU.mult, op1=ALU.mult)
                    dve.scalar_tensor_tensor(out=pick[:, j, :], in0=diff[:, ts(b, 1), :].squeeze(1), scalar=0.0,
                                             in1=decay[:, ts(b, 1), :].squeeze(1),
                                             op0=ALU.is_ge, op1=ALU.mult).then_inc(s_pick, 1)
                    finish(b, j)


def norm_stage(nc, S, stage, prefetch=None, residual=None):
    with Scope(nc, stage) as c:
        raw = c.sb("raw", [P, NT, 6])
        tmp = c.sb("tmp", [P, NT])
        z = c.sb("z", [P, 2, D])
        s_dve, s_stats, s_var, s_root = (c.sem(n) for n in ("dve", "stats", "var", "root"))
        s_z, s_tr, s_hi, s_lo, s_res = (c.sem(n) for n in ("z", "tr", "hi", "lo", "res"))
        ps = S.ps
        block = c.block()

        @block.sync
        def _(sp):
            start_ahead(sp, s_lo)
            if prefetch:
                prefetch.load_first(sp)

        if prefetch:
            @block.gpsimd
            def _(pool):
                prefetch.split_first(pool)

        @block.scalar
        def _(act):
            act.wait_ge(s_var, 1)
            act.activation(S.rstd[:, :], S.rstd[:, :], ACT.Sqrt).then_inc(s_root, 1)
            with act.Fori(0, NT // 2) as i:
                for j in range(2):
                    b = 2 * i + j
                    act.wait_ge(s_tr, b + 1)
                    act.activation(S.zt[:, 0, :, ts(b * P, P)], ps[:, j, 0:D].rearrange("p (k s) -> p k s", k=KD),
                                   ACT.Copy).then_inc(s_hi, 1)

        @block.tensor
        def _(pe):
            with pe.Fori(0, NT // 2) as i:
                for j in range(2):
                    b = 2 * i + j
                    pe.wait_ge(s_z, b + 1)
                    pe.wait_ge(s_lo, b + AHEAD)
                    for k in range(KD):
                        mm = pe.transpose(ps[:, j, k * P:k * P + P], z[:, j, k * P:k * P + P], S.ident[:, :])
                    mm.then_inc(s_tr, 1)

        @block.vector
        def _(dve):
            chain = Chain(dve, s_dve)
            stats_loop(dve, S.x, raw, s_stats)
            dve.wait_ge(s_stats, NT)
            combine_stats(dve, chain, raw, S.mean[:, :], S.rstd[:, :], tmp[:, :], D)
            dve.tensor_scalar(S.rstd[:, :], S.rstd[:, :], LN_EPS, None, ALU.add).then_inc(s_var, 1)
            dve.wait_ge(s_root, 1)
            chain.link(dve.reciprocal(S.rstd[:, :], S.rstd[:, :]))

            def normalise(b, j):
                x = S.x[:, ts(b, 1), :].squeeze(1)
                dve.tensor_scalar(z[:, j, :], x, S.mean[:, ts(b, 1)], S.rstd[:, ts(b, 1)],
                                  ALU.subtract, ALU.mult).then_inc(s_z, 1)
                if residual is not None:
                    dve.wait_ge(s_z, b + 1)
                    dve.scalar_tensor_tensor(out=x, in0=z[:, j, :], scalar=S.gates[:, residual:residual + 1],
                                             in1=x, op0=ALU.mult, op1=ALU.add).then_inc(s_res, 1)

            def low_part(b, j):
                dve.wait_ge(s_hi, b + 1)
                tok = ts(b * P, P)
                dve.tensor_tensor(S.zt[:, 1, :, tok], ps[:, j, 0:D].rearrange("p (k s) -> p k s", k=KD),
                                  S.zt[:, 0, :, tok], ALU.subtract).then_inc(s_lo, 1)

            normalise(0, 0)
            with dve.Fori(0, NT // 2 - 1) as i:
                normalise(2 * i + 1, 1)
                low_part(2 * i, 0)
                normalise(2 * i + 2, 0)
                low_part(2 * i + 1, 1)
            normalise(NT - 1, 1)
            low_part(NT - 2, 0)
            low_part(NT - 1, 1)


def gate_stage(nc, S, stage, A, wg, bg, b2, gate, top_of_probs, factor=1.0, prefetch=None):
    with Scope(nc, stage) as c:
        wraw = c.sb("wraw", [P, KD, E])
        w = c.sb("w", [P, 2, KD, E], BF16)
        brow = c.sb("brow", [P, E])
        b2rep = c.sb("b2rep", [P, D])
        ones = c.sb("ones", [P, NT])
        own = c.sb("own", [P, NT])
        earlier = c.sb("earlier", [P, E, E])
        lg = c.sb("lg", [P, NT, E])
        top = c.sb("top", [P, NT])
        pr = c.sb("pr", [P, NT, E])
        beat = c.sb("beat", [P, NT, E, E])
        tie = c.sb("tie", [P, NT, E, E])
        rank = c.sb("rank", [P, NT, E])
        scale = c.sb("scale", [P, 1])
        cwT = c.sb("cwT", [P, P])
        rhs = c.sb("rhs", [P, 2, D])
        s_w, s_b2, s_pool, s_dve, s_split = (c.sem(n) for n in ("w", "b2", "pool", "dve", "split"))
        s_lg, s_sub, s_exp, s_cw, s_cwT, s_cwTs, s_rhs, s_bias, s_res = (
            c.sem(n) for n in ("lg", "sub", "exp", "cw", "cwT", "cwTs", "rhs", "bias", "res"))
        ps = S.ps
        block = c.block()

        @block.sync
        def _(sp):
            start_ahead(sp, s_bias, s_res)
            sp.dma_start(wraw[:, :, :], wg.rearrange("(k p) e -> p k e", p=P)).then_inc(s_w, 16)
            sp.dma_start(brow[:, :], bg.partition_broadcast(P)).then_inc(s_w, 16)
            for t in range(NT):
                sp.dma_start(b2rep[E * t:E * t + E, :], b2).then_inc(s_b2, 16)

        @block.gpsimd
        def _(pool):
            chain = Chain(pool, s_pool)
            chain.link(pool.memset(ones[:, :], 1.0))
            chain.link(pool.affine_select(out=own[:, :], in_=ones[:, :], compare_op=ALU.is_ge, fill=0.0,
                                          base=0, pattern=[[-E, NT]], channel_multiplier=1))
            chain.link(pool.affine_select(out=own[:, :], in_=own[:, :], compare_op=ALU.is_ge, fill=0.0,
                                          base=E - 1, pattern=[[E, NT]], channel_multiplier=-1))
            chain.link(pool.memset(earlier[:, :, :], 1.0))
            chain.link(pool.affine_select(out=earlier[:, :, :], in_=earlier[:, :, :], compare_op=ALU.is_ge, fill=0.0,
                                          base=-1, pattern=[[1, E], [-1, E]], channel_multiplier=0))
            pool.wait_ge(s_b2, 16 * NT)
            with pool.Fori(0, NT // 2) as i:
                for j in range(2):
                    b = 2 * i + j
                    pool.wait_ge(s_bias, b + AHEAD)
                    pool.tensor_tensor(rhs[:, j, :], b2rep[:, :], own[:, ts(b, 1)].broadcast_to([P, D]),
                                       ALU.mult).then_inc(s_rhs, 1)

        @block.scalar
        def _(act):
            act.wait_ge(s_sub, 1)
            act.activation(pr[:, :, :], pr[:, :, :], ACT.Exp).then_inc(s_exp, 1)

        @block.tensor
        def _(pe):
            pe.wait_ge(s_split, 2)
            with pe.Fori(0, NT) as b:
                n = 0
                for wp, ap in PASSES:
                    for k in range(KD):
                        mm = pe.matmul(ps[:, 7, ts(b * E, E)], S.zt[:, ap, k, ts(b * P, P)], w[:, wp, k, :],
                                       start=(n == 0), stop=(n == 3 * KD - 1))
                        n += 1
                mm.then_inc(s_lg, 1)
            pe.wait_ge(s_cw, 1)
            pe.transpose(ps[:, 6, 0:P], S.cw[:, :, :].rearrange("p t e -> p (t e)"), S.ident[:, :]).then_inc(s_cwT, 1)
            pe.wait_ge(s_cwTs, 1)
            with pe.Fori(0, NT // 2) as i:
                for j in range(2):
                    b = 2 * i + j
                    pe.wait_ge(s_rhs, b + 1)
                    pe.wait_ge(s_res, b + AHEAD)
                    pe.matmul(ps[:, j, 0:D], cwT[:, :], rhs[:, j, :], start=True, stop=True).then_inc(s_bias, 1)

        @block.vector
        def _(dve):
            chain = Chain(dve, s_dve)
            dve.wait_ge(s_w, 32)
            dve.tensor_copy(w[:, 0, :, :], wraw[:, :, :]).then_inc(s_split, 1)
            dve.wait_ge(s_split, 1)
            dve.tensor_tensor(w[:, 1, :, :], wraw[:, :, :], w[:, 0, :, :], ALU.subtract).then_inc(s_split, 1)
            dve.wait_ge(s_lg, NT)
            chain.link(dve.tensor_tensor(lg[:, :, :], ps[:, 7, 0:NT * E].rearrange("p (t e) -> p t e", e=E),
                                         brow[:, :].unsqueeze(1).broadcast_to([P, NT, E]), ALU.add))
            chain.link(dve.tensor_reduce(top[:, :], lg[:, :, :], AX.X, ALU.max))
            dve.tensor_tensor(pr[:, :, :], lg[:, :, :], top[:, :].unsqueeze(2).broadcast_to([P, NT, E]),
                              ALU.subtract).then_inc(s_sub, 1)
            dve.wait_ge(s_exp, 1)
            dve.wait_ge(s_pool, 5)

            def share(values):
                chain.link(dve.tensor_reduce(top[:, :], values, AX.X, ALU.add))

            ranked = lg
            if top_of_probs:
                share(pr[:, :, :])
                chain.link(dve.reciprocal(top[:, :], top[:, :]))
                chain.link(dve.tensor_tensor(pr[:, :, :], pr[:, :, :], top[:, :].unsqueeze(2).broadcast_to([P, NT, E]),
                                             ALU.mult))
                ranked = pr
            me = ranked[:, :, :].unsqueeze(3).broadcast_to([P, NT, E, E])
            others = ranked[:, :, :].unsqueeze(2).broadcast_to([P, NT, E, E])
            chain.link(dve.tensor_tensor(beat[:, :, :, :], others, me, ALU.is_gt))
            chain.link(dve.tensor_tensor(tie[:, :, :, :], others, me, ALU.is_equal))
            flat = lambda t: t[:, :, :, :].rearrange("p t e f -> p t (e f)")
            chain.link(dve.tensor_tensor(flat(tie), flat(tie),
                                         earlier[:, :, :].rearrange("p e f -> p (e f)").unsqueeze(1)
                                         .broadcast_to([P, NT, E * E]), ALU.mult))
            chain.link(dve.tensor_tensor(flat(beat), flat(beat), flat(tie), ALU.add))
            chain.link(dve.tensor_reduce(rank[:, :, :], beat[:, :, :, :], AX.X, ALU.add))
            flat2 = lambda t: t[:, :, :].rearrange("p t e -> p (t e)")
            chain.link(dve.scalar_tensor_tensor(out=flat2(pr), in0=flat2(rank), scalar=2.0, in1=flat2(pr),
                                                op0=ALU.is_lt, op1=ALU.mult))
            share(pr[:, :, :])
            if top_of_probs:
                chain.link(dve.tensor_scalar(top[:, :], top[:, :], 1e-8, None, ALU.add))
            chain.link(dve.reciprocal(top[:, :], top[:, :]))
            chain.link(dve.tensor_scalar(scale[:, :], S.gates[:, gate:gate + 1], factor, None, ALU.mult))
            chain.link(dve.tensor_scalar(top[:, :], top[:, :], scale[:, :], None, ALU.mult))
            dve.tensor_tensor(S.cw[:, :, :], pr[:, :, :], top[:, :].unsqueeze(2).broadcast_to([P, NT, E]),
                              ALU.mult).then_inc(s_cw, 1)
            dve.wait_ge(s_cwT, 1)
            dve.tensor_copy(cwT[:, :], ps[:, 6, 0:P]).then_inc(s_cwTs, 1)
            with dve.Fori(0, NT // 2) as i:
                for j in range(2):
                    b = 2 * i + j
                    x = S.x[:, ts(b, 1), :].squeeze(1)
                    dve.wait_ge(s_bias, b + 1 + AHEAD)
                    dve.tensor_tensor(x, ps[:, j, 0:D], x, ALU.add).then_inc(s_res, 1)


class Ring:

    def __init__(self, nc, scope, mats):
        self.mats = mats
        self.n = len(mats)
        self.raw, self.split = [], []
        for i, m in enumerate(mats):
            rows, cols = m.shape[1], m.shape[2]
            self.raw.append(scope.sb(f"raw{i}", [P, rows // P, cols]))
            self.split.append([scope.sb(f"w{i}_{j}", [P, 2, rows // P, cols], BF16) for j in range(2)])
        self.s_turn = scope.sem("wturn")
        self.s_raw, self.s_split, self.s_free = scope.sem("wraw"), scope.sem("wsplit"), scope.sem("wfree")

    def load(self, sp, e, wait=True):
        if wait:
            sp.wait_ge(self.s_split, 2 * self.n * e)
        for raw, m in zip(self.raw, self.mats):
            src = m[e] if isinstance(e, int) else m[ts(e, 1)].squeeze(0)
            sp.dma_start(raw[:, :, :], src.rearrange("(k p) h -> p k h", p=P)).then_inc(self.s_raw, 16)

    def halves(self, pool, e, j, wait=True):
        pool.wait_ge(self.s_raw, 16 * self.n * (e + 1))
        if wait:
            pool.wait_ge(self.s_free, e - 1)
            pool.sem_inc(self.s_turn)
        for i in range(self.n):
            hi, lo = self.split[i][j][:, 0, :, :], self.split[i][j][:, 1, :, :]
            pool.tensor_copy(hi, self.raw[i][:, :, :]).then_inc(self.s_split, 1)
            pool.wait_ge(self.s_split, 2 * self.n * e + 2 * i + 1)
            pool.tensor_tensor(lo, self.raw[i][:, :, :], hi, ALU.subtract).then_inc(self.s_split, 1)

    def load_first(self, sp):
        self.load(sp, 0, wait=False)

    def split_first(self, pool):
        self.halves(pool, 0, 0, wait=False)


def expert_stage(nc, S, stage, ring, up_bias, gate_bias, hid):
    M = hid // P
    NB, BT = 4, 4
    W = BT * P
    LAG = 2
    HB = 4
    gated = up_bias is not None
    with Scope(nc, stage) as c:
        nb = 2 if gated else 1
        brow = c.sb("brow", [E * M, nb, P])
        bcol = c.sb("bcol", [P, nb, E * M])
        prime = c.sb("prime", [P, 2, 2])
        acted = c.sb("acted", [P, 2, W])
        prod = c.sb("prod", [P, 2, W]) if gated else acted
        hg = c.sb("hg", [P, HB, 2, W], BF16)
        s_b, s_bT, s_bcol, s_turn = c.sem("b"), c.sem("bT"), c.sem("bcol"), c.sem("turn")
        s_gate, s_up, s_act, s_prod, s_hi, s_lo, s_down, s_y = (
            c.sem(n) for n in ("gate", "up", "act", "prod", "hi", "lo", "down", "y"))
        ps = S.ps
        GB, UB, YB = (0, 1), (2, 3), (4, 5)
        PRIMED = 2
        LOWS = AHEAD if gated else PRIMED
        block = c.block()
        w_gate, w_up, w_down = 0, 1, ring.n - 1

        def over_blocks(eng, body, tail):
            with eng.Fori(0, E // 2) as pair:
                for j in range(2):
                    e = 2 * pair + j
                    body(e, j, 0, first=True)
                    with eng.Fori(1, NB) as tb:
                        body(e, j, tb, first=False)
                    tail(e, j)

        @block.sync
        def _(sp):
            start_ahead(sp, s_y)
            if gated:
                start_ahead(sp, s_lo)
            sp.dma_start(brow[:, 0, :], gate_bias.rearrange("e (m p) -> (e m) p", p=P)).then_inc(s_b, 16)
            if gated:
                sp.dma_start(brow[:, 1, :], up_bias.rearrange("e (m p) -> (e m) p", p=P)).then_inc(s_b, 16)
            with sp.Fori(1, E) as e:
                ring.load(sp, e)

        @block.gpsimd
        def _(pool):
            ring.halves(pool, 1, 1, wait=False)
            with pool.Fori(1, E // 2) as pair:
                for j in range(2):
                    ring.halves(pool, 2 * pair + j, j)

        @block.scalar
        def _(act):
            act.wait_ge(s_bT, 1)
            act.activation(bcol[:, :, :], ps[:, 7, 0:nb * E * M].rearrange("p (b m) -> p b m", b=nb), ACT.Copy).then_inc(s_bcol, 1)
            act.wait_ge(s_bcol, 1)
            for j in range(PRIMED):
                act.activation(prime[:, 0, j:j + 1], bcol[:, 0, 0:1], ACT.Copy).then_inc(s_act, 1)

            def body(e, j, tb, first):
                for m in range(M):
                    s = (e * NB + tb) * M + m
                    act.wait_ge(s_gate, s + 1)
                    act.sem_inc(s_turn)
                    act.activation(acted[:, m % 2, :], ps[:, GB[m % 2], :], ACT.Silu if gated else ACT.Gelu,
                                   bias=bcol[:, 0, ts(e * M + m, 1)]).then_inc(s_act, 1)

            over_blocks(act, body, lambda e, j: None)

        @block.tensor
        def _(pe):
            pe.wait_ge(s_b, 16 * nb)
            for i in range(nb):
                mm = pe.transpose(ps[:, 7, i * E * M:(i + 1) * E * M], brow[:, i, :], S.ident[0:E * M, 0:E * M])
            mm.then_inc(s_bT, 1)

            def up(e, j, tb, m):
                s = (e * NB + tb) * M + m
                if gated:
                    pe.wait_ge(s_prod, s - 1 + PRIMED)
                else:
                    pe.wait_ge(s_act, s - 1 + PRIMED)
                    pe.wait_ge(s_lo, s - 1 + PRIMED)
                for which, bank, ready in ((w_gate, GB[m % 2], s_gate), (w_up, UB[m % 2], s_up))[:nb]:
                    n = 0
                    for wp, ap in PASSES:
                        for k in range(KD):
                            mm = pe.matmul(ps[:, bank, :], ring.split[which][j][:, wp, k, m * P:m * P + P],
                                           S.zt[:, ap, k, ts(tb * W, W)], start=(n == 0), stop=(n == 3 * KD - 1))
                            n += 1
                    mm.then_inc(ready, 1)

            def down(e, j, tb, m):
                s = (e * NB + tb) * M + m
                pe.wait_ge(s_lo, s + 1 + LOWS)
                if m == 0:
                    pe.wait_ge(s_y, e * NB + tb + AHEAD)
                for t in range(BT):
                    n = 0
                    for wp, ap in PASSES:
                        mm = pe.matmul(ps[:, YB[t // 2], (t % 2) * D:(t % 2) * D + D],
                                       hg[:, m % HB, ap, t * P:t * P + P], ring.split[w_down][j][:, wp, m, :],
                                       start=(m == 0 and n == 0 and t % 2 == 0), stop=(m == M - 1 and n == 2),
                                       skip_group_check=True)
                        n += 1
                mm.then_inc(s_down, 1)
                return mm

            def body(e, j, tb, first):
                if first:
                    pe.wait_ge(ring.s_split, 2 * ring.n * (e + 1))
                for m in range(M):
                    up(e, j, tb, m)
                    if m >= LAG:
                        down(e, j, tb, m - LAG)
                    elif not first:
                        down(e, j, tb - 1, M - LAG + m)

            def tail(e, j):
                for m in range(M - LAG, M):
                    mm = down(e, j, NB - 1, m)
                pe.matmul(ps[:, 7, 0:8], hg[:, 0, 0, 0:P], ring.split[w_down][j][:, 0, 0, 0:8], start=True, stop=True
                          ).then_inc(ring.s_free, 1)

            over_blocks(pe, body, tail)

        @block.vector
        def _(dve):
            dve.wait_ge(s_bcol, 1)
            for j in range(PRIMED):
                dve.tensor_copy(prime[:, 1, j:j + 1], bcol[:, 0, 0:1]).then_inc(s_prod if gated else s_lo, 1)

            def hidden(e, tb, m):
                s = (e * NB + tb) * M + m
                if gated:
                    dve.wait_ge(s_lo, s + LOWS)
                    dve.wait_ge(s_up, s + 1)
                    dve.wait_ge(s_act, s + 1 + PRIMED)
                    dve.scalar_tensor_tensor(out=prod[:, m % 2, :], in0=ps[:, UB[m % 2], :],
                                             scalar=bcol[:, 1, ts(e * M + m, 1)], in1=acted[:, m % 2, :],
                                             op0=ALU.add, op1=ALU.mult).then_inc(s_prod, 1)
                    dve.wait_ge(s_prod, s + 1 + PRIMED)
                else:
                    dve.wait_ge(s_act, s + 1 + PRIMED)
                dve.tensor_copy(hg[:, m % HB, 0, :], prod[:, m % 2, :]).then_inc(s_hi, 1)
                dve.wait_ge(s_hi, s + 1)
                dve.tensor_tensor(hg[:, m % HB, 1, :], prod[:, m % 2, :], hg[:, m % HB, 0, :],
                                  ALU.subtract).then_inc(s_lo, 1)

            def collect(e, tb):
                dve.wait_ge(s_down, (e * NB + tb + 1) * M)
                for t in range(BT):
                    b = tb * BT + t
                    x = S.x[:, ts(b, 1), :].squeeze(1)
                    add = dve.scalar_tensor_tensor(out=x, in0=ps[:, YB[t // 2], (t % 2) * D:(t % 2) * D + D],
                                                   scalar=S.cw[:, ts(b, 1), ts(e, 1)].squeeze(1), in1=x,
                                                   op0=ALU.mult, op1=ALU.add)
                add.then_inc(s_y, 1)

            def body(e, j, tb, first):
                for m in range(M):
                    hidden(e, tb, m)
                    if m == LAG - 1 and not first:
                        collect(e, tb - 1)

            over_blocks(dve, body, lambda e, j: collect(e, NB - 1))


class CrossWeights:

    CHUNK = 2048
    SLOTS = 2

    def __init__(self, nc, scope, wq, wkv, wout):
        inner = wq.shape[1]
        self.q = scope.sb("wq", [P, 2, KD, inner], BF16)
        self.kv = scope.sb("wkv", [P, 2, KC, 2 * inner], BF16)
        self.out = scope.sb("wout", [P, 2, inner // P, D], BF16)
        self.raw = scope.sb("xraw", [P, self.SLOTS, self.CHUNK])
        self.s_raw = [scope.sem(f"xraw{i}") for i in range(self.SLOTS)]
        self.s_split = scope.sem("xsplit")
        self.parts = [(wq.rearrange("(k p) h -> p k h", p=P), lambda a: self.q[:, a, :, :])]
        self.parts += [(wkv[k * P:(k + 1) * P, :].unsqueeze(1), lambda a, k=k: self.kv[:, a, k:k + 1, :]) for k in range(KC)]
        self.parts += [(wout.rearrange("(m p) d -> p m d", p=P), lambda a: self.out[:, a, :, :])]
        self.n = 2 * len(self.parts)

    def slot(self, i, like):
        return self.raw[:, i % self.SLOTS, :].rearrange("p (k h) -> p k h", k=like.shape[1])

    def load_first(self, sp):
        for i, (src, _) in enumerate(self.parts):
            if i >= self.SLOTS:
                sp.wait_ge(self.s_split, 2 * (i - self.SLOTS + 1))
            sp.dma_start(self.slot(i, src), src).then_inc(self.s_raw[i % self.SLOTS], 16)

    def split_first(self, pool):
        for i, (src, dst) in enumerate(self.parts):
            pool.wait_ge(self.s_raw[i % self.SLOTS], 16 * (i // self.SLOTS + 1))
            pool.tensor_copy(dst(0), self.slot(i, src)).then_inc(self.s_split, 1)
            pool.wait_ge(self.s_split, 2 * i + 1)
            pool.tensor_tensor(dst(1), self.slot(i, src), dst(0), ALU.subtract).then_inc(self.s_split, 1)


def cross_stage(nc, S, A, cross):
    GB = 4
    NG = NT // GB
    W = GB * P
    INNER = XHEADS * XDH
    MI = INNER // P
    UNITS = XHEADS // 4
    SCALE = XDH ** -0.5
    with Scope(nc, "xa") as c:
        cin = c.sb("cin", [P, GB, CTX])
        ctxT = c.sb("ctxT", [P, 2, KC, W], BF16)
        kt = c.sb("kt", [P, 2, MI, GB, XW], BF16)
        v = c.sb("v", [P, 2, GB, INNER], BF16)
        qt = c.sb("qt", [P, 2, MI, W], BF16)
        nk = c.sb("nk", [P, 3])
        nkh = c.sb("nkh", [P, 2], BF16)
        nv = c.sb("nv", [P, XDH])
        lns = c.sb("lns", [P, D])
        lnb = c.sb("lnb", [P, D])
        mx = c.sb("mx", [P, 2, XHEADS])
        nmx = c.sb("nmx", [P, 2, XHEADS])
        sums = c.sb("sums", [P, 2, XHEADS])
        rsum = c.sb("rsum", [P, XHEADS])
        pexp = c.sb("pexp", [P, 2, 4, XW])
        pt = c.sb("pt", [P, 2, 2, 4 * P], BF16)
        pn = c.sb("pn", [P, 2, XHEADS])
        pnv = c.sb("pnv", [P, XHEADS, XDH])
        o = c.sb("o", [P, XHEADS, XDH])
        ot = c.sb("ot", [P, 2, MI, P], BF16)
        o2 = c.sb("o2", [P, NT, D])
        raw = c.sb("raw", [P, NT, 6])
        tmp = c.sb("tmp", [P, NT])
        t1 = c.sb("t1", [P, 2, D])
        (s_rows, s_cin, s_null, s_xb, s_pj, s_pjh, s_pjl, s_sc, s_max, s_mx, s_ex, s_t, s_th, s_tl, s_pv, s_pn,
         s_pnv, s_osum, s_o, s_rs, s_dve, s_stats, s_var, s_root, s_t1, s_lns, s_turn, s_res) = (
            c.sem(n) for n in ("rows", "cin", "null", "xb", "pj", "pjh", "pjl", "sc", "max", "mx", "ex", "t", "th",
                               "tl", "pv", "pn", "pnv", "osum", "o", "rs", "dve", "stats", "var", "root", "t1",
                               "lns", "turn", "res"))
        ps = S.ps
        block = c.block()

        PJ = ([("ctx", i) for i in range(GB)] + [("k", i) for i in range(MI)]
              + [("v", i) for i in range(2 * GB)] + [("q", i) for i in range(MI)])
        NPJ = len(PJ)
        PBANKS = 4

        def destination(kind, i, part):
            if kind == "ctx":
                return ctxT[:, part, :, i * P:(i + 1) * P], "p (k s) -> p k s", KC
            if kind == "k":
                return kt[:, part, i, :, 0:P], "p (k s) -> p k s", GB
            if kind == "v":
                return v[:, part, i // 2, (i % 2) * 512:(i % 2) * 512 + 512].unsqueeze(1), "p (k s) -> p k s", 1
            return qt[:, part, i, :].unsqueeze(1), "p (k s) -> p k s", 1

        def bank(u, split, k):
            return ps[:, u % PBANKS, :].rearrange(split, k=k)

        HG = GB * UNITS

        def extra(n):
            bb = n // UNITS
            return {2: [("ot", bb - 1, 0)] if bb >= 1 else [], 3: [("ot", bb - 1, 1)] if bb >= 1 else [],
                    0: [("out", bb - 2, 0)] if bb >= 2 else []}.get(n % UNITS, [])

        LAST = GB - 1
        TRAIL = extra(HG) + [("ot", LAST, 0), ("ot", LAST, 1), ("out", LAST, 0)]
        BETWEEN = ([TRAIL[0]] + [("pj", u) for u in range(GB)] + [TRAIL[1], ("pj", GB), TRAIL[2], ("pj", GB + 1), TRAIL[3]]
                   + [("pj", u) for u in range(GB + 2, NPJ)])
        TU = [u for n in range(HG) for u in [("tr", n // UNITS, n % UNITS)] + extra(n)] + TRAIL
        NTU = len(TU)
        LOWS = [u for u in TU if u[0] != "out"]
        NLOW = len(LOWS)

        def heads(u, p):
            return [4 * u + 2 * mm + p for mm in range(2)]

        def over_groups(eng, project, attention, turned):
            for u in range(NPJ):
                project(0, u)
            with eng.Fori(0, NG - 1) as g:
                attention(g)
                for unit in BETWEEN:
                    if unit[0] == "pj":
                        project(g + 1, unit[1])
                    else:
                        turned(g, unit)
            attention(NG - 1)
            for unit in TRAIL:
                turned(NG - 1, unit)

        @block.sync
        def _(sp):
            start_ahead(sp, s_pjl, s_pn, s_osum, s_ex, s_tl, s_th, s_res)
            null = A["L1_xattn_null_kv"]
            for h in range(2):
                sp.dma_start(nk[h * XDH:(h + 1) * XDH, 0:1], null[0].rearrange("(p a) -> p a", a=1)).then_inc(s_rows, 16)
            sp.dma_start(nv[:, :], null[1].partition_broadcast(P)).then_inc(s_rows, 16)
            sp.dma_start(lns[:, :], A["L1_xattn_ln_scale"].partition_broadcast(P)).then_inc(s_rows, 16)
            sp.dma_start(lnb[:, :], A["L1_xattn_ln_bias"].partition_broadcast(P)).then_inc(s_rows, 16)
            sp.dma_start(cin[:, :, :], A["ctx_2048"][0:GB].rearrange("b p d -> p b d")).then_inc(s_cin, 16)
            with sp.Fori(1, NG) as g:
                sp.wait_ge(s_pjl, (g - 1) * NPJ + GB + AHEAD)
                sp.dma_start(cin[:, :, :], A["ctx_2048"][ts(g * GB, GB)].rearrange("b p d -> p b d")).then_inc(s_cin, 16)

        @block.gpsimd
        def _(pool):
            pool.wait_ge(s_lns, 2)
            pool.tensor_tensor(S.x[:, :, :], S.x[:, :, :], lnb[:, :].unsqueeze(1).broadcast_to([P, NT, D]),
                               ALU.add).then_inc(s_xb, 1)
            with pool.Fori(0, NG) as g:
                for bb in range(GB):
                    for u in range(UNITS):
                        n = bb * UNITS + u
                        pool.wait_ge(s_ex, g * GB * UNITS + n + 1 + AHEAD)
                        for p in range(2):
                            hs = heads(u, p)
                            cp = pool.tensor_tensor(pn[:, bb % 2, hs[0]:hs[1] + 1:2], pexp[:, n % 2, 2 * p:2 * p + 2, P],
                                                    nk[:, 2:3].broadcast_to([P, 2]), ALU.mult)
                        cp.then_inc(s_pn, 1)
                    pool.wait_ge(s_pn, g * GB * UNITS + (bb + 1) * UNITS + AHEAD)
                    pool.wait_ge(s_osum, g * GB + bb + AHEAD)
                    pool.tensor_tensor(pnv[:, :, :], pn[:, bb % 2, :].unsqueeze(2).broadcast_to([P, XHEADS, XDH]),
                                       nv[:, :].unsqueeze(1).broadcast_to([P, XHEADS, XDH]), ALU.mult).then_inc(s_pnv, 1)

        @block.scalar
        def _(act):
            def high(g, u):
                kind, i = PJ[u]
                dst, split, k = destination(kind, i, 0)
                act.wait_ge(s_pj, g * NPJ + u + 1)
                act.activation(dst, bank(u, split, k), ACT.Copy).then_inc(s_pjh, 1)

            def exps(g, bb, u):
                n = bb * UNITS + u
                act.wait_ge(s_mx, g * GB * UNITS + n + 1)
                act.wait_ge(s_pn, g * GB * UNITS + max(n - 1, 0) + AHEAD)
                if n >= 2:
                    act.wait_ge(s_t, g * NTU + TU.index(("tr", (n - 2) // UNITS, (n - 2) % UNITS)) + 1)
                for p in range(2):
                    for mm in range(2):
                        h = heads(u, p)[mm]
                        ex = act.activation(pexp[:, n % 2, 2 * p + mm, :], ps[:, 2 * (n % 2) + p, mm * XW:(mm + 1) * XW],
                                            ACT.Exp, bias=nmx[:, bb % 2, h:h + 1], scale=SCALE,
                                            accum_out=sums[:, bb % 2, h:h + 1])
                ex.then_inc(s_ex, 1)

            def turned(g, unit):
                t = TU.index(unit)
                act.wait_ge(s_t, g * NTU + t + 1)
                kind, bb, u = unit
                if kind == "out":
                    act.activation(o2[:, ts(g * GB + bb, 1), :].squeeze(1), ps[:, 4 + t % 2, 0:D], ACT.Copy).then_inc(s_th, 1)
                elif kind == "tr":
                    act.activation(pt[:, u % 2, 0, :], ps[:, 4 + t % 2, :], ACT.Copy).then_inc(s_th, 1)
                else:
                    act.activation(ot[:, 0, 4 * u:4 * u + 4, :], ps[:, 4 + t % 2, :].rearrange("p (k s) -> p k s", k=4),
                                   ACT.Copy).then_inc(s_th, 1)

            def attention(g):
                exps(g, 0, 0)
                for n in range(HG):
                    if n + 1 < HG:
                        exps(g, (n + 1) // UNITS, (n + 1) % UNITS)
                    for unit in [("tr", n // UNITS, n % UNITS)] + extra(n):
                        turned(g, unit)

            over_groups(act, high, attention, turned)
            act.wait_ge(s_var, 1)
            act.activation(S.rstd[:, :], S.rstd[:, :], ACT.Sqrt).then_inc(s_root, 1)

        @block.tensor
        def _(pe):
            def project(g, u):
                kind, i = PJ[u]
                if u >= PBANKS:
                    pe.wait_ge(s_pjl, g * NPJ + u - PBANKS + 1 + AHEAD)
                else:
                    pe.wait_ge(s_ex, g * GB * UNITS + AHEAD)
                out = ps[:, u % PBANKS, :]
                if kind == "ctx":
                    if i == 0:
                        pe.wait_ge(s_cin, 16 * (g + 1))
                    for k in range(KC):
                        mm = pe.transpose(out[:, k * P:k * P + P], cin[:, i, k * P:k * P + P], S.ident[:, :])
                else:
                    if u == GB:
                        pe.wait_ge(s_pjl, g * NPJ + GB + AHEAD)
                        pe.wait_ge(cross.s_split, cross.n)
                    n, ks = 0, KD if kind == "q" else KC
                    for wp, ap in PASSES:
                        for k in range(ks):
                            if kind == "k":
                                lhs, rhs = cross.kv[:, wp, k, i * P:i * P + P], ctxT[:, ap, k, :]
                            elif kind == "v":
                                half = INNER + (i % 2) * 512
                                lhs, rhs = ctxT[:, ap, k, (i // 2) * P:(i // 2) * P + P], cross.kv[:, wp, k, half:half + 512]
                            else:
                                lhs, rhs = cross.q[:, wp, k, i * P:i * P + P], S.zt[:, ap, k, ts(g * W, W)]
                            mm = pe.matmul(out, lhs, rhs, start=(n == 0), stop=(n == 3 * ks - 1))
                            n += 1
                mm.then_inc(s_pj, 1)

            def scores(g, bb, u):
                n = bb * UNITS + u
                if n == 0:
                    pe.wait_ge(s_pjl, (g + 1) * NPJ + AHEAD)
                elif n >= 2:
                    pe.wait_ge(s_ex, g * GB * UNITS + n - 1 + AHEAD)
                for mm in range(2):
                    m = 2 * u + mm
                    for i, (wp, ap) in enumerate(PASSES):
                        for p in range(2):
                            half = slice(p * XDH, (p + 1) * XDH)
                            q = pe.matmul(ps[:, 2 * (n % 2) + p, mm * XW:(mm + 1) * XW],
                                          qt[half, ap, m, bb * P:(bb + 1) * P], kt[half, wp, m, bb, :],
                                          start=(i == 0), stop=(i == 2))
                q.then_inc(s_sc, 1)

            def bank_free(g, t):
                if t < 2:
                    pe.wait_ge(s_tl, g * NLOW + AHEAD)
                    pe.wait_ge(s_th, g * NTU + AHEAD)
                elif TU[t - 2][0] == "out":
                    pe.wait_ge(s_th, g * NTU + t - 1 + AHEAD)
                else:
                    pe.wait_ge(s_tl, g * NLOW + LOWS.index(TU[t - 2]) + 1 + AHEAD)

            def turn(g, unit):
                kind, bb, u = unit
                t = TU.index(unit)
                bank_free(g, t)
                out = ps[:, 4 + t % 2, :]
                if kind == "tr":
                    n = bb * UNITS + u
                    pe.wait_ge(s_ex, g * GB * UNITS + n + 1 + AHEAD)
                    for i in range(4):
                        mm = pe.transpose(out[:, i * P:i * P + P], pexp[:, n % 2, i, 0:P], S.ident[:, :])
                elif kind == "ot":
                    pe.wait_ge(s_o, g * GB + bb + 1)
                    flat = o[:, :, :].rearrange("p h d -> p (h d)")
                    for i in range(4):
                        k = 4 * u + i
                        mm = pe.transpose(out[:, i * P:i * P + P], flat[:, k * P:k * P + P], S.ident[:, :])
                else:
                    pe.wait_ge(s_tl, g * NLOW + LOWS.index(("ot", bb, 1)) + 1 + AHEAD)
                    n = 0
                    for m in range(MI):
                        for wp, ap in PASSES:
                            mm = pe.matmul(out[:, 0:D], ot[:, ap, m, :], cross.out[:, wp, m, :],
                                           start=(n == 0), stop=(n == 3 * MI - 1))
                            n += 1
                mm.then_inc(s_t, 1)

            def values(g, bb, u):
                pe.wait_ge(s_tl, g * NLOW + LOWS.index(("tr", bb, u)) + 1 + AHEAD)
                if u == 0:
                    pe.wait_ge(s_osum, g * GB + bb + AHEAD)
                for p in range(2):
                    for mm in range(2):
                        h = heads(u, p)[mm]
                        at = (h % 8) * XDH
                        for i, (wp, ap) in enumerate(PASSES):
                            q = pe.matmul(ps[:, 6 + h // 8, at:at + XDH],
                                          pt[:, u % 2, ap, (2 * p + mm) * P:(2 * p + mm + 1) * P],
                                          v[:, wp, bb, h * XDH:(h + 1) * XDH], start=(i == 0), stop=(i == 2))
                q.then_inc(s_pv, 1)

            def attention(g):
                scores(g, 0, 0)
                scores(g, 0, 1)
                for n in range(HG):
                    turn(g, ("tr", n // UNITS, n % UNITS))
                    if n + 2 < HG:
                        scores(g, (n + 2) // UNITS, (n + 2) % UNITS)
                    if n >= 1:
                        values(g, (n - 1) // UNITS, (n - 1) % UNITS)
                    for unit in extra(n):
                        turn(g, unit)
                values(g, LAST, UNITS - 1)

            over_groups(pe, project, attention, turn)

        @block.vector
        def _(dve):
            chain = Chain(dve, s_dve)
            dve.wait_ge(s_rows, 80)
            chain.link(dve.tensor_copy(nkh[:, 0:1], nk[:, 0:1]))
            chain.link(dve.tensor_tensor(nkh[:, 1:2], nk[:, 0:1], nkh[:, 0:1], ALU.subtract))
            chain.link(dve.memset(nk[:, 2:3], 1.0))
            for part in range(2):
                chain.link(dve.tensor_copy(kt[:, part, :, :, P], nkh[:, part:part + 1].unsqueeze(2)
                                           .broadcast_to([P, MI, GB])))
            dve.tensor_scalar(lns[:, :], lns[:, :], S.gates[:, 1:2], None, ALU.mult).then_inc(s_lns, 1)
            dve.tensor_scalar(lnb[:, :], lnb[:, :], S.gates[:, 1:2], None, ALU.mult).then_inc(s_lns, 1)

            def low(g, u):
                kind, i = PJ[u]
                dst, split, k = destination(kind, i, 1)
                dve.wait_ge(s_pjh, g * NPJ + u + 1)
                dve.tensor_tensor(dst, bank(u, split, k), destination(kind, i, 0)[0], ALU.subtract).then_inc(s_pjl, 1)

            def maxima(g, bb, u):
                n = bb * UNITS + u
                dve.wait_ge(s_sc, g * GB * UNITS + n + 1)
                for p in range(2):
                    hs = heads(u, p)
                    dve.tensor_reduce(mx[:, bb % 2, hs[0]:hs[1] + 1:2],
                                      ps[:, 2 * (n % 2) + p, 0:2 * XW].rearrange("p (h k) -> p h k", h=2),
                                      AX.X, ALU.max).then_inc(s_max, 1)
                dve.wait_ge(s_max, 2 * (g * GB * UNITS + n + 1))
                dve.tensor_scalar(nmx[:, bb % 2, 4 * u:4 * u + 4], mx[:, bb % 2, 4 * u:4 * u + 4], -SCALE, None,
                                  ALU.mult).then_inc(s_mx, 1)

            def turned(g, unit):
                t = TU.index(unit)
                kind, bb, u = unit
                if kind == "out":
                    return
                dve.wait_ge(s_th, g * NTU + t + 1 + AHEAD)
                if kind == "tr":
                    dve.tensor_tensor(pt[:, u % 2, 1, :], ps[:, 4 + t % 2, :], pt[:, u % 2, 0, :],
                                      ALU.subtract).then_inc(s_tl, 1)
                else:
                    four = slice(4 * u, 4 * u + 4)
                    dve.tensor_tensor(ot[:, 1, four, :], ps[:, 4 + t % 2, :].rearrange("p (k s) -> p k s", k=4),
                                      ot[:, 0, four, :], ALU.subtract).then_inc(s_tl, 1)

            def normalise(g, bb):
                done = g * GB + bb
                dve.reciprocal(rsum[:, :], sums[:, bb % 2, :]).then_inc(s_rs, 1)
                dve.wait_ge(s_pnv, done + 1)
                dve.wait_ge(s_pv, (done + 1) * UNITS)
                dve.tensor_tensor(o[:, :, :], ps[:, 6:8, :].rearrange("p b (h d) -> p (b h) d", d=XDH), pnv[:, :, :],
                                  ALU.add).then_inc(s_osum, 1)
                dve.wait_ge(s_osum, done + 1 + AHEAD)
                dve.wait_ge(s_rs, done + 1)
                dve.tensor_tensor(o[:, :, :], o[:, :, :], rsum[:, :].unsqueeze(2).broadcast_to([P, XHEADS, XDH]),
                                  ALU.mult).then_inc(s_o, 1)

            def attention(g):
                maxima(g, 0, 0)
                maxima(g, 0, 1)
                for n in range(HG):
                    if n + 2 < HG:
                        maxima(g, (n + 2) // UNITS, (n + 2) % UNITS)
                    for unit in [("tr", n // UNITS, n % UNITS)] + extra(n):
                        turned(g, unit)
                    if n % UNITS == 0 and n > 0:
                        normalise(g, n // UNITS - 1)
                normalise(g, LAST)

            over_groups(dve, low, attention, turned)
            dve.wait_ge(s_th, NG * NTU + AHEAD)
            stats_loop(dve, o2, raw, s_stats)
            dve.wait_ge(s_stats, NT)
            combine_stats(dve, chain, raw, S.mean[:, :], S.rstd[:, :], tmp[:, :], D)
            dve.tensor_scalar(S.rstd[:, :], S.rstd[:, :], 1e-6, None, ALU.add).then_inc(s_var, 1)
            dve.wait_ge(s_root, 1)
            chain.link(dve.reciprocal(S.rstd[:, :], S.rstd[:, :]))
            dve.wait_ge(s_xb, 1)
            with dve.Fori(0, NT // 2) as i:
                for j in range(2):
                    b = 2 * i + j
                    x = S.x[:, ts(b, 1), :].squeeze(1)
                    dve.wait_ge(s_res, b + AHEAD)
                    dve.scalar_tensor_tensor(out=t1[:, j, :], in0=o2[:, ts(b, 1), :].squeeze(1), scalar=S.mean[:, ts(b, 1)],
                                             in1=lns[:, :], op0=ALU.subtract, op1=ALU.mult).then_inc(s_t1, 1)
                    dve.wait_ge(s_t1, b + 1)
                    dve.scalar_tensor_tensor(out=x, in0=t1[:, j, :], scalar=S.rstd[:, ts(b, 1)], in1=x,
                                             op0=ALU.mult, op1=ALU.add).then_inc(s_res, 1)


def latent_stage(nc, S, A):
    GB = 4
    NG = NT // GB
    U = LHEADS // 4
    HG = GB * U
    LAT = LHEADS * LDH
    SCALE = LDH ** -0.5
    SB = 3
    with Scope(nc, "la") as c:
        wraw = c.sb("wraw", [P, KD, D + 2 * LAT])
        w = c.sb("w", [P, 2, KD, 3, LAT], BF16)
        ow = c.sb("ow", [LAT, D])
        brow = c.sb("brow", [4, P])
        bcol = c.sb("bcol", [P, 4])
        vrow = c.sb("vrow", [P, LAT])
        ones = c.sb("ones", [P, LHEADS])
        own = c.sb("own", [P, LHEADS])
        qT = c.sb("qT", [P, 2, P])
        kT = c.sb("kT", [P, 2, P])
        km = c.sb("km", [P, 2, LHEADS, P])
        vf = c.sb("vf", [P, 2, LAT])
        v = c.sb("v", [P, 2, 2, LAT], BF16)
        mx = c.sb("mx", [P, 2, LHEADS])
        nmx = c.sb("nmx", [P, 2, LHEADS])
        sums = c.sb("sums", [P, 2, LHEADS])
        rsum = c.sb("rsum", [P, 2, LHEADS])
        pexp = c.sb("pexp", [P, 2, 4, P])
        pt = c.sb("pt", [P, 2, 2, 4 * P], BF16)
        ao = c.sb("ao", [P, 2, LHEADS, LDH])
        aoT = c.sb("aoT", [P, 2, P])
        (s_w, s_b, s_pool, s_split, s_bT, s_bcol, s_pj, s_k, s_v, s_vp, s_km, s_sc, s_max, s_mx, s_ex, s_t, s_th, s_tl,
         s_pv, s_rs, s_ao, s_aoT, s_aoc, s_mla, s_mh, s_ml) = (
            c.sem(n) for n in ("w", "b", "pool", "split", "bT", "bcol", "pj", "k", "v", "vp", "km", "sc", "max", "mx",
                               "ex", "t", "th", "tl", "pv", "rs", "ao", "aoT", "aoc", "mla", "mh", "ml"))
        ps = S.ps
        PJB = 3
        block = c.block()

        @block.sync
        def _(sp):
            start_ahead(sp, s_v, s_ex, s_tl, s_ml)
            rows = lambda m: m.rearrange("(k p) c -> p k c", p=P)
            sp.dma_start(wraw[:, :, 0:D], rows(A["L1_ffn_q_w"])).then_inc(s_w, 16)
            sp.dma_start(wraw[:, :, D:D + LAT], rows(A["L1_ffn_k_w"])).then_inc(s_w, 16)
            sp.dma_start(wraw[:, :, D + LAT:], rows(A["L1_ffn_v_w"])).then_inc(s_w, 16)
            sp.dma_start(brow[0:1, :].rearrange("a (h r) -> a h r", r=LDH),
                         A["L1_ffn_q_b"].rearrange("(a h r) -> a h r", a=1, h=LHEADS)[:, :, 0:LDH]).then_inc(s_b, 16)
            sp.dma_start(brow[1:2, :], A["L1_ffn_k_b"].rearrange("(a n) -> a n", a=1)).then_inc(s_b, 16)
            sp.dma_start(brow[2:4, :], A["L1_ffn_o_b"].rearrange("(a n) -> a n", a=2)).then_inc(s_b, 16)
            sp.dma_start(vrow[:, :], A["L1_ffn_v_b"].partition_broadcast(P)).then_inc(s_b, 16)
            sp.dma_start(ow[:, :], A["L1_ffn_o_w"][0:LAT, :]).then_inc(s_b, 16)

        @block.gpsimd
        def _(pool):
            chain = Chain(pool, s_pool)
            chain.link(pool.memset(ones[:, :], 1.0))
            chain.link(pool.affine_select(out=own[:, :], in_=ones[:, :], compare_op=ALU.is_ge, fill=0.0,
                                          base=0, pattern=[[-LDH, LHEADS]], channel_multiplier=1))
            chain.link(pool.affine_select(out=own[:, :], in_=own[:, :], compare_op=ALU.is_ge, fill=0.0,
                                          base=LDH - 1, pattern=[[LDH, LHEADS]], channel_multiplier=-1))
            chain.link(pool.memset(km[:, :, :, :], 0.0))
            with pool.Fori(0, NG) as g:
                for bb in range(GB):
                    done = g * GB + bb
                    pool.wait_ge(s_k, done + 1)
                    for u in range(U):
                        rows, hs = slice(32 * u, 32 * u + 32), slice(4 * u, 4 * u + 4)
                        q = pool.tensor_tensor(km[rows, bb % 2, hs, :],
                                               kT[rows, bb % 2, :].unsqueeze(1).broadcast_to([32, 4, P]),
                                               own[rows, hs].unsqueeze(2).broadcast_to([32, 4, P]), ALU.mult)
                    q.then_inc(s_km, 1)

        @block.scalar
        def _(act):
            def exps(g, bb, u):
                n = bb * U + u
                act.wait_ge(s_mx, g * HG + n + 1)
                if n >= 2:
                    act.wait_ge(s_t, g * HG + n - 1)
                for i in range(4):
                    h = 4 * u + i
                    ex = act.activation(pexp[:, n % 2, i, :], ps[:, n % SB, i * P:(i + 1) * P], ACT.Exp,
                                        bias=nmx[:, bb % 2, h:h + 1], scale=SCALE, accum_out=sums[:, bb % 2, h:h + 1])
                ex.then_inc(s_ex, 1)

            def turned(g, bb, u):
                n = bb * U + u
                act.wait_ge(s_t, g * HG + n + 1)
                act.activation(pt[:, n % 2, 0, :], ps[:, 4 + n % 2, :], ACT.Copy).then_inc(s_th, 1)

            def output(g, bb):
                tok = (g * GB + bb) * P
                act.wait_ge(s_mla, g * GB + bb + 1)
                for k in range(KD):
                    cp = act.activation(S.zt[:, 0, k, ts(tok, P)], ps[:, 6 + bb % 2, (2 + k) * P:(3 + k) * P], ACT.Identity,
                                        bias=bcol[:, 2 + k:3 + k])
                cp.then_inc(s_mh, 1)

            act.wait_ge(s_bcol, 1)
            with act.Fori(0, NG) as g:
                for bb in range(GB):
                    exps(g, bb, 0)
                    exps(g, bb, 1)
                    turned(g, bb, 0)
                    exps(g, bb, 2)
                    turned(g, bb, 1)
                    if bb > 0:
                        output(g, bb - 1)
                    exps(g, bb, 3)
                    turned(g, bb, 2)
                    turned(g, bb, 3)
                output(g, GB - 1)

        @block.tensor
        def _(pe):
            def project(g, bb):
                done = g * GB + bb
                pe.wait_ge(s_v, done + AHEAD)
                for which in range(3):
                    n = 0
                    for wp, ap in PASSES:
                        for k in range(KD):
                            wk, zk = w[:, wp, k, which, :], S.zt[:, ap, k, ts(done * P, P)]
                            lhs, rhs = (zk, wk) if which == 2 else (wk, zk)
                            mm = pe.matmul(ps[:, PJB, which * P:which * P + P], lhs, rhs, start=(n == 0), stop=(n == 3 * KD - 1))
                            n += 1
                mm.then_inc(s_pj, 1)

            def scores(g, bb, u):
                n = bb * U + u
                if u == 0:
                    pe.wait_ge(s_km, g * GB + bb + 1)
                pe.wait_ge(s_ex, g * HG + max(n - SB + 1, 0) + AHEAD)
                pe.matmul(ps[:, n % SB, :], qT[:, bb % 2, :], km[:, bb % 2, 4 * u:4 * u + 4, :].rearrange("p h k -> p (h k)"),
                          start=True, stop=True).then_inc(s_sc, 1)

            def turn(g, bb, u):
                n = bb * U + u
                pe.wait_ge(s_tl, g * HG + max(n - 1, 0) + AHEAD)
                pe.wait_ge(s_ex, g * HG + n + 1 + AHEAD)
                for i in range(4):
                    mm = pe.transpose(ps[:, 4 + n % 2, i * P:i * P + P], pexp[:, n % 2, i, :], S.ident[:, :])
                mm.then_inc(s_t, 1)

            def values(g, bb, u):
                n = bb * U + u
                if u == 0:
                    pe.wait_ge(s_ml, g * GB + max(bb - 1, 0) + AHEAD)
                    pe.wait_ge(s_v, g * GB + bb + 1 + AHEAD)
                pe.wait_ge(s_tl, g * HG + n + 1 + AHEAD)
                for i in range(4):
                    h = 4 * u + i
                    for j, (wp, ap) in enumerate(PASSES):
                        mm = pe.matmul(ps[:, 6 + bb % 2, h * LDH:(h + 1) * LDH], pt[:, n % 2, ap, i * P:i * P + P],
                                       v[:, bb % 2, wp, h * LDH:(h + 1) * LDH], start=(j == 0), stop=(j == 2))
                mm.then_inc(s_pv, 1)

            def turn_out(g, bb):
                pe.wait_ge(s_ao, g * GB + bb + 1)
                pe.transpose(ps[:, 6 + bb % 2, P:2 * P], ao[:, bb % 2, :, :].rearrange("p h d -> p (h d)"),
                             S.ident[:, :]).then_inc(s_aoT, 1)

            def output(g, bb):
                pe.wait_ge(s_aoc, g * GB + bb + 1)
                for k in range(KD):
                    mm = pe.matmul(ps[:, 6 + bb % 2, (2 + k) * P:(3 + k) * P], ow[:, k * P:k * P + P], aoT[:, bb % 2, :],
                                   start=True, stop=True)
                mm.then_inc(s_mla, 1)

            pe.wait_ge(s_b, 80)
            pe.transpose(ps[:, 0, 0:4], brow[:, :], S.ident[0:4, 0:4]).then_inc(s_bT, 1)
            pe.wait_ge(s_split, 6)
            with pe.Fori(0, NG) as g:
                project(g, 0)
                for bb in range(GB):
                    if bb == 0:
                        pe.wait_ge(s_bcol, 1)
                    scores(g, bb, 0)
                    scores(g, bb, 1)
                    turn(g, bb, 0)
                    if bb > 0:
                        turn_out(g, bb - 1)
                    scores(g, bb, 2)
                    values(g, bb, 0)
                    turn(g, bb, 1)
                    if bb > 0:
                        output(g, bb - 1)
                    scores(g, bb, 3)
                    values(g, bb, 1)
                    turn(g, bb, 2)
                    if bb < GB - 1:
                        project(g, bb + 1)
                    values(g, bb, 2)
                    turn(g, bb, 3)
                    values(g, bb, 3)
                turn_out(g, GB - 1)
                output(g, GB - 1)

        @block.vector
        def _(dve):
            dve.wait_ge(s_w, 48)
            parts = [wraw[:, :, 0:D].rearrange("p k (h r) -> p k h r", r=2 * LDH)[:, :, :, 0:LDH],
                     wraw[:, :, D:D + LAT].rearrange("p k (h r) -> p k h r", r=LDH),
                     wraw[:, :, D + LAT:].rearrange("p k (h r) -> p k h r", r=LDH)]
            for i, part in enumerate(parts):
                for k in range(KD):
                    hi, lo = (w[:, a, k, i, :].rearrange("p (h r) -> p h r", r=LDH) for a in range(2))
                    dve.tensor_copy(hi, part[:, k, :, :]).then_inc(s_vp, 1)
                    dve.wait_ge(s_vp, KD * i + k + 1)
                    dve.tensor_tensor(lo, part[:, k, :, :], hi, ALU.subtract).then_inc(s_split, 1)
            dve.wait_ge(s_bT, 1)
            dve.tensor_copy(bcol[:, :], ps[:, 0, 0:4]).then_inc(s_bcol, 1)
            dve.wait_ge(s_bcol, 1)
            SPLITS = 3 * KD

            def projected(g, bb):
                done = g * GB + bb
                j = bb % 2
                dve.wait_ge(s_pj, done + 1)
                dve.tensor_scalar(qT[:, j, :], ps[:, PJB, 0:P], bcol[:, 0:1], None, ALU.add)
                dve.tensor_scalar(kT[:, j, :], ps[:, PJB, P:2 * P], bcol[:, 1:2], None, ALU.add).then_inc(s_k, 1)
                dve.tensor_tensor(vf[:, j, :], ps[:, PJB, 2 * P:3 * P], vrow[:, :], ALU.add).then_inc(s_vp, 1)
                dve.wait_ge(s_vp, 2 * done + 1 + SPLITS)
                dve.tensor_copy(v[:, j, 0, :], vf[:, j, :]).then_inc(s_vp, 1)
                dve.wait_ge(s_vp, 2 * done + 2 + SPLITS)
                dve.tensor_tensor(v[:, j, 1, :], vf[:, j, :], v[:, j, 0, :], ALU.subtract).then_inc(s_v, 1)

            def maxima(g, bb, u):
                n = bb * U + u
                hs = slice(4 * u, 4 * u + 4)
                dve.wait_ge(s_sc, g * HG + n + 1)
                dve.tensor_reduce(mx[:, bb % 2, hs], ps[:, n % SB, :].rearrange("p (h k) -> p h k", h=4), AX.X,
                                  ALU.max).then_inc(s_max, 1)
                dve.wait_ge(s_max, g * HG + n + 1)
                dve.tensor_scalar(nmx[:, bb % 2, hs], mx[:, bb % 2, hs], -SCALE, None, ALU.mult).then_inc(s_mx, 1)

            def turned(g, bb, u):
                n = bb * U + u
                dve.wait_ge(s_th, g * HG + n + 1)
                dve.tensor_tensor(pt[:, n % 2, 1, :], ps[:, 4 + n % 2, :], pt[:, n % 2, 0, :], ALU.subtract).then_inc(s_tl, 1)

            def normalise(g, bb):
                done = g * GB + bb
                j = bb % 2
                dve.reciprocal(rsum[:, j, :], sums[:, j, :]).then_inc(s_rs, 1)
                dve.wait_ge(s_rs, done + 1)
                dve.wait_ge(s_pv, (done + 1) * U)
                dve.tensor_tensor(ao[:, j, :, :], ps[:, 6 + j, 0:LAT].rearrange("p (h d) -> p h d", d=LDH),
                                  rsum[:, j, :].unsqueeze(2).broadcast_to([P, LHEADS, LDH]), ALU.mult).then_inc(s_ao, 1)

            def copy_out(g, bb):
                dve.wait_ge(s_aoT, g * GB + bb + 1)
                dve.tensor_copy(aoT[:, bb % 2, :], ps[:, 6 + bb % 2, P:2 * P]).then_inc(s_aoc, 1)

            def output(g, bb):
                tok = (g * GB + bb) * P
                dve.wait_ge(s_mh, g * GB + bb + 1)
                for k in range(KD):
                    q = dve.scalar_tensor_tensor(out=S.zt[:, 1, k, ts(tok, P)], in0=ps[:, 6 + bb % 2, (2 + k) * P:(3 + k) * P],
                                                 scalar=bcol[:, 2 + k:3 + k], in1=S.zt[:, 0, k, ts(tok, P)],
                                                 op0=ALU.add, op1=ALU.subtract)
                q.then_inc(s_ml, 1)

            with dve.Fori(0, NG) as g:
                projected(g, 0)
                for bb in range(GB):
                    maxima(g, bb, 0)
                    maxima(g, bb, 1)
                    if bb > 0:
                        normalise(g, bb - 1)
                    turned(g, bb, 0)
                    if bb > 0:
                        copy_out(g, bb - 1)
                    maxima(g, bb, 2)
                    turned(g, bb, 1)
                    if bb > 0:
                        output(g, bb - 1)
                    maxima(g, bb, 3)
                    turned(g, bb, 2)
                    if bb < GB - 1:
                        projected(g, bb + 1)
                    turned(g, bb, 3)
                normalise(g, GB - 1)
                copy_out(g, GB - 1)
                output(g, GB - 1)


def store_stage(nc, S, A, out):
    with Scope(nc, "st") as c:
        s_out = c.sem("out")
        block = c.block()

        @block.sync
        def _(sp):
            for q in range(4):
                sp.dma_start(out[4 * q:4 * q + 4].rearrange("b p d -> p b d"), S.x[:, 4 * q:4 * q + 4, :]).then_inc(s_out, 16)
            sp.wait_ge(s_out, 64)


def build(nc, A, out, upto=99, skip=0):
    with Scope(nc, "g") as g:
        S = Shared(nc, g)
        depool_stage(nc, S, A)
        if skip <= 1 and upto >= 2:
            with Scope(nc, "r0") as r:
                ring = Ring(nc, r, [A["L0_ffn_W1"], A["L0_ffn_W0"], A["L0_ffn_W2"]])
                norm_stage(nc, S, "n0", prefetch=ring)
                gate_stage(nc, S, "g0", A, A["L0_ffn_Wg"], A["L0_ffn_bg"], A["L0_ffn_b2"], 2, False)
                expert_stage(nc, S, "e0", ring, A["L0_ffn_b0"], A["L0_ffn_b1"], 1024)
        if skip <= 2 and upto >= 3:
            with Scope(nc, "r1") as r:
                cross = CrossWeights(nc, r, A["L1_xattn_Wq"], A["L1_xattn_Wkv"], A["L1_xattn_Wout"])
                norm_stage(nc, S, "n1", prefetch=cross)
                cross_stage(nc, S, A, cross)
        if upto >= 4:
            with Scope(nc, "r2") as r:
                ring = Ring(nc, r, [A["L1_ffn_w1"], A["L1_ffn_w2"]])
                norm_stage(nc, S, "n2", prefetch=ring, residual=3)
                latent_stage(nc, S, A)
                gate_stage(nc, S, "g1", A, A["L1_ffn_router_w"], A["L1_ffn_router_b"], A["L1_ffn_b2"], 3, True, 0.3)
                expert_stage(nc, S, "e1", ring, None, A["L1_ffn_b1"], 512)
        store_stage(nc, S, A, out)


_INS = ["x", "ctx_2048", "mask_BxS2_if0", "g_xattn", "g_ffn", "L0_xattn_W_in", "L0_xattn_b_in", "L0_xattn_g_res",
        "L0_xattn_g_init", "L0_ffn_Wg", "L0_ffn_bg", "L0_ffn_W0", "L0_ffn_b0", "L0_ffn_W1", "L0_ffn_b1", "L0_ffn_W2",
        "L0_ffn_b2", "L1_xattn_Wq", "L1_xattn_Wkv", "L1_xattn_null_kv", "L1_xattn_Wout", "L1_xattn_ln_scale",
        "L1_xattn_ln_bias", "L1_ffn_q_w", "L1_ffn_q_b", "L1_ffn_k_w", "L1_ffn_k_b", "L1_ffn_v_w", "L1_ffn_v_b",
        "L1_ffn_o_w", "L1_ffn_o_b", "L1_ffn_router_w", "L1_ffn_router_b", "L1_ffn_w1", "L1_ffn_b1", "L1_ffn_w2",
        "L1_ffn_b2"]


def kernel(**inputs):
    import numpy as _np
    import concourse.bacc as _bacc
    from concourse import mybir as _mybir
    from concourse.bass_utils import run_bass_kernel_spmd as _run

    nc = _bacc.Bacc("TRN2", target_bir_lowering=False, num_devices=1)
    arrays, args = {}, {}
    for name in _INS:
        a = _np.ascontiguousarray(inputs[name])
        arrays[f"in_{name}_dram"] = a
        args[name] = nc.dram_tensor(f"in_{name}_dram", a.shape, _mybir.dt.from_np(a.dtype), kind="ExternalInput").ap()
    out = nc.dram_tensor("out_0_dram", (NT, P, D), F32, kind="ExternalOutput").ap()
    build(nc, args, out)
    r = _run(nc, [arrays], core_ids=[0])
    return r.results[0]["out_0_dram"]
```

```python
import math
from contextlib import ExitStack

import concourse.bass as bass
from concourse import mybir

F32 = mybir.dt.float32
BF16 = mybir.dt.bfloat16
I32 = mybir.dt.int32
ACT = mybir.ActivationFunctionType
ALU = mybir.AluOpType
AX = mybir.AxisListType

P = 128
NT = 16
T = NT * P
D = 256
KD = D // P
CTX = 512
KC = CTX // P
E = 8
PASSES = ((0, 0), (0, 1), (1, 0))
LN_EPS = 1e-5
RMS_EPS = 1e-5
DECAY_EPS = 0.001
DECAY_DT = -math.log(-math.expm1(-DECAY_EPS))
XHEADS, XDH = 16, 64
LHEADS, LDH = 16, 8
XW = P + 1


def ts(start, size):
    return bass.ds(start, size)


AHEAD = 1


def start_ahead(sp, *sems):
    for sem in sems:
        sp.sem_inc(sem, AHEAD)


def wait_past_zero(eng, sem, value):
    if not isinstance(value, int) or value > 0:
        eng.wait_ge(sem, value)


class Chain:

    def __init__(self, eng, sem):
        self.eng, self.sem, self.n = eng, sem, 0

    def link(self, ins):
        self.n += 1
        ins.then_inc(self.sem, 1)
        self.eng.wait_ge(self.sem, self.n)


class Scope(ExitStack):

    def __init__(self, nc, stage):
        super().__init__()
        self.nc, self.stage, self.sems = nc, stage, []
        self.callback(self.clear)

    def sb(self, name, shape, dt=F32):
        return self.enter_context(self.nc.sbuf_tensor(f"{self.stage}_{name}", shape, dt))

    def sem(self, name):
        self.sems.append(self.nc.alloc_semaphore(f"{self.stage}_{name}"))
        return self.sems[-1]

    def clear(self):
        if self.sems:
            self.nc.clear_and_free_semaphores(self.sems)
            self.nc.all_engine_barrier()

    def block(self):
        return self.enter_context(self.nc.Block())


class Shared:

    def __init__(self, nc, scope):
        self.ps = scope.enter_context(nc.psum_tensor("banks", [P, 8, 512], F32))
        self.x = scope.sb("x_res", [P, NT, D])
        self.zt = scope.sb("zt", [P, 2, KD, T], BF16)
        self.ident = scope.sb("ident", [P, P])
        self.gates = scope.sb("gates", [P, 4])
        self.cw = scope.sb("cw", [P, NT, E])
        self.mean = scope.sb("mean", [P, NT])
        self.rstd = scope.sb("rstd", [P, NT])


def tile_stats(eng, src, raw, done):
    for b in range(NT):
        eng.bn_stats(raw[:, b, :], src[:, b, :]).then_inc(done, 1)


def combine_stats(eng, chain, raw, mean, var, tmp, width):
    half = width // 2
    me, mo, ve, vo = raw[:, :, 1], raw[:, :, 4], raw[:, :, 2], raw[:, :, 5]
    chain.link(eng.tensor_tensor(mean, me, mo, ALU.add))
    chain.link(eng.tensor_scalar(mean, mean, 0.5, None, ALU.mult))
    chain.link(eng.tensor_tensor(tmp, me, mo, ALU.subtract))
    chain.link(eng.tensor_tensor(tmp, tmp, tmp, ALU.mult))
    chain.link(eng.tensor_tensor(var, ve, vo, ALU.add))
    chain.link(eng.tensor_scalar(var, var, 1.0 / width, None, ALU.mult))
    chain.link(eng.scalar_tensor_tensor(out=var, in0=tmp, scalar=0.25, in1=var, op0=ALU.mult, op1=ALU.add))


def depool_stage(nc, S, A):
    with Scope(nc, "dp") as c:
        ctx = c.sb("ctx", [P, NT, CTX])
        lens = c.sb("lens", [NT, 2, P], I32)
        bidx = c.sb("bidx", [NT, 3, P])
        idxT = c.sb("idxT", [P, NT])
        iota_i = c.sb("iota_i", [P, P], I32)
        iota_s = c.sb("iota_s", [P, P])
        part_i = c.sb("part_i", [P, 1], I32)
        part = c.sb("part", [P, 1])
        ones = c.sb("ones", [P, P], BF16)
        tri = c.sb("tri", [P, P], BF16)
        hot = c.sb("hot", [P, NT, P], BF16)
        hit = c.sb("hit", [P, NT])
        diff = c.sb("diff", [P, NT, P])
        decay = c.sb("decay", [P, NT, P])
        win = c.sb("win", [P, KD, D])
        winT = c.sb("winT", [P, KD, D])
        gres = c.sb("gres", [P, KD])
        ginit = c.sb("ginit", [P, D])
        bin_row = c.sb("bin_row", [P, D])
        graw = c.sb("graw", [P, 4])
        raw = c.sb("raw", [P, NT, 6])
        var = c.sb("var", [P, 2, NT])
        tmp = c.sb("tmp", [P, NT])
        ssq = c.sb("ssq", [P, NT])
        rctx = c.sb("rctx", [P, NT])
        sq = c.sb("sq", [P, 2, CTX])
        z = c.sb("z", [P, 2, D])
        zT = c.sb("zT", [P, 2, D])
        pick = c.sb("pick", [P, 2, P])
        cg = c.sb("cg", [P, 2, D])
        xb = c.sb("xb", [P, 2, D])

        s_len, s_win, s_rows, s_x, s_ctx = (c.sem(n) for n in ("len", "win", "rows", "x", "ctx"))
        s_pool = c.sem("pool")
        s_dve = c.sem("dve")
        s_idx, s_idxT, s_hot, s_hits, s_step, s_cum, s_diff = (
            c.sem(n) for n in ("idx", "idxT", "hot", "hits", "step", "cum", "diff"))
        s_decay, s_wT, s_wTs, s_stats, s_var, s_root, s_ssq, s_act = (
            c.sem(n) for n in ("decay", "wT", "wTs", "stats", "var", "root", "ssq", "act"))
        s_rstd, s_gate, s_bias = c.sem("rstd"), c.sem("gate"), c.sem("bias")
        s_z, s_zt, s_ztc, s_pick, s_out, s_xb, s_res = (
            c.sem(n) for n in ("z", "zt", "ztc", "pick", "out", "xb", "res"))
        ps = S.ps
        block = c.block()
        CONSTS = 7

        @block.sync
        def _(sp):
            start_ahead(sp, s_act, s_out, s_ztc, s_zt)
            sp.dma_start(lens[:, 0, :], A["mask_BxS2_if0"]).then_inc(s_len, 16)
            for q in range(4):
                sp.dma_start(S.x[:, 4 * q:4 * q + 4, :],
                             A["x"][4 * q:4 * q + 4].rearrange("b p d -> p b d")).then_inc(s_x, 16)
            sp.dma_start(win[:, :, :], A["L0_xattn_W_in"].rearrange("(c p) d -> p c d", p=P)).then_inc(s_win, 16)
            for q in range(4):
                sp.dma_start(ctx[:, 4 * q:4 * q + 4, :],
                             A["ctx_2048"][4 * q:4 * q + 4].rearrange("b p d -> p b d")).then_inc(s_ctx, 16)

        @block.gpsimd
        def _(pool):
            chain = Chain(pool, s_pool)
            chain.link(pool.memset(S.ident[:, :], 0.0))
            chain.link(pool.affine_select(out=S.ident[:, :], in_=S.ident[:, :], compare_op=ALU.not_equal, fill=1.0,
                                          base=0, pattern=[[-1, P]], channel_multiplier=1))
            chain.link(pool.iota(iota_i[:, :], pattern=[[1, P]], base=0, channel_multiplier=0))
            chain.link(pool.iota(part_i[:, :], pattern=[[0, 1]], base=0, channel_multiplier=1))
            chain.link(pool.memset(ones[:, :], 1.0))
            chain.link(pool.memset(tri[:, :], 1.0))
            chain.link(pool.affine_select(out=tri[:, :], in_=tri[:, :], compare_op=ALU.is_ge, fill=0.0,
                                          base=0, pattern=[[1, P]], channel_multiplier=-1))
            assert chain.n == CONSTS
            pool.wait_ge(s_bias, 1)
            pool.wait_ge(s_x, 64)
            with pool.Fori(0, NT // 2) as i:
                for j in range(2):
                    b = 2 * i + j
                    pool.wait_ge(s_res, b + 1)
                    pool.tensor_tensor(xb[:, j, :], S.x[:, ts(b, 1), :].squeeze(1), bin_row[:, :],
                                       ALU.add).then_inc(s_xb, 1)

        @block.scalar
        def _(act):
            act.dma_start(graw[:, 0:2], A["g_xattn"].partition_broadcast(P)).then_inc(s_rows, 16)
            act.dma_start(graw[:, 2:4], A["g_ffn"].partition_broadcast(P)).then_inc(s_rows, 16)
            act.dma_start(ginit[:, :], A["L0_xattn_g_init"][0:D].partition_broadcast(P)).then_inc(s_rows, 16)
            act.dma_start(bin_row[:, :], A["L0_xattn_b_in"].partition_broadcast(P)).then_inc(s_rows, 16)
            for k in range(KD):
                act.dma_start(gres[:, k:k + 1],
                              A["L0_xattn_g_res"][k * P:(k + 1) * P].rearrange("(p a) -> p a", a=1)).then_inc(s_rows, 16)
            act.wait_ge(s_rows, 96)
            act.activation(S.gates[:, :], graw[:, :], ACT.Tanh).then_inc(s_gate, 1)
            act.wait_ge(s_ctx, 64)
            with act.Fori(0, NT // 2) as i:
                for j in range(2):
                    b = 2 * i + j
                    act.wait_ge(s_act, b + AHEAD)
                    act.activation(sq[:, j, :], ctx[:, ts(b, 1), :].squeeze(1), ACT.Square,
                                   accum_out=ssq[:, ts(b, 1)]).then_inc(s_act, 1)
            act.wait_ge(s_var, 1)
            act.activation(S.rstd[:, :], var[:, 0, :], ACT.Sqrt).then_inc(s_root, 1)
            act.activation(rctx[:, :], var[:, 1, :], ACT.Sqrt).then_inc(s_root, 1)
            act.wait_ge(s_diff, 1)
            act.activation(decay[:, :, :], decay[:, :, :], ACT.Exp, scale=-DECAY_DT).then_inc(s_decay, 1)
            with act.Fori(0, NT // 2) as i:
                for j in range(2):
                    b = 2 * i + j
                    act.wait_ge(s_zt, b + 1 + AHEAD)
                    act.wait_ge(s_out, b + AHEAD)
                    act.activation(zT[:, j, :], ps[:, j, 0:D], ACT.Copy).then_inc(s_ztc, 1)

        @block.tensor
        def _(pe):
            pe.wait_ge(s_pool, CONSTS)
            pe.wait_ge(s_win, 16)
            for k in range(KD):
                for e in range(KD):
                    mm = pe.transpose(ps[:, 7, k * D + e * P:k * D + e * P + P], win[:, e, k * P:k * P + P], S.ident[:, :])
            mm.then_inc(s_wT, 1)
            pe.wait_ge(s_idx, 1)
            pe.transpose(ps[:, 6, 0:NT], bidx[:, 2, :], S.ident[0:NT, 0:NT]).then_inc(s_idxT, 1)
            pe.wait_ge(s_hot, 1)
            for b in range(NT):
                mm = pe.matmul(ps[:, 5, b:b + 1], hot[:, b, :], ones[:, 0:1], start=True, stop=True)
            mm.then_inc(s_hits, 1)
            pe.wait_ge(s_step, 1)
            for q in range(4):
                mm = pe.matmul(ps[:, q, :], ones[:, :], hot[:, 4 * q:4 * q + 4, :].rearrange("p b s -> p (b s)"),
                               start=True, stop=True)
            mm.then_inc(s_cum, 1)
            pe.wait_ge(s_diff, 1)
            pe.wait_ge(s_wTs, 1)
            with pe.Fori(0, NT // 2) as i:
                for j in range(2):
                    b = 2 * i + j
                    pe.wait_ge(s_z, b + 1)
                    if j == 0:
                        pe.wait_ge(s_ztc, b + AHEAD)
                    else:
                        pe.wait_ge(s_ztc, b + AHEAD)
                    for k in range(KD):
                        mm = pe.transpose(ps[:, j, k * P:k * P + P], z[:, j, k * P:k * P + P], S.ident[:, :])
                    mm.then_inc(s_zt, 1)
                    pe.wait_ge(s_pick, b + 1)
                    pe.wait_ge(s_res, b + 1)
                    pe.matmul(ps[:, 2 + j, 0:D], pick[:, j, :], cg[:, j, :], start=True, stop=False)
                    pe.wait_ge(s_ztc, b + 1 + AHEAD)
                    for k in range(KD):
                        mm = pe.matmul(ps[:, 2 + j, 0:D], zT[:, j, k * P:k * P + P], winT[:, k, :],
                                       start=False, stop=(k == KD - 1))
                    mm.then_inc(s_out, 1)

        @block.vector
        def _(dve):
            chain = Chain(dve, s_dve)
            dve.wait_ge(s_len, 16)
            src = 0
            for step in (1, 2, 4, 8, 16, 32, 64):
                a, b = lens[:, src, :], lens[:, 1 - src, :]
                chain.link(dve.tensor_copy(b[:, 0:step], a[:, 0:step]))
                chain.link(dve.tensor_tensor(b[:, step:P], a[:, step:P], a[:, 0:P - step], ALU.add))
                src = 1 - src
            chain.link(dve.tensor_copy(bidx[:, 0, :], lens[:, src, :]))
            chain.link(dve.tensor_scalar(bidx[:, 0, :], bidx[:, 0, :], -1.0, None, ALU.add))
            chain.link(dve.tensor_scalar(bidx[:, 1, :], bidx[:, 0, :], 0.0, float(P), ALU.is_lt, ALU.mult))
            dve.tensor_tensor(bidx[:, 2, :], bidx[:, 0, :], bidx[:, 1, :], ALU.add).then_inc(s_idx, 1)
            dve.wait_ge(s_pool, CONSTS)
            chain.link(dve.tensor_copy(iota_s[:, :], iota_i[:, :]))
            chain.link(dve.tensor_copy(part[:, :], part_i[:, :]))
            dve.wait_ge(s_idxT, 1)
            chain.link(dve.tensor_copy(idxT[:, :], ps[:, 6, 0:NT]))
            dve.tensor_tensor(hot[:, :, :], iota_s[:, :].unsqueeze(1).broadcast_to([P, NT, P]),
                              idxT[:, :].unsqueeze(2).broadcast_to([P, NT, P]), ALU.is_equal).then_inc(s_hot, 1)
            dve.wait_ge(s_wT, 1)
            dve.wait_ge(s_rows, 96)
            for k in range(KD):
                w = dve.tensor_scalar(winT[:, k, :], ps[:, 7, k * D:k * D + D], gres[:, k:k + 1], None, ALU.mult)
            w.then_inc(s_wTs, 1)
            dve.wait_ge(s_hits, 1)
            chain.link(dve.tensor_scalar(hit[:, :], ps[:, 5, 0:NT], 1.0, None, ALU.min))
            dve.tensor_tensor(hot[:, :, :], tri[:, :].unsqueeze(1).broadcast_to([P, NT, P]),
                              hit[:, :].unsqueeze(2).broadcast_to([P, NT, P]), ALU.mult).then_inc(s_step, 1)
            dve.wait_ge(s_x, 64)
            tile_stats(dve, S.x, raw, s_stats)
            dve.wait_ge(s_stats, NT)
            combine_stats(dve, chain, raw, S.mean[:, :], var[:, 0, :], tmp[:, :], D)
            chain.link(dve.tensor_scalar(var[:, 0, :], var[:, 0, :], 1.0 + RMS_EPS, RMS_EPS * LN_EPS, ALU.mult, ALU.add))
            dve.wait_ge(s_act, NT + AHEAD)
            dve.tensor_scalar(var[:, 1, :], ssq[:, :], 1.0 / CTX, RMS_EPS, ALU.mult, ALU.add).then_inc(s_var, 1)
            dve.wait_ge(s_cum, 1)
            for q in range(4):
                chain.link(dve.tensor_scalar(diff[:, 4 * q:4 * q + 4, :].rearrange("p b s -> p (b s)"), ps[:, q, :],
                                             -1.0, 0.0, ALU.add, ALU.max))
            chain.link(dve.tensor_scalar(diff[:, :, :], diff[:, :, :], float(P - 1), part[:, :], ALU.min, ALU.subtract))
            dve.tensor_scalar(decay[:, :, :], diff[:, :, :], 0.0, None, ALU.max).then_inc(s_diff, 1)
            dve.wait_ge(s_root, 2)
            chain.link(dve.reciprocal(S.rstd[:, :], S.rstd[:, :]))
            chain.link(dve.reciprocal(rctx[:, :], rctx[:, :]))
            chain.link(dve.tensor_scalar(rctx[:, :], rctx[:, :], math.exp(-DECAY_EPS), None, ALU.mult))
            dve.wait_ge(s_gate, 1)
            dve.tensor_scalar(bin_row[:, :], bin_row[:, :], S.gates[:, 0:1], None, ALU.mult).then_inc(s_bias, 1)
            dve.wait_ge(s_bias, 1)
            dve.tensor_copy(tmp[:, 0:1], part[:, :]).then_inc(s_res, 1)
            dve.tensor_copy(tmp[:, 1:2], part[:, :]).then_inc(s_res, 1)
            dve.wait_ge(s_decay, 1)

            def finish(b, j):
                dve.wait_ge(s_out, b + 1 + AHEAD)
                dve.wait_ge(s_xb, b + 1)
                dve.scalar_tensor_tensor(out=S.x[:, ts(b, 1), :].squeeze(1), in0=ps[:, 2 + j, 0:D],
                                         scalar=S.gates[:, 0:1], in1=xb[:, j, :],
                                         op0=ALU.mult, op1=ALU.add).then_inc(s_res, 1)

            with dve.Fori(0, NT // 2) as i:
                for j in range(2):
                    b = 2 * i + j
                    dve.wait_ge(s_zt, b + AHEAD)
                    dve.tensor_scalar(z[:, j, :], S.x[:, ts(b, 1), :].squeeze(1), S.mean[:, ts(b, 1)],
                                      S.rstd[:, ts(b, 1)], ALU.subtract, ALU.mult).then_inc(s_z, 1)
                    dve.wait_ge(s_out, b + AHEAD)
                    dve.scalar_tensor_tensor(out=cg[:, j, :], in0=ctx[:, ts(b, 1), 0:D].squeeze(1),
                                             scalar=rctx[:, ts(b, 1)], in1=ginit[:, :], op0=ALU.mult, op1=ALU.mult)
                    dve.scalar_tensor_tensor(out=pick[:, j, :], in0=diff[:, ts(b, 1), :].squeeze(1), scalar=0.0,
                                             in1=decay[:, ts(b, 1), :].squeeze(1),
                                             op0=ALU.is_ge, op1=ALU.mult).then_inc(s_pick, 1)
                    finish(b, j)


def norm_stage(nc, S, stage, prefetch=None, residual=None):
    UNITS, DEEP, LAG = NT // 2, 4, 2
    with Scope(nc, stage) as c:
        raw = c.sb("raw", [P, NT, 6])
        tmp = c.sb("tmp", [P, NT])
        z = c.sb("z", [P, DEEP, 2, D])
        s_dve, s_stats, s_var, s_root = (c.sem(n) for n in ("dve", "stats", "var", "root"))
        s_z, s_tr, s_hi, s_lo, s_res = (c.sem(n) for n in ("z", "tr", "hi", "lo", "res"))
        ps = S.ps
        block = c.block()

        def bank(u):
            return ps[:, u % DEEP, :].rearrange("p (t k s) -> p k t s", t=2, k=KD)

        def part(u, a):
            return S.zt[:, a, :, 2 * u * P:(2 * u + 2) * P].rearrange("p k (t s) -> p k t s", t=2)

        if prefetch:
            @block.sync
            def _(sp):
                prefetch.load_first(sp)

            @block.gpsimd
            def _(pool):
                prefetch.split_first(pool)

        @block.scalar
        def _(act):
            act.wait_ge(s_var, 1)
            act.activation(S.rstd[:, :], S.rstd[:, :], ACT.Sqrt).then_inc(s_root, 1)
            for u in range(UNITS):
                act.wait_ge(s_tr, u + 1)
                act.activation(part(u, 0), bank(u), ACT.Copy).then_inc(s_hi, 1)

        @block.tensor
        def _(pe):
            for u in range(UNITS):
                pe.wait_ge(s_z, 2 * u + 2)
                if u >= DEEP:
                    pe.wait_ge(s_lo, u - DEEP + 1)
                for t in range(2):
                    for k in range(KD):
                        mm = pe.transpose(ps[:, u % DEEP, (t * KD + k) * P:(t * KD + k + 1) * P],
                                          z[:, u % DEEP, t, k * P:k * P + P], S.ident[:, :])
                mm.then_inc(s_tr, 1)

        @block.vector
        def _(dve):
            chain = Chain(dve, s_dve)
            tile_stats(dve, S.x, raw, s_stats)
            dve.wait_ge(s_stats, NT)
            combine_stats(dve, chain, raw, S.mean[:, :], S.rstd[:, :], tmp[:, :], D)
            dve.tensor_scalar(S.rstd[:, :], S.rstd[:, :], LN_EPS, None, ALU.add).then_inc(s_var, 1)
            dve.wait_ge(s_root, 1)
            chain.link(dve.reciprocal(S.rstd[:, :], S.rstd[:, :]))
            for u in range(UNITS + LAG):
                if u < UNITS:
                    for t in range(2):
                        b = 2 * u + t
                        dve.tensor_scalar(z[:, u % DEEP, t, :], S.x[:, b, :], S.mean[:, b:b + 1], S.rstd[:, b:b + 1],
                                          ALU.subtract, ALU.mult).then_inc(s_z, 1)
                if u >= LAG:
                    dve.wait_ge(s_hi, u - LAG + 1)
                    dve.tensor_tensor(part(u - LAG, 1), bank(u - LAG), part(u - LAG, 0), ALU.subtract).then_inc(s_lo, 1)
                if residual is not None and u < UNITS:
                    dve.wait_ge(s_z, 2 * u + 2)
                    for t in range(2):
                        x = S.x[:, 2 * u + t, :]
                        dve.scalar_tensor_tensor(out=x, in0=z[:, u % DEEP, t, :], scalar=S.gates[:, residual:residual + 1],
                                                 in1=x, op0=ALU.mult, op1=ALU.add).then_inc(s_res, 1)


def gate_stage(nc, S, stage, A, wg, bg, b2, gate, top_of_probs, factor=1.0, prefetch=None):
    with Scope(nc, stage) as c:
        wraw = c.sb("wraw", [P, KD, E])
        w = c.sb("w", [P, 2, KD, E], BF16)
        brow = c.sb("brow", [P, E])
        b2rep = c.sb("b2rep", [P, D])
        ones = c.sb("ones", [P, NT])
        own = c.sb("own", [P, NT])
        earlier = c.sb("earlier", [P, E, E])
        lg = c.sb("lg", [P, NT, E])
        top = c.sb("top", [P, NT])
        pr = c.sb("pr", [P, NT, E])
        beat = c.sb("beat", [P, NT, E, E])
        tie = c.sb("tie", [P, NT, E, E])
        rank = c.sb("rank", [P, NT, E])
        scale = c.sb("scale", [P, 1])
        cwT = c.sb("cwT", [P, P])
        rhs = c.sb("rhs", [P, NT, D])
        s_w, s_b2, s_pool, s_dve, s_split = (c.sem(n) for n in ("w", "b2", "pool", "dve", "split"))
        s_lg, s_sub, s_exp, s_cw, s_cwT, s_cwTs, s_rhs, s_bias, s_res = (
            c.sem(n) for n in ("lg", "sub", "exp", "cw", "cwT", "cwTs", "rhs", "bias", "res"))
        ps = S.ps
        block = c.block()
        BANKS = 4

        @block.sync
        def _(sp):
            sp.dma_start(wraw[:, :, :], wg.rearrange("(k p) e -> p k e", p=P)).then_inc(s_w, 16)
            sp.dma_start(brow[:, :], bg.partition_broadcast(P)).then_inc(s_w, 16)
            for t in range(NT):
                sp.dma_start(b2rep[E * t:E * t + E, :], b2).then_inc(s_b2, 16)

        @block.gpsimd
        def _(pool):
            chain = Chain(pool, s_pool)
            chain.link(pool.memset(ones[:, :], 1.0))
            chain.link(pool.affine_select(out=own[:, :], in_=ones[:, :], compare_op=ALU.is_ge, fill=0.0,
                                          base=0, pattern=[[-E, NT]], channel_multiplier=1))
            chain.link(pool.affine_select(out=own[:, :], in_=own[:, :], compare_op=ALU.is_ge, fill=0.0,
                                          base=E - 1, pattern=[[E, NT]], channel_multiplier=-1))
            chain.link(pool.memset(earlier[:, :, :], 1.0))
            chain.link(pool.affine_select(out=earlier[:, :, :], in_=earlier[:, :, :], compare_op=ALU.is_ge, fill=0.0,
                                          base=-1, pattern=[[1, E], [-1, E]], channel_multiplier=0))
            pool.wait_ge(s_b2, 16 * NT)
            for u in range(NT // 2):
                pool.tensor_tensor(rhs[:, 2 * u:2 * u + 2, :], b2rep[:, :].unsqueeze(1).broadcast_to([P, 2, D]),
                                   own[:, 2 * u:2 * u + 2].unsqueeze(2).broadcast_to([P, 2, D]), ALU.mult).then_inc(s_rhs, 1)

        @block.scalar
        def _(act):
            act.wait_ge(s_sub, 1)
            act.activation(pr[:, :, :], pr[:, :, :], ACT.Exp).then_inc(s_exp, 1)

        @block.tensor
        def _(pe):
            pe.wait_ge(s_split, 2)
            for b in range(NT):
                n = 0
                for wp, ap in PASSES:
                    for k in range(KD):
                        mm = pe.matmul(ps[:, 7, b * E:b * E + E], S.zt[:, ap, k, b * P:b * P + P], w[:, wp, k, :],
                                       start=(n == 0), stop=(n == 3 * KD - 1))
                        n += 1
            mm.then_inc(s_lg, 1)
            pe.wait_ge(s_cw, 1)
            pe.transpose(ps[:, 6, 0:P], S.cw[:, :, :].rearrange("p t e -> p (t e)"), S.ident[:, :]).then_inc(s_cwT, 1)
            pe.wait_ge(s_cwTs, 1)
            for u in range(NT // 2):
                pe.wait_ge(s_rhs, u + 1)
                if u >= BANKS:
                    pe.wait_ge(s_res, u - BANKS + 1)
                pe.matmul(ps[:, u % BANKS, :], cwT[:, :], rhs[:, 2 * u:2 * u + 2, :].rearrange("p t d -> p (t d)"),
                          start=True, stop=True).then_inc(s_bias, 1)

        @block.vector
        def _(dve):
            chain = Chain(dve, s_dve)
            dve.wait_ge(s_w, 32)
            dve.tensor_copy(w[:, 0, :, :], wraw[:, :, :]).then_inc(s_split, 1)
            dve.wait_ge(s_split, 1)
            dve.tensor_tensor(w[:, 1, :, :], wraw[:, :, :], w[:, 0, :, :], ALU.subtract).then_inc(s_split, 1)
            dve.wait_ge(s_lg, 1)
            chain.link(dve.tensor_tensor(lg[:, :, :], ps[:, 7, 0:NT * E].rearrange("p (t e) -> p t e", e=E),
                                         brow[:, :].unsqueeze(1).broadcast_to([P, NT, E]), ALU.add))
            chain.link(dve.tensor_reduce(top[:, :], lg[:, :, :], AX.X, ALU.max))
            dve.tensor_tensor(pr[:, :, :], lg[:, :, :], top[:, :].unsqueeze(2).broadcast_to([P, NT, E]),
                              ALU.subtract).then_inc(s_sub, 1)
            dve.wait_ge(s_exp, 1)
            dve.wait_ge(s_pool, 5)

            def share(values):
                chain.link(dve.tensor_reduce(top[:, :], values, AX.X, ALU.add))

            ranked = lg
            if top_of_probs:
                share(pr[:, :, :])
                chain.link(dve.reciprocal(top[:, :], top[:, :]))
                chain.link(dve.tensor_tensor(pr[:, :, :], pr[:, :, :], top[:, :].unsqueeze(2).broadcast_to([P, NT, E]),
                                             ALU.mult))
                ranked = pr
            me = ranked[:, :, :].unsqueeze(3).broadcast_to([P, NT, E, E])
            others = ranked[:, :, :].unsqueeze(2).broadcast_to([P, NT, E, E])
            chain.link(dve.tensor_tensor(beat[:, :, :, :], others, me, ALU.is_gt))
            chain.link(dve.tensor_tensor(tie[:, :, :, :], others, me, ALU.is_equal))
            flat = lambda t: t[:, :, :, :].rearrange("p t e f -> p t (e f)")
            chain.link(dve.tensor_tensor(flat(tie), flat(tie),
                                         earlier[:, :, :].rearrange("p e f -> p (e f)").unsqueeze(1)
                                         .broadcast_to([P, NT, E * E]), ALU.mult))
            chain.link(dve.tensor_tensor(flat(beat), flat(beat), flat(tie), ALU.add))
            chain.link(dve.tensor_reduce(rank[:, :, :], beat[:, :, :, :], AX.X, ALU.add))
            flat2 = lambda t: t[:, :, :].rearrange("p t e -> p (t e)")
            chain.link(dve.scalar_tensor_tensor(out=flat2(pr), in0=flat2(rank), scalar=2.0, in1=flat2(pr),
                                                op0=ALU.is_lt, op1=ALU.mult))
            share(pr[:, :, :])
            if top_of_probs:
                chain.link(dve.tensor_scalar(top[:, :], top[:, :], 1e-8, None, ALU.add))
            chain.link(dve.reciprocal(top[:, :], top[:, :]))
            chain.link(dve.tensor_scalar(scale[:, :], S.gates[:, gate:gate + 1], factor, None, ALU.mult))
            chain.link(dve.tensor_scalar(top[:, :], top[:, :], scale[:, :], None, ALU.mult))
            dve.tensor_tensor(S.cw[:, :, :], pr[:, :, :], top[:, :].unsqueeze(2).broadcast_to([P, NT, E]),
                              ALU.mult).then_inc(s_cw, 1)
            dve.wait_ge(s_cwT, 1)
            dve.tensor_copy(cwT[:, :], ps[:, 6, 0:P]).then_inc(s_cwTs, 1)
            for u in range(NT // 2):
                x = S.x[:, 2 * u:2 * u + 2, :].rearrange("p t d -> p (t d)")
                dve.wait_ge(s_bias, u + 1)
                dve.tensor_tensor(x, ps[:, u % BANKS, :], x, ALU.add).then_inc(s_res, 1)


class Ring:

    def __init__(self, nc, scope, mats):
        self.mats = mats
        self.n = len(mats)
        self.raw, self.split = [], []
        for i, m in enumerate(mats):
            rows, cols = m.shape[1], m.shape[2]
            self.raw.append(scope.sb(f"raw{i}", [P, rows // P, cols]))
            self.split.append([scope.sb(f"w{i}_{j}", [P, 2, rows // P, cols], BF16) for j in range(2)])
        self.s_turn = scope.sem("wturn")
        self.s_raw, self.s_split, self.s_free = scope.sem("wraw"), scope.sem("wsplit"), scope.sem("wfree")

    def load(self, sp, e, wait=True):
        if wait:
            sp.wait_ge(self.s_split, 2 * self.n * e)
        for raw, m in zip(self.raw, self.mats):
            src = m[e] if isinstance(e, int) else m[ts(e, 1)].squeeze(0)
            sp.dma_start(raw[:, :, :], src.rearrange("(k p) h -> p k h", p=P)).then_inc(self.s_raw, 16)

    def halves(self, pool, e, j, wait=True):
        pool.wait_ge(self.s_raw, 16 * self.n * (e + 1))
        if wait:
            pool.wait_ge(self.s_free, e - 1)
            pool.sem_inc(self.s_turn)
        for i in range(self.n):
            hi, lo = self.split[i][j][:, 0, :, :], self.split[i][j][:, 1, :, :]
            pool.tensor_copy(hi, self.raw[i][:, :, :]).then_inc(self.s_split, 1)
            pool.wait_ge(self.s_split, 2 * self.n * e + 2 * i + 1)
            pool.tensor_tensor(lo, self.raw[i][:, :, :], hi, ALU.subtract).then_inc(self.s_split, 1)

    def load_first(self, sp):
        self.load(sp, 0, wait=False)

    def split_first(self, pool):
        self.halves(pool, 0, 0, wait=False)


def expert_stage(nc, S, stage, ring, up_bias, gate_bias, hid):
    M = hid // P
    NB, BT = 4, 4
    W = BT * P
    LAG = 2
    HB = 4
    gated = up_bias is not None
    with Scope(nc, stage) as c:
        nb = 2 if gated else 1
        brow = c.sb("brow", [E * M, nb, P])
        bcol = c.sb("bcol", [P, nb, E * M])
        prime = c.sb("prime", [P, 2, 2])
        acted = c.sb("acted", [P, 2, W])
        prod = c.sb("prod", [P, 2, W]) if gated else acted
        hg = c.sb("hg", [P, HB, 2, W], BF16)
        s_b, s_bT, s_bcol, s_turn = c.sem("b"), c.sem("bT"), c.sem("bcol"), c.sem("turn")
        s_gate, s_up, s_act, s_prod, s_hi, s_lo, s_down, s_y = (
            c.sem(n) for n in ("gate", "up", "act", "prod", "hi", "lo", "down", "y"))
        ps = S.ps
        GB, UB, YB = (0, 1), (2, 3), (4, 5)
        PRIMED = 2
        LOWS = AHEAD if gated else PRIMED
        block = c.block()
        w_gate, w_up, w_down = 0, 1, ring.n - 1

        def over_blocks(eng, body, tail):
            with eng.Fori(0, E // 2) as pair:
                for j in range(2):
                    e = 2 * pair + j
                    body(e, j, 0, first=True)
                    with eng.Fori(1, NB) as tb:
                        body(e, j, tb, first=False)
                    tail(e, j)

        @block.sync
        def _(sp):
            start_ahead(sp, s_y)
            if gated:
                start_ahead(sp, s_lo)
            sp.dma_start(brow[:, 0, :], gate_bias.rearrange("e (m p) -> (e m) p", p=P)).then_inc(s_b, 16)
            if gated:
                sp.dma_start(brow[:, 1, :], up_bias.rearrange("e (m p) -> (e m) p", p=P)).then_inc(s_b, 16)
            with sp.Fori(1, E) as e:
                ring.load(sp, e)

        @block.gpsimd
        def _(pool):
            ring.halves(pool, 1, 1, wait=False)
            with pool.Fori(1, E // 2) as pair:
                for j in range(2):
                    ring.halves(pool, 2 * pair + j, j)

        @block.scalar
        def _(act):
            act.wait_ge(s_bT, 1)
            act.activation(bcol[:, :, :], ps[:, 7, 0:nb * E * M].rearrange("p (b m) -> p b m", b=nb), ACT.Copy).then_inc(s_bcol, 1)
            act.wait_ge(s_bcol, 1)
            for j in range(PRIMED):
                act.activation(prime[:, 0, j:j + 1], bcol[:, 0, 0:1], ACT.Copy).then_inc(s_act, 1)

            def body(e, j, tb, first):
                for m in range(M):
                    s = (e * NB + tb) * M + m
                    act.wait_ge(s_gate, s + 1)
                    act.sem_inc(s_turn)
                    act.activation(acted[:, m % 2, :], ps[:, GB[m % 2], :], ACT.Silu if gated else ACT.Gelu,
                                   bias=bcol[:, 0, ts(e * M + m, 1)]).then_inc(s_act, 1)

            over_blocks(act, body, lambda e, j: None)

        @block.tensor
        def _(pe):
            pe.wait_ge(s_b, 16 * nb)
            for i in range(nb):
                mm = pe.transpose(ps[:, 7, i * E * M:(i + 1) * E * M], brow[:, i, :], S.ident[0:E * M, 0:E * M])
            mm.then_inc(s_bT, 1)

            def up(e, j, tb, m):
                s = (e * NB + tb) * M + m
                if gated:
                    pe.wait_ge(s_prod, s - 1 + PRIMED)
                else:
                    pe.wait_ge(s_act, s - 1 + PRIMED)
                    pe.wait_ge(s_lo, s - 1 + PRIMED)
                for which, bank, ready in ((w_gate, GB[m % 2], s_gate), (w_up, UB[m % 2], s_up))[:nb]:
                    n = 0
                    for wp, ap in PASSES:
                        for k in range(KD):
                            mm = pe.matmul(ps[:, bank, :], ring.split[which][j][:, wp, k, m * P:m * P + P],
                                           S.zt[:, ap, k, ts(tb * W, W)], start=(n == 0), stop=(n == 3 * KD - 1))
                            n += 1
                    mm.then_inc(ready, 1)

            def down(e, j, tb, m):
                s = (e * NB + tb) * M + m
                pe.wait_ge(s_lo, s + 1 + LOWS)
                if m == 0:
                    pe.wait_ge(s_y, e * NB + tb + AHEAD)
                for t in range(BT):
                    n = 0
                    for wp, ap in PASSES:
                        mm = pe.matmul(ps[:, YB[t // 2], (t % 2) * D:(t % 2) * D + D],
                                       hg[:, m % HB, ap, t * P:t * P + P], ring.split[w_down][j][:, wp, m, :],
                                       start=(m == 0 and n == 0 and t % 2 == 0), stop=(m == M - 1 and n == 2),
                                       skip_group_check=True)
                        n += 1
                mm.then_inc(s_down, 1)
                return mm

            def body(e, j, tb, first):
                if first:
                    pe.wait_ge(ring.s_split, 2 * ring.n * (e + 1))
                for m in range(M):
                    up(e, j, tb, m)
                    if m >= LAG:
                        down(e, j, tb, m - LAG)
                    elif not first:
                        down(e, j, tb - 1, M - LAG + m)

            def tail(e, j):
                for m in range(M - LAG, M):
                    mm = down(e, j, NB - 1, m)
                pe.matmul(ps[:, 7, 0:8], hg[:, 0, 0, 0:P], ring.split[w_down][j][:, 0, 0, 0:8], start=True, stop=True
                          ).then_inc(ring.s_free, 1)

            over_blocks(pe, body, tail)

        @block.vector
        def _(dve):
            dve.wait_ge(s_bcol, 1)
            for j in range(PRIMED):
                dve.tensor_copy(prime[:, 1, j:j + 1], bcol[:, 0, 0:1]).then_inc(s_prod if gated else s_lo, 1)

            def hidden(e, tb, m):
                s = (e * NB + tb) * M + m
                if gated:
                    dve.wait_ge(s_lo, s + LOWS)
                    dve.wait_ge(s_up, s + 1)
                    dve.wait_ge(s_act, s + 1 + PRIMED)
                    dve.scalar_tensor_tensor(out=prod[:, m % 2, :], in0=ps[:, UB[m % 2], :],
                                             scalar=bcol[:, 1, ts(e * M + m, 1)], in1=acted[:, m % 2, :],
                                             op0=ALU.add, op1=ALU.mult).then_inc(s_prod, 1)
                    dve.wait_ge(s_prod, s + 1 + PRIMED)
                else:
                    dve.wait_ge(s_act, s + 1 + PRIMED)
                dve.tensor_copy(hg[:, m % HB, 0, :], prod[:, m % 2, :]).then_inc(s_hi, 1)
                dve.wait_ge(s_hi, s + 1)
                dve.tensor_tensor(hg[:, m % HB, 1, :], prod[:, m % 2, :], hg[:, m % HB, 0, :],
                                  ALU.subtract).then_inc(s_lo, 1)

            def collect(e, tb):
                dve.wait_ge(s_down, (e * NB + tb + 1) * M)
                for t in range(BT):
                    b = tb * BT + t
                    x = S.x[:, ts(b, 1), :].squeeze(1)
                    add = dve.scalar_tensor_tensor(out=x, in0=ps[:, YB[t // 2], (t % 2) * D:(t % 2) * D + D],
                                                   scalar=S.cw[:, ts(b, 1), ts(e, 1)].squeeze(1), in1=x,
                                                   op0=ALU.mult, op1=ALU.add)
                add.then_inc(s_y, 1)

            def body(e, j, tb, first):
                for m in range(M):
                    hidden(e, tb, m)
                    if m == LAG - 1 and not first:
                        collect(e, tb - 1)

            over_blocks(dve, body, lambda e, j: collect(e, NB - 1))


class CrossWeights:

    CHUNK = 2048
    SLOTS = 2

    def __init__(self, nc, scope, wq, wkv, wout):
        inner = wq.shape[1]
        self.q = scope.sb("wq", [P, 2, KD, inner], BF16)
        self.kv = scope.sb("wkv", [P, 2, KC, 2 * inner], BF16)
        self.out = scope.sb("wout", [P, 2, inner // P, D], BF16)
        self.raw = scope.sb("xraw", [P, self.SLOTS, self.CHUNK])
        self.s_raw = [scope.sem(f"xraw{i}") for i in range(self.SLOTS)]
        self.s_split = scope.sem("xsplit")
        self.parts = [(wq.rearrange("(k p) h -> p k h", p=P), lambda a: self.q[:, a, :, :])]
        self.parts += [(wkv[k * P:(k + 1) * P, :].unsqueeze(1), lambda a, k=k: self.kv[:, a, k:k + 1, :]) for k in range(KC)]
        self.parts += [(wout.rearrange("(m p) d -> p m d", p=P), lambda a: self.out[:, a, :, :])]
        self.n = 2 * len(self.parts)

    def slot(self, i, like):
        return self.raw[:, i % self.SLOTS, :].rearrange("p (k h) -> p k h", k=like.shape[1])

    def load_first(self, sp):
        for i, (src, _) in enumerate(self.parts):
            if i >= self.SLOTS:
                sp.wait_ge(self.s_split, 2 * (i - self.SLOTS + 1))
            sp.dma_start(self.slot(i, src), src).then_inc(self.s_raw[i % self.SLOTS], 16)

    def split_first(self, pool):
        for i, (src, dst) in enumerate(self.parts):
            pool.wait_ge(self.s_raw[i % self.SLOTS], 16 * (i // self.SLOTS + 1))
            pool.tensor_copy(dst(0), self.slot(i, src)).then_inc(self.s_split, 1)
            pool.wait_ge(self.s_split, 2 * i + 1)
            pool.tensor_tensor(dst(1), self.slot(i, src), dst(0), ALU.subtract).then_inc(self.s_split, 1)


def cross_stage(nc, S, A, cross):
    GB = 4
    NG = NT // GB
    W = GB * P
    INNER = XHEADS * XDH
    MI = INNER // P
    UNITS = XHEADS // 4
    SCALE = XDH ** -0.5
    with Scope(nc, "xa") as c:
        cin = c.sb("cin", [P, GB, CTX])
        ctxT = c.sb("ctxT", [P, 2, KC, W], BF16)
        kt = c.sb("kt", [P, 2, MI, GB, XW], BF16)
        v = c.sb("v", [P, 2, GB, INNER], BF16)
        qt = c.sb("qt", [P, 2, MI, W], BF16)
        nk = c.sb("nk", [P, 3])
        nkh = c.sb("nkh", [P, 2], BF16)
        nv = c.sb("nv", [P, XDH])
        lns = c.sb("lns", [P, D])
        lnb = c.sb("lnb", [P, D])
        mx = c.sb("mx", [P, 2, XHEADS])
        nmx = c.sb("nmx", [P, 2, XHEADS])
        sums = c.sb("sums", [P, 2, XHEADS])
        rsum = c.sb("rsum", [P, XHEADS])
        pexp = c.sb("pexp", [P, 2, 4, XW])
        pt = c.sb("pt", [P, 2, 2, 4 * P], BF16)
        pn = c.sb("pn", [P, 2, XHEADS])
        pnv = c.sb("pnv", [P, XHEADS, XDH])
        o = c.sb("o", [P, XHEADS, XDH])
        ot = c.sb("ot", [P, 2, MI, P], BF16)
        o2 = c.sb("o2", [P, NT, D])
        raw = c.sb("raw", [P, NT, 6])
        tmp = c.sb("tmp", [P, NT])
        t1 = c.sb("t1", [P, 2, D])
        (s_rows, s_cin, s_null, s_xb, s_pj, s_pjh, s_pjl, s_sc, s_max, s_mx, s_ex, s_t, s_th, s_tl, s_pv, s_pn,
         s_pnv, s_osum, s_o, s_rs, s_dve, s_stats, s_var, s_root, s_t1, s_lns, s_turn, s_res) = (
            c.sem(n) for n in ("rows", "cin", "null", "xb", "pj", "pjh", "pjl", "sc", "max", "mx", "ex", "t", "th",
                               "tl", "pv", "pn", "pnv", "osum", "o", "rs", "dve", "stats", "var", "root", "t1",
                               "lns", "turn", "res"))
        ps = S.ps
        block = c.block()

        PJ = ([("ctx", i) for i in range(GB)] + [("k", i) for i in range(MI)]
              + [("v", i) for i in range(2 * GB)] + [("q", i) for i in range(MI)])
        NPJ = len(PJ)
        PBANKS = 4

        def destination(kind, i, part):
            if kind == "ctx":
                return ctxT[:, part, :, i * P:(i + 1) * P], "p (k s) -> p k s", KC
            if kind == "k":
                return kt[:, part, i, :, 0:P], "p (k s) -> p k s", GB
            if kind == "v":
                return v[:, part, i // 2, (i % 2) * 512:(i % 2) * 512 + 512].unsqueeze(1), "p (k s) -> p k s", 1
            return qt[:, part, i, :].unsqueeze(1), "p (k s) -> p k s", 1

        def bank(u, split, k):
            return ps[:, u % PBANKS, :].rearrange(split, k=k)

        HG = GB * UNITS

        def extra(n):
            bb = n // UNITS
            return {2: [("ot", bb - 1, 0)] if bb >= 1 else [], 3: [("ot", bb - 1, 1)] if bb >= 1 else [],
                    0: [("out", bb - 2, 0)] if bb >= 2 else []}.get(n % UNITS, [])

        LAST = GB - 1
        TRAIL = extra(HG) + [("ot", LAST, 0), ("ot", LAST, 1), ("out", LAST, 0)]
        BETWEEN = ([TRAIL[0]] + [("pj", u) for u in range(GB)] + [TRAIL[1], ("pj", GB), TRAIL[2], ("pj", GB + 1), TRAIL[3]]
                   + [("pj", u) for u in range(GB + 2, NPJ)])
        TU = [u for n in range(HG) for u in [("tr", n // UNITS, n % UNITS)] + extra(n)] + TRAIL
        NTU = len(TU)
        LOWS = [u for u in TU if u[0] != "out"]
        NLOW = len(LOWS)

        def heads(u, p):
            return [4 * u + 2 * mm + p for mm in range(2)]

        def over_groups(eng, project, attention, turned):
            for u in range(NPJ):
                project(0, u)
            with eng.Fori(0, NG - 1) as g:
                attention(g)
                for unit in BETWEEN:
                    if unit[0] == "pj":
                        project(g + 1, unit[1])
                    else:
                        turned(g, unit)
            attention(NG - 1)
            for unit in TRAIL:
                turned(NG - 1, unit)

        @block.sync
        def _(sp):
            start_ahead(sp, s_pjl, s_pn, s_osum, s_ex, s_tl, s_th, s_res)
            null = A["L1_xattn_null_kv"]
            for h in range(2):
                sp.dma_start(nk[h * XDH:(h + 1) * XDH, 0:1], null[0].rearrange("(p a) -> p a", a=1)).then_inc(s_rows, 16)
            sp.dma_start(nv[:, :], null[1].partition_broadcast(P)).then_inc(s_rows, 16)
            sp.dma_start(lns[:, :], A["L1_xattn_ln_scale"].partition_broadcast(P)).then_inc(s_rows, 16)
            sp.dma_start(lnb[:, :], A["L1_xattn_ln_bias"].partition_broadcast(P)).then_inc(s_rows, 16)
            sp.dma_start(cin[:, :, :], A["ctx_2048"][0:GB].rearrange("b p d -> p b d")).then_inc(s_cin, 16)
            with sp.Fori(1, NG) as g:
                sp.wait_ge(s_pjl, (g - 1) * NPJ + GB + AHEAD)
                sp.dma_start(cin[:, :, :], A["ctx_2048"][ts(g * GB, GB)].rearrange("b p d -> p b d")).then_inc(s_cin, 16)

        @block.gpsimd
        def _(pool):
            pool.wait_ge(s_lns, 2)
            pool.tensor_tensor(S.x[:, :, :], S.x[:, :, :], lnb[:, :].unsqueeze(1).broadcast_to([P, NT, D]),
                               ALU.add).then_inc(s_xb, 1)
            with pool.Fori(0, NG) as g:
                for bb in range(GB):
                    for u in range(UNITS):
                        n = bb * UNITS + u
                        pool.wait_ge(s_ex, g * GB * UNITS + n + 1 + AHEAD)
                        for p in range(2):
                            hs = heads(u, p)
                            cp = pool.tensor_tensor(pn[:, bb % 2, hs[0]:hs[1] + 1:2], pexp[:, n % 2, 2 * p:2 * p + 2, P],
                                                    nk[:, 2:3].broadcast_to([P, 2]), ALU.mult)
                        cp.then_inc(s_pn, 1)
                    pool.wait_ge(s_pn, g * GB * UNITS + (bb + 1) * UNITS + AHEAD)
                    pool.wait_ge(s_osum, g * GB + bb + AHEAD)
                    pool.tensor_tensor(pnv[:, :, :], pn[:, bb % 2, :].unsqueeze(2).broadcast_to([P, XHEADS, XDH]),
                                       nv[:, :].unsqueeze(1).broadcast_to([P, XHEADS, XDH]), ALU.mult).then_inc(s_pnv, 1)

        @block.scalar
        def _(act):
            def high(g, u):
                kind, i = PJ[u]
                dst, split, k = destination(kind, i, 0)
                act.wait_ge(s_pj, g * NPJ + u + 1)
                act.activation(dst, bank(u, split, k), ACT.Copy).then_inc(s_pjh, 1)

            def exps(g, bb, u):
                n = bb * UNITS + u
                act.wait_ge(s_mx, g * GB * UNITS + n + 1)
                act.wait_ge(s_pn, g * GB * UNITS + max(n - 1, 0) + AHEAD)
                if n >= 2:
                    act.wait_ge(s_t, g * NTU + TU.index(("tr", (n - 2) // UNITS, (n - 2) % UNITS)) + 1)
                for p in range(2):
                    for mm in range(2):
                        h = heads(u, p)[mm]
                        ex = act.activation(pexp[:, n % 2, 2 * p + mm, :], ps[:, 2 * (n % 2) + p, mm * XW:(mm + 1) * XW],
                                            ACT.Exp, bias=nmx[:, bb % 2, h:h + 1], scale=SCALE,
                                            accum_out=sums[:, bb % 2, h:h + 1])
                ex.then_inc(s_ex, 1)

            def turned(g, unit):
                t = TU.index(unit)
                act.wait_ge(s_t, g * NTU + t + 1)
                kind, bb, u = unit
                if kind == "out":
                    act.activation(o2[:, ts(g * GB + bb, 1), :].squeeze(1), ps[:, 4 + t % 2, 0:D], ACT.Copy).then_inc(s_th, 1)
                elif kind == "tr":
                    act.activation(pt[:, u % 2, 0, :], ps[:, 4 + t % 2, :], ACT.Copy).then_inc(s_th, 1)
                else:
                    act.activation(ot[:, 0, 4 * u:4 * u + 4, :], ps[:, 4 + t % 2, :].rearrange("p (k s) -> p k s", k=4),
                                   ACT.Copy).then_inc(s_th, 1)

            def attention(g):
                exps(g, 0, 0)
                for n in range(HG):
                    if n + 1 < HG:
                        exps(g, (n + 1) // UNITS, (n + 1) % UNITS)
                    for unit in [("tr", n // UNITS, n % UNITS)] + extra(n):
                        turned(g, unit)

            over_groups(act, high, attention, turned)
            act.wait_ge(s_var, 1)
            act.activation(S.rstd[:, :], S.rstd[:, :], ACT.Sqrt).then_inc(s_root, 1)

        @block.tensor
        def _(pe):
            def project(g, u):
                kind, i = PJ[u]
                if u >= PBANKS:
                    pe.wait_ge(s_pjl, g * NPJ + u - PBANKS + 1 + AHEAD)
                else:
                    pe.wait_ge(s_ex, g * GB * UNITS + AHEAD)
                out = ps[:, u % PBANKS, :]
                if kind == "ctx":
                    if i == 0:
                        pe.wait_ge(s_cin, 16 * (g + 1))
                    for k in range(KC):
                        mm = pe.transpose(out[:, k * P:k * P + P], cin[:, i, k * P:k * P + P], S.ident[:, :])
                else:
                    if u == GB:
                        pe.wait_ge(s_pjl, g * NPJ + GB + AHEAD)
                        pe.wait_ge(cross.s_split, cross.n)
                    n, ks = 0, KD if kind == "q" else KC
                    for wp, ap in PASSES:
                        for k in range(ks):
                            if kind == "k":
                                lhs, rhs = cross.kv[:, wp, k, i * P:i * P + P], ctxT[:, ap, k, :]
                            elif kind == "v":
                                half = INNER + (i % 2) * 512
                                lhs, rhs = ctxT[:, ap, k, (i // 2) * P:(i // 2) * P + P], cross.kv[:, wp, k, half:half + 512]
                            else:
                                lhs, rhs = cross.q[:, wp, k, i * P:i * P + P], S.zt[:, ap, k, ts(g * W, W)]
                            mm = pe.matmul(out, lhs, rhs, start=(n == 0), stop=(n == 3 * ks - 1))
                            n += 1
                mm.then_inc(s_pj, 1)

            def scores(g, bb, u):
                n = bb * UNITS + u
                if n == 0:
                    pe.wait_ge(s_pjl, (g + 1) * NPJ + AHEAD)
                elif n >= 2:
                    pe.wait_ge(s_ex, g * GB * UNITS + n - 1 + AHEAD)
                for mm in range(2):
                    m = 2 * u + mm
                    for i, (wp, ap) in enumerate(PASSES):
                        for p in range(2):
                            half = slice(p * XDH, (p + 1) * XDH)
                            q = pe.matmul(ps[:, 2 * (n % 2) + p, mm * XW:(mm + 1) * XW],
                                          qt[half, ap, m, bb * P:(bb + 1) * P], kt[half, wp, m, bb, :],
                                          start=(i == 0), stop=(i == 2))
                q.then_inc(s_sc, 1)

            def bank_free(g, t):
                if t < 2:
                    pe.wait_ge(s_tl, g * NLOW + AHEAD)
                    pe.wait_ge(s_th, g * NTU + AHEAD)
                elif TU[t - 2][0] == "out":
                    pe.wait_ge(s_th, g * NTU + t - 1 + AHEAD)
                else:
                    pe.wait_ge(s_tl, g * NLOW + LOWS.index(TU[t - 2]) + 1 + AHEAD)

            def turn(g, unit):
                kind, bb, u = unit
                t = TU.index(unit)
                bank_free(g, t)
                out = ps[:, 4 + t % 2, :]
                if kind == "tr":
                    n = bb * UNITS + u
                    pe.wait_ge(s_ex, g * GB * UNITS + n + 1 + AHEAD)
                    for i in range(4):
                        mm = pe.transpose(out[:, i * P:i * P + P], pexp[:, n % 2, i, 0:P], S.ident[:, :])
                elif kind == "ot":
                    pe.wait_ge(s_o, g * GB + bb + 1)
                    flat = o[:, :, :].rearrange("p h d -> p (h d)")
                    for i in range(4):
                        k = 4 * u + i
                        mm = pe.transpose(out[:, i * P:i * P + P], flat[:, k * P:k * P + P], S.ident[:, :])
                else:
                    pe.wait_ge(s_tl, g * NLOW + LOWS.index(("ot", bb, 1)) + 1 + AHEAD)
                    n = 0
                    for m in range(MI):
                        for wp, ap in PASSES:
                            mm = pe.matmul(out[:, 0:D], ot[:, ap, m, :], cross.out[:, wp, m, :],
                                           start=(n == 0), stop=(n == 3 * MI - 1))
                            n += 1
                mm.then_inc(s_t, 1)

            def values(g, bb, u):
                pe.wait_ge(s_tl, g * NLOW + LOWS.index(("tr", bb, u)) + 1 + AHEAD)
                if u == 0:
                    pe.wait_ge(s_osum, g * GB + bb + AHEAD)
                for p in range(2):
                    for mm in range(2):
                        h = heads(u, p)[mm]
                        at = (h % 8) * XDH
                        for i, (wp, ap) in enumerate(PASSES):
                            q = pe.matmul(ps[:, 6 + h // 8, at:at + XDH],
                                          pt[:, u % 2, ap, (2 * p + mm) * P:(2 * p + mm + 1) * P],
                                          v[:, wp, bb, h * XDH:(h + 1) * XDH], start=(i == 0), stop=(i == 2))
                q.then_inc(s_pv, 1)

            def attention(g):
                scores(g, 0, 0)
                scores(g, 0, 1)
                for n in range(HG):
                    turn(g, ("tr", n // UNITS, n % UNITS))
                    if n + 2 < HG:
                        scores(g, (n + 2) // UNITS, (n + 2) % UNITS)
                    if n >= 1:
                        values(g, (n - 1) // UNITS, (n - 1) % UNITS)
                    for unit in extra(n):
                        turn(g, unit)
                values(g, LAST, UNITS - 1)

            over_groups(pe, project, attention, turn)

        @block.vector
        def _(dve):
            chain = Chain(dve, s_dve)
            dve.wait_ge(s_rows, 80)
            chain.link(dve.tensor_copy(nkh[:, 0:1], nk[:, 0:1]))
            chain.link(dve.tensor_tensor(nkh[:, 1:2], nk[:, 0:1], nkh[:, 0:1], ALU.subtract))
            chain.link(dve.memset(nk[:, 2:3], 1.0))
            for part in range(2):
                chain.link(dve.tensor_copy(kt[:, part, :, :, P], nkh[:, part:part + 1].unsqueeze(2)
                                           .broadcast_to([P, MI, GB])))
            dve.tensor_scalar(lns[:, :], lns[:, :], S.gates[:, 1:2], None, ALU.mult).then_inc(s_lns, 1)
            dve.tensor_scalar(lnb[:, :], lnb[:, :], S.gates[:, 1:2], None, ALU.mult).then_inc(s_lns, 1)

            def low(g, u):
                kind, i = PJ[u]
                dst, split, k = destination(kind, i, 1)
                dve.wait_ge(s_pjh, g * NPJ + u + 1)
                dve.tensor_tensor(dst, bank(u, split, k), destination(kind, i, 0)[0], ALU.subtract).then_inc(s_pjl, 1)

            def maxima(g, bb, u):
                n = bb * UNITS + u
                dve.wait_ge(s_sc, g * GB * UNITS + n + 1)
                for p in range(2):
                    hs = heads(u, p)
                    dve.tensor_reduce(mx[:, bb % 2, hs[0]:hs[1] + 1:2],
                                      ps[:, 2 * (n % 2) + p, 0:2 * XW].rearrange("p (h k) -> p h k", h=2),
                                      AX.X, ALU.max).then_inc(s_max, 1)
                dve.wait_ge(s_max, 2 * (g * GB * UNITS + n + 1))
                dve.tensor_scalar(nmx[:, bb % 2, 4 * u:4 * u + 4], mx[:, bb % 2, 4 * u:4 * u + 4], -SCALE, None,
                                  ALU.mult).then_inc(s_mx, 1)

            def turned(g, unit):
                t = TU.index(unit)
                kind, bb, u = unit
                if kind == "out":
                    return
                dve.wait_ge(s_th, g * NTU + t + 1 + AHEAD)
                if kind == "tr":
                    dve.tensor_tensor(pt[:, u % 2, 1, :], ps[:, 4 + t % 2, :], pt[:, u % 2, 0, :],
                                      ALU.subtract).then_inc(s_tl, 1)
                else:
                    four = slice(4 * u, 4 * u + 4)
                    dve.tensor_tensor(ot[:, 1, four, :], ps[:, 4 + t % 2, :].rearrange("p (k s) -> p k s", k=4),
                                      ot[:, 0, four, :], ALU.subtract).then_inc(s_tl, 1)

            def normalise(g, bb):
                done = g * GB + bb
                dve.reciprocal(rsum[:, :], sums[:, bb % 2, :]).then_inc(s_rs, 1)
                dve.wait_ge(s_pnv, done + 1)
                dve.wait_ge(s_pv, (done + 1) * UNITS)
                dve.tensor_tensor(o[:, :, :], ps[:, 6:8, :].rearrange("p b (h d) -> p (b h) d", d=XDH), pnv[:, :, :],
                                  ALU.add).then_inc(s_osum, 1)
                dve.wait_ge(s_osum, done + 1 + AHEAD)
                dve.wait_ge(s_rs, done + 1)
                dve.tensor_tensor(o[:, :, :], o[:, :, :], rsum[:, :].unsqueeze(2).broadcast_to([P, XHEADS, XDH]),
                                  ALU.mult).then_inc(s_o, 1)

            def attention(g):
                maxima(g, 0, 0)
                maxima(g, 0, 1)
                for n in range(HG):
                    if n + 2 < HG:
                        maxima(g, (n + 2) // UNITS, (n + 2) % UNITS)
                    for unit in [("tr", n // UNITS, n % UNITS)] + extra(n):
                        turned(g, unit)
                    if n % UNITS == 0 and n > 0:
                        normalise(g, n // UNITS - 1)
                normalise(g, LAST)

            over_groups(dve, low, attention, turned)
            dve.wait_ge(s_th, NG * NTU + AHEAD)
            tile_stats(dve, o2, raw, s_stats)
            dve.wait_ge(s_stats, NT)
            combine_stats(dve, chain, raw, S.mean[:, :], S.rstd[:, :], tmp[:, :], D)
            dve.tensor_scalar(S.rstd[:, :], S.rstd[:, :], 1e-6, None, ALU.add).then_inc(s_var, 1)
            dve.wait_ge(s_root, 1)
            chain.link(dve.reciprocal(S.rstd[:, :], S.rstd[:, :]))
            dve.wait_ge(s_xb, 1)
            with dve.Fori(0, NT // 2) as i:
                for j in range(2):
                    b = 2 * i + j
                    x = S.x[:, ts(b, 1), :].squeeze(1)
                    dve.wait_ge(s_res, b + AHEAD)
                    dve.scalar_tensor_tensor(out=t1[:, j, :], in0=o2[:, ts(b, 1), :].squeeze(1), scalar=S.mean[:, ts(b, 1)],
                                             in1=lns[:, :], op0=ALU.subtract, op1=ALU.mult).then_inc(s_t1, 1)
                    dve.wait_ge(s_t1, b + 1)
                    dve.scalar_tensor_tensor(out=x, in0=t1[:, j, :], scalar=S.rstd[:, ts(b, 1)], in1=x,
                                             op0=ALU.mult, op1=ALU.add).then_inc(s_res, 1)


def latent_stage(nc, S, A):
    U = LHEADS // 4
    LAT = LHEADS * LDH
    SCALE = LDH ** -0.5
    with Scope(nc, "la") as c:
        wraw = c.sb("wraw", [P, KD, D + 2 * LAT])
        w = c.sb("w", [P, 2, KD, 3, LAT], BF16)
        ow = c.sb("ow", [LAT, D])
        brow = c.sb("brow", [4, P])
        bcol = c.sb("bcol", [P, 4])
        vrow = c.sb("vrow", [P, LAT])
        ones = c.sb("ones", [P, LHEADS])
        own = c.sb("own", [P, LHEADS])
        qT = c.sb("qT", [P, 2, P])
        kT = c.sb("kT", [P, 2, P])
        km = c.sb("km", [P, 2, LHEADS, P])
        vf = c.sb("vf", [P, 2, LAT])
        v = c.sb("v", [P, 2, 2, LAT], BF16)
        mx = c.sb("mx", [P, 2, LHEADS])
        nmx = c.sb("nmx", [P, 2, LHEADS])
        sums = c.sb("sums", [P, 2, LHEADS])
        rsum = c.sb("rsum", [P, 2, LHEADS])
        pexp = c.sb("pexp", [P, 2, 4, P])
        pt = c.sb("pt", [P, 2, 2, 4 * P], BF16)
        ao = c.sb("ao", [P, 2, LHEADS, LDH])
        aoT = c.sb("aoT", [P, 2, P])
        (s_w, s_b, s_pool, s_split, s_bT, s_bcol, s_pj, s_k, s_v, s_vp, s_km, s_sc, s_max, s_mx, s_ex, s_t, s_th, s_tl,
         s_pv, s_rs, s_ao, s_aoT, s_aoc, s_mla, s_mh, s_ml) = (
            c.sem(n) for n in ("w", "b", "pool", "split", "bT", "bcol", "pj", "k", "v", "vp", "km", "sc", "max", "mx",
                               "ex", "t", "th", "tl", "pv", "rs", "ao", "aoT", "aoc", "mla", "mh", "ml"))
        ps = S.ps
        SCB, TRB, PJB, PVB, OUTB = (0, 1), (2, 3), 4, (5, 6), 7

        def exists(b, u=0):
            return not isinstance(b, int) or 0 <= b * U + u < NT * U

        def unit(b, j, u):
            return b + u // U, (j + u // U) % 2, u % U

        def over_entries(eng, body):
            body(0, 0)
            body(1, 1)
            with eng.Fori(1, NT // 2 - 1) as i:
                body(2 * i, 0)
                body(2 * i + 1, 1)
            body(NT - 2, 0)
            body(NT - 1, 1)

        block = c.block()

        @block.sync
        def _(sp):
            rows = lambda m: m.rearrange("(k p) c -> p k c", p=P)
            sp.dma_start(wraw[:, :, 0:D], rows(A["L1_ffn_q_w"])).then_inc(s_w, 16)
            sp.dma_start(wraw[:, :, D:D + LAT], rows(A["L1_ffn_k_w"])).then_inc(s_w, 16)
            sp.dma_start(wraw[:, :, D + LAT:], rows(A["L1_ffn_v_w"])).then_inc(s_w, 16)
            sp.dma_start(brow[0:1, :].rearrange("a (h r) -> a h r", r=LDH),
                         A["L1_ffn_q_b"].rearrange("(a h r) -> a h r", a=1, h=LHEADS)[:, :, 0:LDH]).then_inc(s_b, 16)
            sp.dma_start(brow[1:2, :], A["L1_ffn_k_b"].rearrange("(a n) -> a n", a=1)).then_inc(s_b, 16)
            sp.dma_start(brow[2:4, :], A["L1_ffn_o_b"].rearrange("(a n) -> a n", a=2)).then_inc(s_b, 16)
            sp.dma_start(vrow[:, :], A["L1_ffn_v_b"].partition_broadcast(P)).then_inc(s_b, 16)
            sp.dma_start(ow[:, :], A["L1_ffn_o_w"][0:LAT, :]).then_inc(s_b, 16)

        @block.gpsimd
        def _(pool):
            chain = Chain(pool, s_pool)
            chain.link(pool.memset(ones[:, :], 1.0))
            chain.link(pool.affine_select(out=own[:, :], in_=ones[:, :], compare_op=ALU.is_ge, fill=0.0,
                                          base=0, pattern=[[-LDH, LHEADS]], channel_multiplier=1))
            chain.link(pool.affine_select(out=own[:, :], in_=own[:, :], compare_op=ALU.is_ge, fill=0.0,
                                          base=LDH - 1, pattern=[[LDH, LHEADS]], channel_multiplier=-1))
            chain.link(pool.memset(km[:, :, :, :], 0.0))
            with pool.Fori(0, NT // 2) as i:
                for j in range(2):
                    pool.wait_ge(s_k, 2 * i + j + 1)
                    for u in range(U):
                        rows, hs = slice(32 * u, 32 * u + 32), slice(4 * u, 4 * u + 4)
                        pool.tensor_tensor(km[rows, j, hs, :], kT[rows, j, :].unsqueeze(1).broadcast_to([32, 4, P]),
                                           own[rows, hs].unsqueeze(2).broadcast_to([32, 4, P]), ALU.mult).then_inc(s_km, 1)

        @block.scalar
        def _(act):
            def exps(b, j, u):
                n = b * U + u
                act.wait_ge(s_mx, n + 1)
                wait_past_zero(act, s_t, n - 1)
                for i in range(4):
                    h = 4 * u + i
                    ex = act.activation(pexp[:, u % 2, i, :], ps[:, SCB[u % 2], i * P:(i + 1) * P], ACT.Exp,
                                        bias=nmx[:, j, h:h + 1], scale=SCALE, accum_out=sums[:, j, h:h + 1])
                ex.then_inc(s_ex, 1)

            def turned(b, j, u):
                act.wait_ge(s_t, b * U + u + 1)
                act.activation(pt[:, u % 2, 0, :], ps[:, TRB[u % 2], :], ACT.Copy).then_inc(s_th, 1)

            def output(b):
                act.wait_ge(s_mla, b + 1)
                for k in range(KD):
                    cp = act.activation(S.zt[:, 0, k, ts(b * P, P)], ps[:, OUTB, (1 + k) * P:(2 + k) * P], ACT.Identity,
                                        bias=bcol[:, 2 + k:3 + k])
                cp.then_inc(s_mh, 1)

            def body(b, j):
                for u in range(U):
                    if exists(b, u + 1):
                        exps(*unit(b, j, u + 1))
                    if u == 0 and exists(b - 2):
                        output(b - 2)
                    turned(b, j, u)

            act.wait_ge(s_bcol, 1)
            exps(0, 0, 0)
            over_entries(act, body)
            output(NT - 2)
            output(NT - 1)

        @block.tensor
        def _(pe):
            def project(b, j):
                wait_past_zero(pe, s_v, b)
                for which in range(3):
                    n = 0
                    for wp, ap in PASSES:
                        for k in range(KD):
                            wk, zk = w[:, wp, k, which, :], S.zt[:, ap, k, ts(b * P, P)]
                            lhs, rhs = (zk, wk) if which == 2 else (wk, zk)
                            mm = pe.matmul(ps[:, PJB, which * P:which * P + P], lhs, rhs, start=(n == 0), stop=(n == 3 * KD - 1))
                            n += 1
                mm.then_inc(s_pj, 1)

            def scores(b, j, u):
                pe.wait_ge(s_km, b * U + u + 1)
                wait_past_zero(pe, s_ex, b * U + u - 1)
                pe.matmul(ps[:, SCB[u % 2], :], qT[:, j, :], km[:, j, 4 * u:4 * u + 4, :].rearrange("p h k -> p (h k)"),
                          start=True, stop=True).then_inc(s_sc, 1)

            def turn(b, j, u):
                wait_past_zero(pe, s_tl, b * U + u - 1)
                pe.wait_ge(s_ex, b * U + u + 1)
                for i in range(4):
                    mm = pe.transpose(ps[:, TRB[u % 2], i * P:i * P + P], pexp[:, u % 2, i, :], S.ident[:, :])
                mm.then_inc(s_t, 1)

            def values(b, j, u):
                if u == 0:
                    wait_past_zero(pe, s_ao, b - 1)
                    pe.wait_ge(s_v, b + 1)
                pe.wait_ge(s_tl, b * U + u + 1)
                for i in range(4):
                    h = 4 * u + i
                    for p, (wp, ap) in enumerate(PASSES):
                        mm = pe.matmul(ps[:, PVB[j], h * LDH:(h + 1) * LDH], pt[:, u % 2, ap, i * P:i * P + P],
                                       v[:, j, wp, h * LDH:(h + 1) * LDH], start=(p == 0), stop=(p == 2))
                mm.then_inc(s_pv, 1)

            def turn_out(b, j):
                pe.wait_ge(s_ao, b + 1)
                wait_past_zero(pe, s_ml, b)
                pe.transpose(ps[:, OUTB, 0:P], ao[:, j, :, :].rearrange("p h d -> p (h d)"), S.ident[:, :]).then_inc(s_aoT, 1)

            def output(b, j):
                pe.wait_ge(s_aoc, b + 1)
                for k in range(KD):
                    mm = pe.matmul(ps[:, OUTB, (1 + k) * P:(2 + k) * P], ow[:, k * P:k * P + P], aoT[:, j, :],
                                   start=True, stop=True)
                mm.then_inc(s_mla, 1)

            def body(b, j):
                for u in range(U):
                    turn(b, j, u)
                    if exists(b, u + 2):
                        scores(*unit(b, j, u + 2))
                    if u > 0:
                        values(b, j, u - 1)
                    elif exists(b - 1):
                        values(b - 1, 1 - j, U - 1)
                    if u == 0 and exists(b + 1):
                        project(b + 1, 1 - j)
                    if u == 1 and exists(b - 1):
                        turn_out(b - 1, 1 - j)
                    if u == 3 and exists(b - 1):
                        output(b - 1, 1 - j)

            pe.wait_ge(s_b, 80)
            pe.transpose(ps[:, 0, 0:4], brow[:, :], S.ident[0:4, 0:4]).then_inc(s_bT, 1)
            pe.wait_ge(s_split, 6)
            project(0, 0)
            pe.wait_ge(s_bcol, 1)
            scores(0, 0, 0)
            scores(0, 0, 1)
            over_entries(pe, body)
            values(NT - 1, 1, U - 1)
            turn_out(NT - 1, 1)
            output(NT - 1, 1)

        @block.vector
        def _(dve):
            dve.wait_ge(s_w, 48)
            parts = [wraw[:, :, 0:D].rearrange("p k (h r) -> p k h r", r=2 * LDH)[:, :, :, 0:LDH],
                     wraw[:, :, D:D + LAT].rearrange("p k (h r) -> p k h r", r=LDH),
                     wraw[:, :, D + LAT:].rearrange("p k (h r) -> p k h r", r=LDH)]
            for i, part in enumerate(parts):
                for k in range(KD):
                    hi, lo = (w[:, a, k, i, :].rearrange("p (h r) -> p h r", r=LDH) for a in range(2))
                    dve.tensor_copy(hi, part[:, k, :, :]).then_inc(s_vp, 1)
                    dve.wait_ge(s_vp, KD * i + k + 1)
                    dve.tensor_tensor(lo, part[:, k, :, :], hi, ALU.subtract).then_inc(s_split, 1)
            dve.wait_ge(s_bT, 1)
            dve.tensor_copy(bcol[:, :], ps[:, 0, 0:4]).then_inc(s_bcol, 1)
            dve.wait_ge(s_bcol, 1)
            SPLITS = 3 * KD

            def projected_qk(b, j):
                dve.wait_ge(s_pj, b + 1)
                dve.tensor_scalar(kT[:, j, :], ps[:, PJB, P:2 * P], bcol[:, 1:2], None, ALU.add)
                dve.tensor_scalar(qT[:, j, :], ps[:, PJB, 0:P], bcol[:, 0:1], None, ALU.add).then_inc(s_k, 1)

            def projected_v(b, j):
                dve.tensor_tensor(vf[:, j, :], ps[:, PJB, 2 * P:3 * P], vrow[:, :], ALU.add).then_inc(s_vp, 1)
                dve.wait_ge(s_vp, 2 * b + 1 + SPLITS)
                dve.tensor_copy(v[:, j, 0, :], vf[:, j, :]).then_inc(s_vp, 1)
                dve.wait_ge(s_vp, 2 * b + 2 + SPLITS)
                dve.tensor_tensor(v[:, j, 1, :], vf[:, j, :], v[:, j, 0, :], ALU.subtract).then_inc(s_v, 1)

            def maxima(b, j, u):
                hs = slice(4 * u, 4 * u + 4)
                dve.wait_ge(s_sc, b * U + u + 1)
                dve.tensor_reduce(mx[:, j, hs], ps[:, SCB[u % 2], :].rearrange("p (h k) -> p h k", h=4), AX.X,
                                  ALU.max).then_inc(s_max, 1)
                dve.wait_ge(s_max, b * U + u + 1)
                dve.tensor_scalar(nmx[:, j, hs], mx[:, j, hs], -SCALE, None, ALU.mult).then_inc(s_mx, 1)

            def turned(b, j, u):
                dve.wait_ge(s_th, b * U + u + 1)
                dve.tensor_tensor(pt[:, u % 2, 1, :], ps[:, TRB[u % 2], :], pt[:, u % 2, 0, :], ALU.subtract).then_inc(s_tl, 1)

            def normalise(b, j):
                dve.reciprocal(rsum[:, j, :], sums[:, j, :]).then_inc(s_rs, 1)
                dve.wait_ge(s_rs, b + 1)
                dve.wait_ge(s_pv, b * U + U)
                dve.tensor_tensor(ao[:, j, :, :], ps[:, PVB[j], 0:LAT].rearrange("p (h d) -> p h d", d=LDH),
                                  rsum[:, j, :].unsqueeze(2).broadcast_to([P, LHEADS, LDH]), ALU.mult).then_inc(s_ao, 1)

            def copy_out(b, j):
                dve.wait_ge(s_aoT, b + 1)
                dve.tensor_copy(aoT[:, j, :], ps[:, OUTB, 0:P]).then_inc(s_aoc, 1)

            def output(b):
                dve.wait_ge(s_mh, b + 1)
                for k in range(KD):
                    q = dve.scalar_tensor_tensor(out=S.zt[:, 1, k, ts(b * P, P)], in0=ps[:, OUTB, (1 + k) * P:(2 + k) * P],
                                                 scalar=bcol[:, 2 + k:3 + k], in1=S.zt[:, 0, k, ts(b * P, P)],
                                                 op0=ALU.add, op1=ALU.subtract)
                q.then_inc(s_ml, 1)

            def body(b, j):
                for u in range(U):
                    if exists(b, u + 2):
                        maxima(*unit(b, j, u + 2))
                    if u == 2 and exists(b - 1):
                        copy_out(b - 1, 1 - j)
                    if u == 0 and exists(b - 2):
                        output(b - 2)
                    turned(b, j, u)
                    if u == 0 and exists(b - 1):
                        normalise(b - 1, 1 - j)
                    if u == 0 and exists(b + 1):
                        projected_qk(b + 1, 1 - j)
                    if u == 1 and exists(b + 1):
                        projected_v(b + 1, 1 - j)

            projected_qk(0, 0)
            projected_v(0, 0)
            maxima(0, 0, 0)
            maxima(0, 0, 1)
            over_entries(dve, body)
            normalise(NT - 1, 1)
            output(NT - 2)
            copy_out(NT - 1, 1)
            output(NT - 1)


def store_stage(nc, S, A, out):
    with Scope(nc, "st") as c:
        s_out = c.sem("out")
        block = c.block()

        @block.sync
        def _(sp):
            for q in range(4):
                sp.dma_start(out[4 * q:4 * q + 4].rearrange("b p d -> p b d"), S.x[:, 4 * q:4 * q + 4, :]).then_inc(s_out, 16)
            sp.wait_ge(s_out, 64)


def build(nc, A, out, upto=99, skip=0):
    with Scope(nc, "g") as g:
        S = Shared(nc, g)
        depool_stage(nc, S, A)
        if skip <= 1 and upto >= 2:
            with Scope(nc, "r0") as r:
                ring = Ring(nc, r, [A["L0_ffn_W1"], A["L0_ffn_W0"], A["L0_ffn_W2"]])
                norm_stage(nc, S, "n0", prefetch=ring)
                gate_stage(nc, S, "g0", A, A["L0_ffn_Wg"], A["L0_ffn_bg"], A["L0_ffn_b2"], 2, False)
                expert_stage(nc, S, "e0", ring, A["L0_ffn_b0"], A["L0_ffn_b1"], 1024)
        if skip <= 2 and upto >= 3:
            with Scope(nc, "r1") as r:
                cross = CrossWeights(nc, r, A["L1_xattn_Wq"], A["L1_xattn_Wkv"], A["L1_xattn_Wout"])
                norm_stage(nc, S, "n1", prefetch=cross)
                cross_stage(nc, S, A, cross)
        if upto >= 4:
            with Scope(nc, "r2") as r:
                ring = Ring(nc, r, [A["L1_ffn_w1"], A["L1_ffn_w2"]])
                norm_stage(nc, S, "n2", prefetch=ring, residual=3)
                latent_stage(nc, S, A)
                gate_stage(nc, S, "g1", A, A["L1_ffn_router_w"], A["L1_ffn_router_b"], A["L1_ffn_b2"], 3, True, 0.3)
                expert_stage(nc, S, "e1", ring, None, A["L1_ffn_b1"], 512)
        store_stage(nc, S, A, out)


_INS = ["x", "ctx_2048", "mask_BxS2_if0", "g_xattn", "g_ffn", "L0_xattn_W_in", "L0_xattn_b_in", "L0_xattn_g_res",
        "L0_xattn_g_init", "L0_ffn_Wg", "L0_ffn_bg", "L0_ffn_W0", "L0_ffn_b0", "L0_ffn_W1", "L0_ffn_b1", "L0_ffn_W2",
        "L0_ffn_b2", "L1_xattn_Wq", "L1_xattn_Wkv", "L1_xattn_null_kv", "L1_xattn_Wout", "L1_xattn_ln_scale",
        "L1_xattn_ln_bias", "L1_ffn_q_w", "L1_ffn_q_b", "L1_ffn_k_w", "L1_ffn_k_b", "L1_ffn_v_w", "L1_ffn_v_b",
        "L1_ffn_o_w", "L1_ffn_o_b", "L1_ffn_router_w", "L1_ffn_router_b", "L1_ffn_w1", "L1_ffn_b1", "L1_ffn_w2",
        "L1_ffn_b2"]


def kernel(**inputs):
    import numpy as _np
    import concourse.bacc as _bacc
    from concourse import mybir as _mybir
    from concourse.bass_utils import run_bass_kernel_spmd as _run

    nc = _bacc.Bacc("TRN2", target_bir_lowering=False, num_devices=1)
    arrays, args = {}, {}
    for name in _INS:
        a = _np.ascontiguousarray(inputs[name])
        arrays[f"in_{name}_dram"] = a
        args[name] = nc.dram_tensor(f"in_{name}_dram", a.shape, _mybir.dt.from_np(a.dtype), kind="ExternalInput").ap()
    out = nc.dram_tensor("out_0_dram", (NT, P, D), F32, kind="ExternalOutput").ap()
    build(nc, args, out)
    r = _run(nc, [arrays], core_ids=[0])
    return r.results[0]["out_0_dram"]
```

```python
import math
from contextlib import ExitStack

import concourse.bass as bass
from concourse import mybir

F32 = mybir.dt.float32
BF16 = mybir.dt.bfloat16
I32 = mybir.dt.int32
ACT = mybir.ActivationFunctionType
ALU = mybir.AluOpType
AX = mybir.AxisListType

P = 128
NT = 16
T = NT * P
D = 256
KD = D // P
CTX = 512
KC = CTX // P
E = 8
PASSES = ((0, 0), (0, 1), (1, 0))
LN_EPS = 1e-5
RMS_EPS = 1e-5
DECAY_EPS = 0.001
DECAY_DT = -math.log(-math.expm1(-DECAY_EPS))
XHEADS, XDH = 16, 64
LHEADS, LDH = 16, 8


def ts(start, size):
    return bass.ds(start, size)


AHEAD = 1


def start_ahead(sp, *sems):
    for sem in sems:
        sp.sem_inc(sem, AHEAD)


def wait_past_zero(eng, sem, value):
    if not isinstance(value, int) or value > 0:
        eng.wait_ge(sem, value)


class Chain:

    def __init__(self, eng, sem):
        self.eng, self.sem, self.n = eng, sem, 0

    def link(self, ins):
        self.n += 1
        ins.then_inc(self.sem, 1)
        self.eng.wait_ge(self.sem, self.n)


class Scope(ExitStack):

    def __init__(self, nc, stage):
        super().__init__()
        self.nc, self.stage, self.sems = nc, stage, []
        self.callback(self.clear)

    def sb(self, name, shape, dt=F32):
        return self.enter_context(self.nc.sbuf_tensor(f"{self.stage}_{name}", shape, dt))

    def sem(self, name):
        self.sems.append(self.nc.alloc_semaphore(f"{self.stage}_{name}"))
        return self.sems[-1]

    def clear(self):
        if self.sems:
            self.nc.clear_and_free_semaphores(self.sems)
            self.nc.all_engine_barrier()

    def block(self):
        return self.enter_context(self.nc.Block())


class Shared:

    def __init__(self, nc, scope):
        self.ps = scope.enter_context(nc.psum_tensor("banks", [P, 8, 512], F32))
        self.x = scope.sb("x_res", [P, NT, D])
        self.zt = scope.sb("zt", [P, 2, KD, T], BF16)
        self.ident = scope.sb("ident", [P, P])
        self.gates = scope.sb("gates", [P, 4])
        self.cw = scope.sb("cw", [P, NT, E])
        self.mean = scope.sb("mean", [P, NT])
        self.rstd = scope.sb("rstd", [P, NT])


def tile_stats(eng, src, raw, done):
    for b in range(NT):
        eng.bn_stats(raw[:, b, :], src[:, b, :]).then_inc(done, 1)


def combine_stats(eng, chain, raw, mean, var, tmp, width):
    half = width // 2
    me, mo, ve, vo = raw[:, :, 1], raw[:, :, 4], raw[:, :, 2], raw[:, :, 5]
    chain.link(eng.tensor_tensor(mean, me, mo, ALU.add))
    chain.link(eng.tensor_scalar(mean, mean, 0.5, None, ALU.mult))
    chain.link(eng.tensor_tensor(tmp, me, mo, ALU.subtract))
    chain.link(eng.tensor_tensor(tmp, tmp, tmp, ALU.mult))
    chain.link(eng.tensor_tensor(var, ve, vo, ALU.add))
    chain.link(eng.tensor_scalar(var, var, 1.0 / width, None, ALU.mult))
    chain.link(eng.scalar_tensor_tensor(out=var, in0=tmp, scalar=0.25, in1=var, op0=ALU.mult, op1=ALU.add))


def depool_stage(nc, S, A):
    with Scope(nc, "dp") as c:
        ctx = c.sb("ctx", [P, NT, CTX])
        lens = c.sb("lens", [NT, 2, P], I32)
        bidx = c.sb("bidx", [NT, 3, P])
        idxT = c.sb("idxT", [P, NT])
        iota_i = c.sb("iota_i", [P, P], I32)
        iota_s = c.sb("iota_s", [P, P])
        part_i = c.sb("part_i", [P, 1], I32)
        part = c.sb("part", [P, 1])
        ones = c.sb("ones", [P, P], BF16)
        tri = c.sb("tri", [P, P], BF16)
        hot = c.sb("hot", [P, NT, P], BF16)
        hit = c.sb("hit", [P, NT])
        diff = c.sb("diff", [P, NT, P])
        decay = c.sb("decay", [P, NT, P])
        win = c.sb("win", [P, KD, D])
        winT = c.sb("winT", [P, KD, D])
        gres = c.sb("gres", [P, KD])
        ginit = c.sb("ginit", [P, D])
        bin_row = c.sb("bin_row", [P, D])
        graw = c.sb("graw", [P, 4])
        raw = c.sb("raw", [P, NT, 6])
        var = c.sb("var", [P, 2, NT])
        tmp = c.sb("tmp", [P, NT])
        ssq = c.sb("ssq", [P, NT])
        rctx = c.sb("rctx", [P, NT])
        sq = c.sb("sq", [P, 2, CTX])
        z = c.sb("z", [P, 2, D])
        zT = c.sb("zT", [P, 2, D])
        pick = c.sb("pick", [P, 2, P])
        cg = c.sb("cg", [P, 2, D])

        s_len, s_win, s_rows, s_x = (c.sem(n) for n in ("len", "win", "rows", "x"))
        s_ctx = [c.sem(f"ctx{q}") for q in range(4)]
        s_pool = c.sem("pool")
        s_dve = c.sem("dve")
        s_idx, s_idxT, s_hot, s_hits, s_step, s_cum, s_diff = (
            c.sem(n) for n in ("idx", "idxT", "hot", "hits", "step", "cum", "diff"))
        s_decay, s_wT, s_wTs, s_stats, s_var, s_root, s_act = (
            c.sem(n) for n in ("decay", "wT", "wTs", "stats", "var", "root", "act"))
        s_gate, s_bias = c.sem("gate"), c.sem("bias")
        s_z, s_zt, s_ztc, s_pick, s_out, s_xb, s_res = (
            c.sem(n) for n in ("z", "zt", "ztc", "pick", "out", "xb", "res"))
        ps = S.ps
        block = c.block()
        CONSTS = 7

        @block.sync
        def _(sp):
            sp.dma_start(lens[:, 0, :], A["mask_BxS2_if0"]).then_inc(s_len, 16)
            for q in range(4):
                sp.dma_start(S.x[:, 4 * q:4 * q + 4, :],
                             A["x"][4 * q:4 * q + 4].rearrange("b p d -> p b d")).then_inc(s_x, 16)
            sp.dma_start(win[:, :, :], A["L0_xattn_W_in"].rearrange("(c p) d -> p c d", p=P)).then_inc(s_win, 16)
            for q in range(4):
                sp.dma_start(ctx[:, 4 * q:4 * q + 4, :],
                             A["ctx_2048"][4 * q:4 * q + 4].rearrange("b p d -> p b d")).then_inc(s_ctx[q], 16)

        @block.gpsimd
        def _(pool):
            chain = Chain(pool, s_pool)
            chain.link(pool.memset(S.ident[:, :], 0.0))
            chain.link(pool.affine_select(out=S.ident[:, :], in_=S.ident[:, :], compare_op=ALU.not_equal, fill=1.0,
                                          base=0, pattern=[[-1, P]], channel_multiplier=1))
            chain.link(pool.iota(iota_i[:, :], pattern=[[1, P]], base=0, channel_multiplier=0))
            chain.link(pool.iota(part_i[:, :], pattern=[[0, 1]], base=0, channel_multiplier=1))
            chain.link(pool.memset(ones[:, :], 1.0))
            chain.link(pool.memset(tri[:, :], 1.0))
            chain.link(pool.affine_select(out=tri[:, :], in_=tri[:, :], compare_op=ALU.is_ge, fill=0.0,
                                          base=0, pattern=[[1, P]], channel_multiplier=-1))
            assert chain.n == CONSTS
            pool.wait_ge(s_bias, 1)
            for b in range(NT):
                pool.wait_ge(s_z, b + 1)
                pool.tensor_tensor(S.x[:, b, :], S.x[:, b, :], bin_row[:, :], ALU.add).then_inc(s_xb, 1)

        @block.scalar
        def _(act):
            act.dma_start(graw[:, 0:2], A["g_xattn"].partition_broadcast(P)).then_inc(s_rows, 16)
            act.dma_start(graw[:, 2:4], A["g_ffn"].partition_broadcast(P)).then_inc(s_rows, 16)
            act.dma_start(ginit[:, :], A["L0_xattn_g_init"][0:D].partition_broadcast(P)).then_inc(s_rows, 16)
            act.dma_start(bin_row[:, :], A["L0_xattn_b_in"].partition_broadcast(P)).then_inc(s_rows, 16)
            for k in range(KD):
                act.dma_start(gres[:, k:k + 1],
                              A["L0_xattn_g_res"][k * P:(k + 1) * P].rearrange("(p a) -> p a", a=1)).then_inc(s_rows, 16)
            act.wait_ge(s_rows, 96)
            act.activation(S.gates[:, :], graw[:, :], ACT.Tanh).then_inc(s_gate, 1)
            for b in range(NT):
                if b % 4 == 0:
                    act.wait_ge(s_ctx[b // 4], 16)
                if b >= 2:
                    act.wait_ge(s_act, b - 1)
                act.activation(sq[:, b % 2, :], ctx[:, b, :], ACT.Square, accum_out=ssq[:, b:b + 1]).then_inc(s_act, 1)
            act.wait_ge(s_var, 1)
            act.activation(S.rstd[:, :], var[:, 0, :], ACT.Sqrt).then_inc(s_root, 1)
            act.activation(rctx[:, :], var[:, 1, :], ACT.Sqrt).then_inc(s_root, 1)
            act.wait_ge(s_diff, 1)
            act.activation(decay[:, :, :], decay[:, :, :], ACT.Exp, scale=-DECAY_DT).then_inc(s_decay, 1)
            for b in range(NT):
                act.wait_ge(s_zt, b + 1)
                if b >= 2:
                    act.wait_ge(s_out, b - 1)
                act.activation(zT[:, b % 2, :], ps[:, b % 2, 0:D], ACT.Copy).then_inc(s_ztc, 1)

        @block.tensor
        def _(pe):
            pe.wait_ge(s_pool, CONSTS)
            pe.wait_ge(s_win, 16)
            for k in range(KD):
                for e in range(KD):
                    mm = pe.transpose(ps[:, 7, k * D + e * P:k * D + e * P + P], win[:, e, k * P:k * P + P], S.ident[:, :])
            mm.then_inc(s_wT, 1)
            pe.wait_ge(s_idx, 1)
            pe.transpose(ps[:, 6, 0:NT], bidx[:, 2, :], S.ident[0:NT, 0:NT]).then_inc(s_idxT, 1)
            pe.wait_ge(s_hot, 1)
            for b in range(NT):
                mm = pe.matmul(ps[:, 5, b:b + 1], hot[:, b, :], ones[:, 0:1], start=True, stop=True)
            mm.then_inc(s_hits, 1)
            pe.wait_ge(s_step, 1)
            for q in range(4):
                mm = pe.matmul(ps[:, q, :], ones[:, :], hot[:, 4 * q:4 * q + 4, :].rearrange("p b s -> p (b s)"),
                               start=True, stop=True)
            mm.then_inc(s_cum, 1)
            pe.wait_ge(s_diff, 1)
            pe.wait_ge(s_wTs, 1)
            for b in range(NT + 1):
                if b < NT:
                    pe.wait_ge(s_z, b + 1)
                    if b >= 2:
                        pe.wait_ge(s_ztc, b - 1)
                    for k in range(KD):
                        mm = pe.transpose(ps[:, b % 2, k * P:k * P + P], z[:, b % 2, k * P:k * P + P], S.ident[:, :])
                    mm.then_inc(s_zt, 1)
                if b > 0:
                    done, j = b - 1, (b - 1) % 2
                    pe.wait_ge(s_pick, done + 1)
                    if done >= 2:
                        pe.wait_ge(s_res, done - 1)
                    pe.matmul(ps[:, 2 + j, 0:D], pick[:, j, :], cg[:, j, :], start=True, stop=False)
                    pe.wait_ge(s_ztc, done + 1)
                    for k in range(KD):
                        mm = pe.matmul(ps[:, 2 + j, 0:D], zT[:, j, k * P:k * P + P], winT[:, k, :],
                                       start=False, stop=(k == KD - 1))
                    mm.then_inc(s_out, 1)

        @block.vector
        def _(dve):
            chain = Chain(dve, s_dve)
            dve.wait_ge(s_len, 16)
            src = 0
            for step in (1, 2, 4, 8, 16, 32, 64):
                a, b = lens[:, src, :], lens[:, 1 - src, :]
                chain.link(dve.tensor_copy(b[:, 0:step], a[:, 0:step]))
                chain.link(dve.tensor_tensor(b[:, step:P], a[:, step:P], a[:, 0:P - step], ALU.add))
                src = 1 - src
            chain.link(dve.tensor_copy(bidx[:, 0, :], lens[:, src, :]))
            chain.link(dve.tensor_scalar(bidx[:, 0, :], bidx[:, 0, :], -1.0, None, ALU.add))
            chain.link(dve.tensor_scalar(bidx[:, 1, :], bidx[:, 0, :], 0.0, float(P), ALU.is_lt, ALU.mult))
            dve.tensor_tensor(bidx[:, 2, :], bidx[:, 0, :], bidx[:, 1, :], ALU.add).then_inc(s_idx, 1)
            dve.wait_ge(s_pool, CONSTS)
            chain.link(dve.tensor_copy(iota_s[:, :], iota_i[:, :]))
            chain.link(dve.tensor_copy(part[:, :], part_i[:, :]))
            dve.wait_ge(s_idxT, 1)
            chain.link(dve.tensor_copy(idxT[:, :], ps[:, 6, 0:NT]))
            dve.tensor_tensor(hot[:, :, :], iota_s[:, :].unsqueeze(1).broadcast_to([P, NT, P]),
                              idxT[:, :].unsqueeze(2).broadcast_to([P, NT, P]), ALU.is_equal).then_inc(s_hot, 1)
            dve.wait_ge(s_wT, 1)
            dve.wait_ge(s_rows, 96)
            for k in range(KD):
                w = dve.tensor_scalar(winT[:, k, :], ps[:, 7, k * D:k * D + D], gres[:, k:k + 1], None, ALU.mult)
            w.then_inc(s_wTs, 1)
            dve.wait_ge(s_hits, 1)
            chain.link(dve.tensor_scalar(hit[:, :], ps[:, 5, 0:NT], 1.0, None, ALU.min))
            dve.tensor_tensor(hot[:, :, :], tri[:, :].unsqueeze(1).broadcast_to([P, NT, P]),
                              hit[:, :].unsqueeze(2).broadcast_to([P, NT, P]), ALU.mult).then_inc(s_step, 1)
            dve.wait_ge(s_x, 64)
            tile_stats(dve, S.x, raw, s_stats)
            dve.wait_ge(s_stats, NT)
            combine_stats(dve, chain, raw, S.mean[:, :], var[:, 0, :], tmp[:, :], D)
            chain.link(dve.tensor_scalar(var[:, 0, :], var[:, 0, :], 1.0 + RMS_EPS, RMS_EPS * LN_EPS, ALU.mult, ALU.add))
            dve.wait_ge(s_cum, 1)
            for q in range(4):
                chain.link(dve.tensor_scalar(diff[:, 4 * q:4 * q + 4, :].rearrange("p b s -> p (b s)"), ps[:, q, :],
                                             -1.0, 0.0, ALU.add, ALU.max))
            dve.wait_ge(s_act, NT)
            dve.tensor_scalar(var[:, 1, :], ssq[:, :], 1.0 / CTX, RMS_EPS, ALU.mult, ALU.add).then_inc(s_var, 1)
            chain.link(dve.tensor_scalar(diff[:, :, :], diff[:, :, :], float(P - 1), part[:, :], ALU.min, ALU.subtract))
            dve.tensor_scalar(decay[:, :, :], diff[:, :, :], 0.0, None, ALU.max).then_inc(s_diff, 1)
            dve.wait_ge(s_gate, 1)
            dve.tensor_scalar(bin_row[:, :], bin_row[:, :], S.gates[:, 0:1], None, ALU.mult).then_inc(s_bias, 1)
            dve.wait_ge(s_root, 2)
            chain.link(dve.reciprocal(S.rstd[:, :], S.rstd[:, :]))
            chain.link(dve.reciprocal(rctx[:, :], rctx[:, :]))
            chain.link(dve.tensor_scalar(rctx[:, :], rctx[:, :], math.exp(-DECAY_EPS), None, ALU.mult))
            for b in range(NT + 2):
                j = b % 2
                if b < NT:
                    if b >= 2:
                        dve.wait_ge(s_zt, b - 1)
                    dve.tensor_scalar(z[:, j, :], S.x[:, b, :], S.mean[:, b:b + 1], S.rstd[:, b:b + 1],
                                      ALU.subtract, ALU.mult).then_inc(s_z, 1)
                if b >= 2:
                    dve.wait_ge(s_out, b - 1)
                if b < NT:
                    dve.scalar_tensor_tensor(out=cg[:, j, :], in0=ctx[:, b, 0:D], scalar=rctx[:, b:b + 1],
                                             in1=ginit[:, :], op0=ALU.mult, op1=ALU.mult)
                    if b == 0:
                        dve.wait_ge(s_decay, 1)
                    dve.scalar_tensor_tensor(out=pick[:, j, :], in0=diff[:, b, :], scalar=0.0, in1=decay[:, b, :],
                                             op0=ALU.is_ge, op1=ALU.mult).then_inc(s_pick, 1)
                if b >= 2:
                    dve.wait_ge(s_xb, b - 1)
                    dve.scalar_tensor_tensor(out=S.x[:, b - 2, :], in0=ps[:, 2 + j, 0:D], scalar=S.gates[:, 0:1],
                                             in1=S.x[:, b - 2, :], op0=ALU.mult, op1=ALU.add).then_inc(s_res, 1)


class Norm:
    UNITS, DEEP, LAG = NT // 2, 4, 2

    def __init__(self, S, c, residual=None, z=None):
        self.S, self.residual = S, residual
        self.raw = c.sb("nraw", [P, NT, 6])
        self.tmp = c.sb("ntmp", [P, NT])
        self.z = c.sb("nz", [P, self.DEEP, 2, D]) if z is None else z
        self.s_dve, self.s_stats, self.s_var, self.s_root = (c.sem(n) for n in ("ndve", "nstats", "nvar", "nroot"))
        self.s_z, self.s_tr, self.s_hi, self.s_lo, self.s_res = (c.sem(n) for n in ("nz", "ntr", "nhi", "nlo", "nres"))

    def bank(self, u):
        return self.S.ps[:, u % self.DEEP, :].rearrange("p (t k s) -> p k t s", t=2, k=KD)

    def part(self, u, a):
        return self.S.zt[:, a, :, 2 * u * P:(2 * u + 2) * P].rearrange("p k (t s) -> p k t s", t=2)

    def root(self, act):
        act.wait_ge(self.s_var, 1)
        act.activation(self.S.rstd[:, :], self.S.rstd[:, :], ACT.Sqrt).then_inc(self.s_root, 1)

    def high(self, act, u):
        act.wait_ge(self.s_tr, u + 1)
        act.activation(self.part(u, 0), self.bank(u), ACT.Copy).then_inc(self.s_hi, 1)

    def turn(self, pe, u):
        pe.wait_ge(self.s_z, 2 * u + 2)
        if u >= self.DEEP:
            pe.wait_ge(self.s_lo, u - self.DEEP + 1)
        for t in range(2):
            for k in range(KD):
                mm = pe.transpose(self.S.ps[:, u % self.DEEP, (t * KD + k) * P:(t * KD + k + 1) * P],
                                  self.z[:, u % self.DEEP, t, k * P:k * P + P], self.S.ident[:, :])
        mm.then_inc(self.s_tr, 1)

    def statistics(self, dve):
        tile_stats(dve, self.S.x, self.raw, self.s_stats)

    def moments(self, dve):
        S = self.S
        chain = Chain(dve, self.s_dve)
        dve.wait_ge(self.s_stats, NT)
        combine_stats(dve, chain, self.raw, S.mean[:, :], S.rstd[:, :], self.tmp[:, :], D)
        dve.tensor_scalar(S.rstd[:, :], S.rstd[:, :], LN_EPS, None, ALU.add).then_inc(self.s_var, 1)
        dve.wait_ge(self.s_root, 1)
        chain.link(dve.reciprocal(S.rstd[:, :], S.rstd[:, :]))

    def normalise(self, dve, u):
        for t in range(2):
            b = 2 * u + t
            dve.tensor_scalar(self.z[:, u % self.DEEP, t, :], self.S.x[:, b, :], self.S.mean[:, b:b + 1],
                              self.S.rstd[:, b:b + 1], ALU.subtract, ALU.mult).then_inc(self.s_z, 1)

    def low(self, dve, u):
        dve.wait_ge(self.s_hi, u + 1)
        dve.tensor_tensor(self.part(u, 1), self.bank(u), self.part(u, 0), ALU.subtract).then_inc(self.s_lo, 1)

    def add_residual(self, dve, u):
        dve.wait_ge(self.s_z, 2 * u + 2)
        for t in range(2):
            x = self.S.x[:, 2 * u + t, :]
            dve.scalar_tensor_tensor(out=x, in0=self.z[:, u % self.DEEP, t, :],
                                     scalar=self.S.gates[:, self.residual:self.residual + 1],
                                     in1=x, op0=ALU.mult, op1=ALU.add).then_inc(self.s_res, 1)

    def step(self, dve, u):
        if u < self.UNITS:
            self.normalise(dve, u)
        if u >= self.LAG:
            self.low(dve, u - self.LAG)
        if self.residual is not None and u < self.UNITS:
            self.add_residual(dve, u)


def norm_stage(nc, S, stage, prefetch=None, residual=None):
    with Scope(nc, stage) as c:
        norm = Norm(S, c, residual)
        block = c.block()

        if prefetch:
            @block.sync
            def _(sp):
                prefetch.load_first(sp)

            @block.gpsimd
            def _(pool):
                prefetch.split_first(pool)

        @block.scalar
        def _(act):
            norm.root(act)
            for u in range(norm.UNITS):
                norm.high(act, u)
                if prefetch and u < prefetch.firsts:
                    prefetch.high_first(act, u)

        @block.tensor
        def _(pe):
            for u in range(norm.UNITS):
                norm.turn(pe, u)

        @block.vector
        def _(dve):
            norm.statistics(dve)
            norm.moments(dve)
            for u in range(norm.UNITS + norm.LAG):
                norm.step(dve, u)


def gate_stage(nc, S, stage, wg, bg, b2, gate, top_of_probs, factor=1.0, prefetch=None, norm_first=False):
    with Scope(nc, stage) as c:
        wraw = c.sb("wraw", [P, KD, E])
        w = c.sb("w", [P, 2, KD, E], BF16)
        brow = c.sb("brow", [P, E])
        b2rep = c.sb("b2rep", [P, D])
        ones = c.sb("ones", [P, NT])
        own = c.sb("own", [P, NT])
        desc = c.sb("desc", [P, E])
        lg = c.sb("lg", [P, NT, E])
        top = c.sb("top", [P, NT])
        pr = c.sb("pr", [P, NT, E])
        best = c.sb("best", [P, NT, E])
        second = c.sb("second", [P, NT, E])
        rest = c.sb("rest", [P, NT, E])
        scale = c.sb("scale", [P, 1])
        cwT = c.sb("cwT", [P, P])
        rhs = c.sb("rhs", [P, NT, D])
        norm = Norm(S, c, z=rhs[:, 0:2 * Norm.DEEP, :].rearrange("p (u t) d -> p u t d", t=2)) if norm_first else None
        s_w, s_b2, s_pool, s_dve, s_split = (c.sem(n) for n in ("w", "b2", "pool", "dve", "split"))
        s_lg, s_sub, s_exp, s_cw, s_cwT, s_cwTs, s_rhs, s_bias, s_res = (
            c.sem(n) for n in ("lg", "sub", "exp", "cw", "cwT", "cwTs", "rhs", "bias", "res"))
        ps = S.ps
        block = c.block()
        BANKS = 4

        @block.sync
        def _(sp):
            sp.dma_start(wraw[:, :, :], wg.rearrange("(k p) e -> p k e", p=P)).then_inc(s_w, 16)
            sp.dma_start(brow[:, :], bg.partition_broadcast(P)).then_inc(s_w, 16)
            for t in range(NT):
                sp.dma_start(b2rep[E * t:E * t + E, :], b2).then_inc(s_b2, 16)
            if prefetch:
                prefetch.load_first(sp)

        @block.gpsimd
        def _(pool):
            chain = Chain(pool, s_pool)
            chain.link(pool.memset(ones[:, :], 1.0))
            chain.link(pool.affine_select(out=own[:, :], in_=ones[:, :], compare_op=ALU.is_ge, fill=0.0,
                                          base=0, pattern=[[-E, NT]], channel_multiplier=1))
            chain.link(pool.affine_select(out=own[:, :], in_=own[:, :], compare_op=ALU.is_ge, fill=0.0,
                                          base=E - 1, pattern=[[E, NT]], channel_multiplier=-1))
            for e in range(E):
                d = pool.memset(desc[:, e:e + 1], float(E - e))
            d.then_inc(s_pool, 1)
            pool.wait_ge(s_b2, 16 * NT)
            if norm:
                pool.wait_ge(norm.s_tr, norm.UNITS)
            for u in range(NT // 2):
                pool.tensor_tensor(rhs[:, 2 * u:2 * u + 2, :], b2rep[:, :].unsqueeze(1).broadcast_to([P, 2, D]),
                                   own[:, 2 * u:2 * u + 2].unsqueeze(2).broadcast_to([P, 2, D]), ALU.mult).then_inc(s_rhs, 1)
            if prefetch:
                prefetch.split_first(pool)

        @block.scalar
        def _(act):
            if norm:
                norm.root(act)
                for u in range(norm.UNITS):
                    norm.high(act, u)
            for i in range(prefetch.firsts if prefetch else 0):
                prefetch.high_first(act, i)
            act.wait_ge(s_sub, 1)
            act.activation(pr[:, :, :], pr[:, :, :], ACT.Exp).then_inc(s_exp, 1)

        @block.tensor
        def _(pe):
            if norm:
                for u in range(norm.UNITS):
                    norm.turn(pe, u)
            pe.wait_ge(s_split, 2)
            for b in range(NT):
                if norm and b % 2 == 0:
                    pe.wait_ge(norm.s_lo, b // 2 + 1)
                n = 0
                for wp, ap in PASSES:
                    for k in range(KD):
                        mm = pe.matmul(ps[:, 7, b * E:b * E + E], S.zt[:, ap, k, b * P:b * P + P], w[:, wp, k, :],
                                       start=(n == 0), stop=(n == 3 * KD - 1))
                        n += 1
            mm.then_inc(s_lg, 1)
            pe.wait_ge(s_cw, 1)
            pe.transpose(ps[:, 6, 0:P], S.cw[:, :, :].rearrange("p t e -> p (t e)"), S.ident[:, :]).then_inc(s_cwT, 1)
            pe.wait_ge(s_cwTs, 1)
            for u in range(NT // 2):
                pe.wait_ge(s_rhs, u + 1)
                if u >= BANKS:
                    pe.wait_ge(s_res, u - BANKS + 1)
                pe.matmul(ps[:, u % BANKS, :], cwT[:, :], rhs[:, 2 * u:2 * u + 2, :].rearrange("p t d -> p (t d)"),
                          start=True, stop=True).then_inc(s_bias, 1)

        @block.vector
        def _(dve):
            chain = Chain(dve, s_dve)
            if norm:
                norm.statistics(dve)
                norm.moments(dve)
            dve.wait_ge(s_w, 32)
            dve.tensor_copy(w[:, 0, :, :], wraw[:, :, :]).then_inc(s_split, 1)
            dve.wait_ge(s_split, 1)
            dve.tensor_tensor(w[:, 1, :, :], wraw[:, :, :], w[:, 0, :, :], ALU.subtract).then_inc(s_split, 1)
            for u in range(norm.UNITS + norm.LAG if norm else 0):
                norm.step(dve, u)
            dve.wait_ge(s_lg, 1)
            chain.link(dve.tensor_tensor(lg[:, :, :], ps[:, 7, 0:NT * E].rearrange("p (t e) -> p t e", e=E),
                                         brow[:, :].unsqueeze(1).broadcast_to([P, NT, E]), ALU.add))
            chain.link(dve.tensor_reduce(top[:, :], lg[:, :, :], AX.X, ALU.max))
            dve.tensor_tensor(pr[:, :, :], lg[:, :, :], top[:, :].unsqueeze(2).broadcast_to([P, NT, E]),
                              ALU.subtract).then_inc(s_sub, 1)
            dve.wait_ge(s_exp, 1)
            dve.wait_ge(s_pool, 4)

            def sum_up(values):
                chain.link(dve.tensor_reduce(top[:, :], values, AX.X, ALU.add))

            ranked = lg
            if top_of_probs:
                sum_up(pr[:, :, :])
                chain.link(dve.reciprocal(top[:, :], top[:, :]))
                chain.link(dve.tensor_tensor(pr[:, :, :], pr[:, :, :], top[:, :].unsqueeze(2).broadcast_to([P, NT, E]),
                                             ALU.mult))
                ranked = pr
            flat = lambda t: t[:, :, :].rearrange("p t e -> p (t e)")
            row = lambda t: t[:, :].unsqueeze(2).broadcast_to([P, NT, E])
            for rank, (left, kept) in enumerate(((ranked, best), (rest, second))):
                if rank == 1 or top_of_probs:
                    chain.link(dve.tensor_reduce(top[:, :], left[:, :, :], AX.X, ALU.max))
                chain.link(dve.tensor_tensor(kept[:, :, :], left[:, :, :], row(top), ALU.is_equal))
                chain.link(dve.tensor_tensor(kept[:, :, :], kept[:, :, :], desc[:, :].unsqueeze(1).broadcast_to([P, NT, E]),
                                             ALU.mult))
                chain.link(dve.tensor_reduce(top[:, :], kept[:, :, :], AX.X, ALU.max))
                chain.link(dve.tensor_tensor(kept[:, :, :], kept[:, :, :], row(top), ALU.is_equal))
                if rank == 0:
                    chain.link(dve.scalar_tensor_tensor(out=flat(rest), in0=flat(best), scalar=-3e38, in1=flat(ranked),
                                                        op0=ALU.mult, op1=ALU.add))
            chain.link(dve.tensor_tensor(best[:, :, :], best[:, :, :], second[:, :, :], ALU.add))
            chain.link(dve.tensor_tensor(pr[:, :, :], pr[:, :, :], best[:, :, :], ALU.mult))
            sum_up(pr[:, :, :])
            if top_of_probs:
                chain.link(dve.tensor_scalar(top[:, :], top[:, :], 1e-8, None, ALU.add))
            chain.link(dve.reciprocal(top[:, :], top[:, :]))
            chain.link(dve.tensor_scalar(scale[:, :], S.gates[:, gate:gate + 1], factor, None, ALU.mult))
            chain.link(dve.tensor_scalar(top[:, :], top[:, :], scale[:, :], None, ALU.mult))
            dve.tensor_tensor(S.cw[:, :, :], pr[:, :, :], top[:, :].unsqueeze(2).broadcast_to([P, NT, E]),
                              ALU.mult).then_inc(s_cw, 1)
            dve.wait_ge(s_cwT, 1)
            dve.tensor_copy(cwT[:, :], ps[:, 6, 0:P]).then_inc(s_cwTs, 1)
            for u in range(NT // 2):
                x = S.x[:, 2 * u:2 * u + 2, :].rearrange("p t d -> p (t d)")
                dve.wait_ge(s_bias, u + 1)
                dve.tensor_tensor(x, ps[:, u % BANKS, :], x, ALU.add).then_inc(s_res, 1)


class Ring:

    def __init__(self, nc, scope, mats):
        self.mats = mats
        self.n = len(mats)
        self.raw, self.split = [], []
        for i, m in enumerate(mats):
            rows, cols = m.shape[1], m.shape[2]
            self.raw.append(scope.sb(f"raw{i}", [P, rows // P, cols]))
            self.split.append([scope.sb(f"w{i}_{j}", [P, 2, rows // P, cols], BF16) for j in range(2)])
        self.s_turn = scope.sem("wturn")
        self.s_raw, self.s_split, self.s_free = scope.sem("wraw"), scope.sem("wsplit"), scope.sem("wfree")
        self.s_high, self.firsts = scope.sem("whigh"), self.n

    def load(self, sp, e, wait=True):
        if wait:
            sp.wait_ge(self.s_split, 2 * self.n * e)
        for raw, m in zip(self.raw, self.mats):
            src = m[e] if isinstance(e, int) else m[ts(e, 1)].squeeze(0)
            sp.dma_start(raw[:, :, :], src.rearrange("(k p) h -> p k h", p=P)).then_inc(self.s_raw, 16)

    def halves(self, pool, e, j, wait=True):
        pool.wait_ge(self.s_raw, 16 * self.n * (e + 1))
        if wait:
            pool.wait_ge(self.s_free, e - 1)
            pool.sem_inc(self.s_turn)
        for i in range(self.n):
            hi, lo = self.split[i][j][:, 0, :, :], self.split[i][j][:, 1, :, :]
            pool.tensor_copy(hi, self.raw[i][:, :, :]).then_inc(self.s_split, 1)
            pool.wait_ge(self.s_split, 2 * self.n * e + 2 * i + 1)
            pool.tensor_tensor(lo, self.raw[i][:, :, :], hi, ALU.subtract).then_inc(self.s_split, 1)

    def load_first(self, sp):
        self.load(sp, 0, wait=False)

    def high_first(self, act, i):
        act.wait_ge(self.s_raw, 16 * self.n)
        act.activation(self.split[i][0][:, 0, :, :], self.raw[i][:, :, :], ACT.Copy).then_inc(self.s_high, 1)

    def split_first(self, pool):
        for i in range(self.n):
            pool.wait_ge(self.s_high, i + 1)
            pool.tensor_tensor(self.split[i][0][:, 1, :, :], self.raw[i][:, :, :], self.split[i][0][:, 0, :, :],
                               ALU.subtract).then_inc(self.s_split, 2)


def expert_stage(nc, S, stage, ring, up_bias, gate_bias, hid, following=None, out=None):
    M = hid // P
    NB, BT = 4, 4
    W = BT * P
    LAG = 2
    HB = 4
    gated = up_bias is not None
    with Scope(nc, stage) as c:
        nb = 2 if gated else 1
        brow = c.sb("brow", [E * M, nb, P])
        bcol = c.sb("bcol", [P, nb, E * M])
        prime = c.sb("prime", [P, 2, 2])
        acted = c.sb("acted", [P, 2, W])
        prod = c.sb("prod", [P, 2, W]) if gated else acted
        hg = c.sb("hg", [P, HB, 2, W], BF16)
        s_b, s_bT, s_bcol, s_turn, s_out = c.sem("b"), c.sem("bT"), c.sem("bcol"), c.sem("turn"), c.sem("out")
        s_gate, s_up, s_act, s_prod, s_hi, s_lo, s_down, s_y = (
            c.sem(n) for n in ("gate", "up", "act", "prod", "hi", "lo", "down", "y"))
        ps = S.ps
        GB, UB = (0, 1), (2, 3)
        YSETS = 1 if gated else 2
        def outputs(tb):
            return (4, 5) if gated or tb % 2 == 0 else UB

        PRIMED = 2
        LOWS = AHEAD if gated else PRIMED
        block = c.block()
        w_gate, w_up, w_down = 0, 1, ring.n - 1

        def over_blocks(eng, body, tail):
            with eng.Fori(0, E // 2) as pair:
                for j in range(2):
                    e = 2 * pair + j
                    body(e, j, 0, first=True)
                    if gated:
                        with eng.Fori(1, NB) as tb:
                            body(e, j, tb, first=False)
                    else:
                        for tb in range(1, NB):
                            body(e, j, tb, first=False)
                    tail(e, j)

        @block.sync
        def _(sp):
            start_ahead(sp, *[s_y] * YSETS)
            if gated:
                start_ahead(sp, s_lo)
            sp.dma_start(brow[:, 0, :], gate_bias.rearrange("e (m p) -> (e m) p", p=P)).then_inc(s_b, 16)
            if gated:
                sp.dma_start(brow[:, 1, :], up_bias.rearrange("e (m p) -> (e m) p", p=P)).then_inc(s_b, 16)
            with sp.Fori(1, E) as e:
                ring.load(sp, e)
            if following:
                following.load(sp)
            if out is not None:
                for tb in range(NB):
                    sp.wait_ge(s_y, (E - 1) * NB + tb + 1 + YSETS)
                    tiles = slice(tb * BT, (tb + 1) * BT)
                    sp.dma_start(out[tiles].rearrange("b p d -> p b d"), S.x[:, tiles, :]).then_inc(s_out, 16)
                sp.wait_ge(s_out, 16 * NB)

        @block.gpsimd
        def _(pool):
            ring.halves(pool, 1, 1, wait=False)
            with pool.Fori(1, E // 2) as pair:
                for j in range(2):
                    ring.halves(pool, 2 * pair + j, j)
            if following:
                following.halves(pool)

        @block.scalar
        def _(act):
            act.wait_ge(s_bT, 1)
            act.activation(bcol[:, :, :], ps[:, 7, 0:nb * E * M].rearrange("p (b m) -> p b m", b=nb), ACT.Copy).then_inc(s_bcol, 1)
            act.wait_ge(s_bcol, 1)
            for j in range(PRIMED):
                act.activation(prime[:, 0, j:j + 1], bcol[:, 0, 0:1], ACT.Copy).then_inc(s_act, 1)

            def body(e, j, tb, first):
                for m in range(M):
                    s = (e * NB + tb) * M + m
                    act.wait_ge(s_gate, s + 1)
                    act.sem_inc(s_turn)
                    act.activation(acted[:, m % 2, :], ps[:, GB[m % 2], :], ACT.Silu if gated else ACT.Gelu,
                                   bias=bcol[:, 0, ts(e * M + m, 1)]).then_inc(s_act, 1)

            over_blocks(act, body, lambda e, j: None)

        @block.tensor
        def _(pe):
            pe.wait_ge(s_b, 16 * nb)
            for i in range(nb):
                mm = pe.transpose(ps[:, 7, i * E * M:(i + 1) * E * M], brow[:, i, :], S.ident[0:E * M, 0:E * M])
            mm.then_inc(s_bT, 1)

            def up(e, j, tb, m):
                s = (e * NB + tb) * M + m
                if gated:
                    pe.wait_ge(s_prod, s - 1 + PRIMED)
                else:
                    pe.wait_ge(s_act, s - 1 + PRIMED)
                    pe.wait_ge(s_lo, s - 1 + PRIMED)
                for which, bank, ready in ((w_gate, GB[m % 2], s_gate), (w_up, UB[m % 2], s_up))[:nb]:
                    n = 0
                    for wp, ap in PASSES:
                        for k in range(KD):
                            mm = pe.matmul(ps[:, bank, :], ring.split[which][j][:, wp, k, m * P:m * P + P],
                                           S.zt[:, ap, k, ts(tb * W, W)], start=(n == 0), stop=(n == 3 * KD - 1))
                            n += 1
                    mm.then_inc(ready, 1)

            def down(e, j, tb, m):
                s = (e * NB + tb) * M + m
                pe.wait_ge(s_lo, s + 1 + LOWS)
                if m == 0:
                    pe.wait_ge(s_y, e * NB + tb + 1)
                for t in range(BT):
                    n = 0
                    for wp, ap in PASSES:
                        mm = pe.matmul(ps[:, outputs(tb)[t // 2], (t % 2) * D:(t % 2) * D + D],
                                       hg[:, m % HB, ap, t * P:t * P + P], ring.split[w_down][j][:, wp, m, :],
                                       start=(m == 0 and n == 0 and t % 2 == 0), stop=(m == M - 1 and n == 2),
                                       skip_group_check=True)
                        n += 1
                mm.then_inc(s_down, 1)
                return mm

            def body(e, j, tb, first):
                if first:
                    pe.wait_ge(ring.s_split, 2 * ring.n * (e + 1))
                for m in range(M):
                    up(e, j, tb, m)
                    if m >= LAG:
                        down(e, j, tb, m - LAG)
                    elif not first:
                        down(e, j, tb - 1, M - LAG + m)

            def tail(e, j):
                for m in range(M - LAG, M):
                    mm = down(e, j, NB - 1, m)
                pe.matmul(ps[:, 7, 0:8], hg[:, 0, 0, 0:P], ring.split[w_down][j][:, 0, 0, 0:8], start=True, stop=True
                          ).then_inc(ring.s_free, 1)

            over_blocks(pe, body, tail)

        @block.vector
        def _(dve):
            dve.wait_ge(s_bcol, 1)
            for j in range(PRIMED):
                dve.tensor_copy(prime[:, 1, j:j + 1], bcol[:, 0, 0:1]).then_inc(s_prod if gated else s_lo, 1)

            def hidden(e, tb, m):
                s = (e * NB + tb) * M + m
                if gated:
                    dve.wait_ge(s_lo, s + LOWS)
                    dve.wait_ge(s_up, s + 1)
                    dve.wait_ge(s_act, s + 1 + PRIMED)
                    dve.scalar_tensor_tensor(out=prod[:, m % 2, :], in0=ps[:, UB[m % 2], :],
                                             scalar=bcol[:, 1, ts(e * M + m, 1)], in1=acted[:, m % 2, :],
                                             op0=ALU.add, op1=ALU.mult).then_inc(s_prod, 1)
                    dve.wait_ge(s_prod, s + 1 + PRIMED)
                else:
                    dve.wait_ge(s_act, s + 1 + PRIMED)
                dve.tensor_copy(hg[:, m % HB, 0, :], prod[:, m % 2, :]).then_inc(s_hi, 1)
                dve.wait_ge(s_hi, s + 1)
                dve.tensor_tensor(hg[:, m % HB, 1, :], prod[:, m % 2, :], hg[:, m % HB, 0, :],
                                  ALU.subtract).then_inc(s_lo, 1)

            def collect(e, tb):
                dve.wait_ge(s_down, (e * NB + tb + 1) * M)
                for t in range(BT):
                    b = tb * BT + t
                    x = S.x[:, ts(b, 1), :].squeeze(1)
                    add = dve.scalar_tensor_tensor(out=x, in0=ps[:, outputs(tb)[t // 2], (t % 2) * D:(t % 2) * D + D],
                                                   scalar=S.cw[:, ts(b, 1), ts(e, 1)].squeeze(1), in1=x,
                                                   op0=ALU.mult, op1=ALU.add)
                add.then_inc(s_y, 1)

            def body(e, j, tb, first):
                for m in range(M):
                    hidden(e, tb, m)
                    if m == LAG - 1 and not first:
                        collect(e, tb - 1)

            over_blocks(dve, body, lambda e, j: collect(e, NB - 1))


class CrossWeights:

    CHUNK = 2048
    SLOTS = 2

    def __init__(self, nc, scope, wq, wkv, wout):
        inner = wq.shape[1]
        self.q = scope.sb("wq", [P, 2, KD, inner], BF16)
        self.kv = scope.sb("wkv", [P, 2, KC, 2 * inner], BF16)
        self.out = scope.sb("wout", [P, 2, inner // P, D], BF16)
        self.raw = scope.sb("xraw", [P, self.SLOTS, self.CHUNK])
        self.s_raw = [scope.sem(f"xraw{i}") for i in range(self.SLOTS)]
        self.s_split = scope.sem("xsplit")
        self.parts = [(wq.rearrange("(k p) h -> p k h", p=P), lambda a: self.q[:, a, :, :])]
        self.parts += [(wkv[k * P:(k + 1) * P, :].unsqueeze(1), lambda a, k=k: self.kv[:, a, k:k + 1, :]) for k in range(KC)]
        self.parts += [(wout.rearrange("(m p) d -> p m d", p=P), lambda a: self.out[:, a, :, :])]

    def slot(self, i, like):
        return self.raw[:, i % self.SLOTS, :].rearrange("p (k h) -> p k h", k=like.shape[1])

    def load(self, sp):
        for i, (src, _) in enumerate(self.parts):
            if i >= self.SLOTS:
                sp.wait_ge(self.s_split, 2 * (i - self.SLOTS + 1))
            sp.dma_start(self.slot(i, src), src).then_inc(self.s_raw[i % self.SLOTS], 16)

    def halves(self, pool):
        for i, (src, dst) in enumerate(self.parts):
            pool.wait_ge(self.s_raw[i % self.SLOTS], 16 * (i // self.SLOTS + 1))
            pool.tensor_copy(dst(0), self.slot(i, src)).then_inc(self.s_split, 1)
            pool.wait_ge(self.s_split, 2 * i + 1)
            pool.tensor_tensor(dst(1), self.slot(i, src), dst(0), ALU.subtract).then_inc(self.s_split, 1)


def cross_stage(nc, S, A, cross):
    GB = 2
    NG = NT // GB
    W = GB * P
    INNER = XHEADS * XDH
    MI = INNER // P
    UNITS = XHEADS // 4
    STEPS = GB * UNITS
    SCALE = XDH ** -0.5
    with Scope(nc, "xa") as c:
        cin = c.sb("cin", [P, 2, GB, CTX])
        ctxT = c.sb("ctxT", [P, 2, KC, W], BF16)
        kt = c.sb("kt", [P, 2, 2, MI, W], BF16)
        v = c.sb("v", [P, 2, 2, GB, INNER], BF16)
        qt = c.sb("qt", [P, 2, 2, MI, W], BF16)
        nk = c.sb("nk", [P, 1])
        nkb = c.sb("nkb", [P, 2, 2], BF16)
        nv = c.sb("nv", [P, XDH])
        lns = c.sb("lns", [P, D])
        lnb = c.sb("lnb", [P, D])
        nnull = c.sb("nnull", [P, 2, GB, XHEADS])
        mx = c.sb("mx", [P, 2, XHEADS])
        nmx = c.sb("nmx", [P, 2, XHEADS])
        dn = c.sb("dn", [P, 2, XHEADS])
        pn = c.sb("pn", [P, 2, XHEADS])
        sums = c.sb("sums", [P, 2, XHEADS])
        rsum = c.sb("rsum", [P, XHEADS])
        pexp = c.sb("pexp", [P, 2, 8, P])
        pt = c.sb("pt", [P, 2, 2, 4 * P], BF16)
        pnv = c.sb("pnv", [P, XHEADS, XDH])
        o = c.sb("o", [P, XHEADS, XDH])
        ot = c.sb("ot", [P, 2, MI, P], BF16)
        o2 = c.sb("o2", [P, NT, D])
        norm = Norm(S, c, z=o2[:, 0:2 * Norm.DEEP, :].rearrange("p (u t) d -> p u t d", t=2))
        raw = c.sb("raw", [P, NT, 6])
        tmp = c.sb("tmp", [P, NT])
        s_cin = [c.sem(f"cin{i}") for i in range(2)]
        (s_rows, s_nkb, s_xb, s_side, s_high, s_low, s_sc, s_max, s_mx, s_ex, s_t, s_th, s_tl, s_pv, s_dn, s_pn,
         s_pnv, s_osum, s_o, s_rs, s_dve, s_stats, s_var, s_root, s_t1, s_lns, s_res) = (
            c.sem(n) for n in ("rows", "nkb", "xb", "side", "high", "low", "sc", "max", "mx", "ex", "t", "th", "tl",
                               "pv", "dn", "pn", "pnv", "osum", "o", "rs", "dve", "stats", "var", "root", "t1",
                               "lns", "res"))
        ps = S.ps
        SCB, TRB, SIDEB, PVB = (0, 1), (2, 3), (4, 5), 6
        block = c.block()

        PROJ = [("ctx", 0), ("ctx", 1), ("q", 0), ("k", 0), ("q", 1), ("k", 1), ("q", 2), ("k", 2), ("q", 3), ("k", 3),
                ("null", 0), ("v", 0), ("v", 1), ("null", 1), ("v", 2), ("v", 3)]
        FIRST = ([("ctx", 0), ("ctx", 1)] + [(kind, i) for kind in "kv" for i in range(4)]
                 + [("q", i) for i in range(4)] + [("null", 0), ("null", 1)])
        assert sorted(FIRST) == sorted(PROJ) and norm.UNITS == 8
        NORM_FROM = 2
        ENDS = {0: ("out", 0, -2), 1: ("ot", 0, -1), 2: ("ot", 1, -1)}

        def ending(s):
            if s % UNITS not in ENDS:
                return []
            kind, i, e = ENDS[s % UNITS]
            return [(kind, i, s // UNITS + e)]

        def side(g, s):
            units = PROJ[2 * s:2 * s + 2] + ending(s)
            if isinstance(g, int):
                units = [u for u in units if (g < NG - 1 if len(u) == 2 else 2 * g + u[2] >= 0)]
            return units

        FULL = [u for s in range(STEPS) for u in PROJ[2 * s:2 * s + 2] + ending(s)]
        LAST_END = [("out", 0, -2), ("ot", 0, -1), ("ot", 1, -1), ("out", 0, -1)]
        ORDER = ([(-1, u) for u in FIRST] + [(g, u) for g in range(NG) for s in range(STEPS) for u in side(g, s)]
                 + [(NG, u) for u in LAST_END])
        any_kind = lambda u: True
        has_parts = lambda u: u[0] not in ("null", "out")

        def number(g, u, kind=any_kind):
            of_kind = [x for x in ORDER if kind(x[1])]
            if isinstance(g, int):
                return of_kind.index((g, u))
            return of_kind.index((1, u)) + len([x for x in FULL if kind(x)]) * (g - 1)

        def bank(g, u):
            assert len(FULL) % 2 == 0
            return ps[:, SIDEB[number(g if isinstance(g, int) else 1, u) % 2], :]

        def destination(u, j, part):
            kind, i = u[:2]
            if kind == "ctx":
                return ctxT[:, part, :, i * P:(i + 1) * P], KC
            if kind == "k":
                return kt[:, j, part, 2 * i:2 * i + 2, :], 2
            if kind == "q":
                return qt[:, j, part, 2 * i:2 * i + 2, :], 2
            if kind == "v":
                return v[:, j, part, i // 2, (i % 2) * 512:(i % 2) * 512 + 512].unsqueeze(1), 1
            return ot[:, part, 4 * i:4 * i + 4, :], 4

        def over_groups(eng, before, body):
            for i, u in enumerate(FIRST):
                before(i, u)
            body(0, 0, 0)
            with eng.Fori(0, NG // 2 - 1) as i:
                body(2 * i + 1, 1, i)
                body(2 * i + 2, 0, i + 1)
            body(NG - 1, 1, NG // 2 - 1)

        def unit(g, j, s):
            return g + s // STEPS, (j + s // STEPS) % 2, s % STEPS

        def exists(g, s):
            return not isinstance(g, int) or 0 <= g * STEPS + s < NG * STEPS

        @block.sync
        def _(sp):
            null = A["L1_xattn_null_kv"]
            for g in range(NG):
                if g >= 2:
                    sp.wait_ge(s_side, number(g - 3, ("ctx", 1)) + 1)
                sp.dma_start(cin[:, g % 2, :, :], A["ctx_2048"][GB * g:GB * g + GB].rearrange("b p d -> p b d")
                             ).then_inc(s_cin[g % 2], 16)
                if g == 0:
                    for h in range(2):
                        sp.dma_start(nk[h * XDH:(h + 1) * XDH, 0:1], null[0].rearrange("(p a) -> p a", a=1)).then_inc(s_rows, 16)
                    sp.dma_start(nv[:, :], null[1].partition_broadcast(P)).then_inc(s_rows, 16)
                    sp.dma_start(lns[:, :], A["L1_xattn_ln_scale"].partition_broadcast(P)).then_inc(s_rows, 16)
                    sp.dma_start(lnb[:, :], A["L1_xattn_ln_bias"].partition_broadcast(P)).then_inc(s_rows, 16)

        @block.gpsimd
        def _(pool):
            pool.wait_ge(s_lns, 2)
            pool.wait_ge(norm.s_z, NT)
            pool.tensor_tensor(S.x[:, :, :], S.x[:, :, :], lnb[:, :].unsqueeze(1).broadcast_to([P, NT, D]),
                               ALU.add).then_inc(s_xb, 1)

            def null_values(b, e):
                pool.wait_ge(s_pn, b + 1)
                wait_past_zero(pool, s_osum, b)
                pool.tensor_tensor(pnv[:, :, :], pn[:, e, :].unsqueeze(2).broadcast_to([P, XHEADS, XDH]),
                                   nv[:, :].unsqueeze(1).broadcast_to([P, XHEADS, XDH]), ALU.mult).then_inc(s_pnv, 1)

            null_values(0, 0)
            with pool.Fori(0, NT // 2 - 1) as i:
                null_values(2 * i + 1, 1)
                null_values(2 * i + 2, 0)
            null_values(NT - 1, 1)

        @block.scalar
        def _(act):
            def high(g, u, j):
                if not has_parts(u):
                    return
                dst, k = destination(u, j, 0)
                act.wait_ge(s_side, number(g, u) + 1)
                act.activation(dst, bank(g, u).rearrange("p (k s) -> p k s", k=k), ACT.Copy).then_inc(s_high, 1)

            def exps(g, j, s):
                e, u = s // UNITS, s % UNITS
                n = g * STEPS + s
                act.wait_ge(s_mx, g * (STEPS // 2) + s // 2 + 1)
                wait_past_zero(act, s_t, n - 3)
                for i in range(4):
                    h = 4 * u + i
                    ex = act.activation(pexp[:, (u // 2) % 2, h % 8, :], ps[:, SCB[h % 2], (h % 8) // 2 * P:((h % 8) // 2 + 1) * P],
                                        ACT.Exp, bias=nmx[:, e, h:h + 1], scale=SCALE, accum_out=sums[:, e, h:h + 1])
                ex.then_inc(s_ex, 1)
                if u == UNITS - 1:
                    act.wait_ge(s_dn, g * GB + e + 1)
                    act.activation(pn[:, e, :], dn[:, e, :], ACT.Exp).then_inc(s_pn, 1)

            def turned(g, s):
                act.wait_ge(s_t, g * STEPS + s + 1)
                act.activation(pt[:, s % 2, 0, :], ps[:, TRB[s % 2], :], ACT.Copy).then_inc(s_th, 1)

            def before(i, u):
                if i == NORM_FROM:
                    norm.root(act)
                high(-1, u, 0)
                if 0 <= i - NORM_FROM < norm.UNITS:
                    norm.high(act, i - NORM_FROM)
                if u == FIRST[-1]:
                    exps(0, 0, 0)
                    exps(0, 0, 1)

            def body(g, j, half):
                for s in range(STEPS):
                    turned(g, s)
                    units = side(g, s)
                    for u in units[:1]:
                        high(g, u, 1 - j)
                    if exists(g, s + 2):
                        exps(*unit(g, j, s + 2))
                    for u in units[1:]:
                        high(g, u, 1 - j)

            over_groups(act, before, body)
            for u in LAST_END:
                high(NG, u, 0)
            act.wait_ge(s_var, 1)
            act.activation(S.rstd[:, :], S.rstd[:, :], ACT.Sqrt).then_inc(s_root, 1)

        @block.tensor
        def _(pe):
            def side_unit(g, u, j, half):
                kind, i = u[:2]
                wait_past_zero(pe, s_low, number(g, u) - 1)
                out = bank(g, u)
                if kind == "ctx":
                    if i == 0:
                        pe.wait_ge(s_cin[j], 16 * (half + 1))
                    for k in range(KC):
                        mm = pe.transpose(out[:, k * P:k * P + P], cin[:, j, i, k * P:k * P + P], S.ident[:, :])
                elif kind in ("k", "q"):
                    if u == ("k", 0):
                        pe.wait_ge(s_low, number(g, ("ctx", 1)) + 1)
                    w, ks = (cross.kv, KC) if kind == "k" else (cross.q, KD)
                    for m in (2 * i, 2 * i + 1):
                        n = 0
                        for wp, ap in PASSES:
                            for k in range(ks):
                                rhs = ctxT[:, ap, k, :] if kind == "k" else S.zt[:, ap, k, ts((g + 1) * W, W)]
                                mm = pe.matmul(out[:, (m % 2) * W:(m % 2) * W + W], w[:, wp, k, m * P:m * P + P], rhs,
                                               start=(n == 0), stop=(n == 3 * ks - 1))
                                n += 1
                elif kind == "v":
                    n, at = 0, INNER + (i % 2) * 512
                    for wp, ap in PASSES:
                        for k in range(KC):
                            mm = pe.matmul(out, ctxT[:, ap, k, (i // 2) * P:(i // 2) * P + P], cross.kv[:, wp, k, at:at + 512],
                                           start=(n == 0), stop=(n == 3 * KC - 1))
                            n += 1
                elif kind == "null":
                    pe.wait_ge(s_low, number(g, ("q", 3)) + 1)
                    for m in range(MI):
                        for n, (wp, ap) in enumerate(PASSES):
                            mm = pe.matmul(out[:, 2 * m:2 * m + 2], qt[:, j, ap, m, i * P:i * P + P], nkb[:, wp, :],
                                           start=(n == 0), stop=(n == 2))
                elif kind == "ot":
                    pe.wait_ge(s_o, GB * g + u[2] + 1)
                    flat = o[:, :, :].rearrange("p h d -> p (h d)")
                    for k in range(4):
                        mm = pe.transpose(out[:, k * P:k * P + P], flat[:, (4 * i + k) * P:(4 * i + k + 1) * P], S.ident[:, :])
                else:
                    turned = (g - 1, ("ot", 1, 0)) if u[2] == -2 else (g, ("ot", 1, u[2]))
                    pe.wait_ge(s_low, number(*turned) + 1)
                    n = 0
                    for m in range(MI):
                        for wp, ap in PASSES:
                            mm = pe.matmul(out[:, 0:D], ot[:, ap, m, :], cross.out[:, wp, m, :],
                                           start=(n == 0), stop=(n == 3 * MI - 1))
                            n += 1
                mm.then_inc(s_side, 1)

            def scores(g, j, s):
                e, u = s // UNITS, s % UNITS
                wait_past_zero(pe, s_ex, g * STEPS + s)
                if isinstance(g, int) and g == 0:
                    pe.wait_ge(s_low, number(-1, ("q", 3)) + 1)
                else:
                    pe.wait_ge(s_low, number(g - 1, ("k", 1) if s == 0 else ("v", 0)) + 1)
                for m in range(2 * u, 2 * u + 4):
                    for n, (wp, ap) in enumerate(PASSES):
                        for p in range(2):
                            rows, at = slice(p * XDH, (p + 1) * XDH), (m % 4) * P
                            mm = pe.matmul(ps[:, SCB[p], at:at + P], qt[rows, j, ap, m, e * P:e * P + P],
                                           kt[rows, j, wp, m, e * P:e * P + P], start=(n == 0), stop=(n == 2))
                mm.then_inc(s_sc, 1)

            def turn(g, s):
                wait_past_zero(pe, s_tl, g * STEPS + s - 1)
                pe.wait_ge(s_ex, g * STEPS + s + 1)
                for i in range(4):
                    mm = pe.transpose(ps[:, TRB[s % 2], i * P:i * P + P], pexp[:, (s // 2) % 2, 4 * (s % 2) + i, :], S.ident[:, :])
                mm.then_inc(s_t, 1)

            def values(g, j, s):
                e, u = s // UNITS, s % UNITS
                pe.wait_ge(s_tl, g * STEPS + s + 1)
                if u == 0:
                    wait_past_zero(pe, s_osum, g * GB + e)
                    pe.wait_ge(s_low, number(g - 1, ("v", 2 * e + 1)) + 1)
                for i in range(4):
                    h = 4 * u + i
                    for n, (wp, ap) in enumerate(PASSES):
                        mm = pe.matmul(ps[:, PVB + h // 8, (h % 8) * XDH:(h % 8 + 1) * XDH], pt[:, u % 2, ap, i * P:(i + 1) * P],
                                       v[:, j, wp, e, h * XDH:(h + 1) * XDH], start=(n == 0), stop=(n == 2))
                mm.then_inc(s_pv, 1)

            def before(i, u):
                if u == ("q", 0):
                    pe.wait_ge(norm.s_lo, 1)
                if u == ("null", 0):
                    pe.wait_ge(s_nkb, 1)
                    pe.wait_ge(norm.s_lo, norm.UNITS)
                side_unit(-1, u, 0, 0)
                if 0 <= i - NORM_FROM < norm.UNITS:
                    norm.turn(pe, i - NORM_FROM)
                if u == FIRST[-1]:
                    scores(0, 0, 0)

            def body(g, j, half):
                for s in range(STEPS):
                    if s % 2 == 0 and exists(g, s + 2):
                        scores(*unit(g, j, s + 2))
                    turn(g, s)
                    units = side(g, s)
                    for u in units[:1]:
                        side_unit(g, u, 1 - j, half + j)
                    if exists(g, s - 1):
                        values(*unit(g, j, s - 1))
                    for u in units[1:]:
                        side_unit(g, u, 1 - j, half + j)

            over_groups(pe, before, body)
            values(NG - 1, 1, STEPS - 1)
            for u in LAST_END:
                side_unit(NG, u, 0, 0)

        @block.vector
        def _(dve):
            chain = Chain(dve, s_dve)
            norm.statistics(dve)
            AHEAD_Z = 1
            dve.wait_ge(s_rows, 80)
            chain.link(dve.memset(nkb[:, :, :], 0.0))
            for h in range(2):
                rows = slice(h * XDH, (h + 1) * XDH)
                chain.link(dve.tensor_copy(nkb[rows, 0, h:h + 1], nk[rows, :]))
                nb = dve.tensor_tensor(nkb[rows, 1, h:h + 1], nk[rows, :], nkb[rows, 0, h:h + 1], ALU.subtract)
            nb.then_inc(s_nkb, 1)
            dve.tensor_scalar(lns[:, :], lns[:, :], S.gates[:, 1:2], None, ALU.mult).then_inc(s_lns, 1)
            dve.tensor_scalar(lnb[:, :], lnb[:, :], S.gates[:, 1:2], None, ALU.mult).then_inc(s_lns, 1)

            def low(g, u, j):
                kind, i = u[:2]
                if has_parts(u):
                    dst, k = destination(u, j, 1)
                    dve.wait_ge(s_high, number(g, u, has_parts) + 1)
                    dve.tensor_tensor(dst, bank(g, u).rearrange("p (k s) -> p k s", k=k), destination(u, j, 0)[0],
                                      ALU.subtract).then_inc(s_low, 1)
                    return
                dve.wait_ge(s_side, number(g, u) + 1)
                if kind == "null":
                    dve.tensor_scalar(nnull[:, j, i, :], bank(g, u)[:, 0:XHEADS], -SCALE, None, ALU.mult).then_inc(s_low, 1)
                else:
                    tile = ts(GB * g + u[2], 1)
                    dve.tensor_copy(o2[:, tile, :].squeeze(1), bank(g, u)[:, 0:D]).then_inc(s_low, 1)
                    dve.wait_ge(s_low, number(g, u) + 1)
                    dve.bn_stats(raw[:, tile, :].squeeze(1), o2[:, tile, :].squeeze(1)).then_inc(s_stats, 1)

            def maxima(g, j, s):
                e, u = s // UNITS, s % UNITS
                n = g * (STEPS // 2) + s // 2
                dve.wait_ge(s_sc, n + 1)
                for p in range(2):
                    dve.tensor_reduce(mx[:, e, 4 * u + p:4 * u + 8:2], ps[:, SCB[p], :].rearrange("p (h k) -> p h k", h=4),
                                      AX.X, ALU.max).then_inc(s_max, 1)
                hs = slice(4 * u, 4 * u + 8)
                dve.wait_ge(s_max, 2 * n + 2)
                dve.scalar_tensor_tensor(out=nmx[:, e, hs], in0=mx[:, e, hs], scalar=-SCALE, in1=nnull[:, j, e, hs],
                                         op0=ALU.mult, op1=ALU.min).then_inc(s_mx, 1)
                if u == UNITS - 2:
                    dve.wait_ge(s_mx, n + 1)
                    dve.tensor_tensor(dn[:, e, :], nmx[:, e, :], nnull[:, j, e, :], ALU.subtract).then_inc(s_dn, 1)

            def turned(g, s):
                dve.wait_ge(s_th, g * STEPS + s + 1)
                dve.tensor_tensor(pt[:, s % 2, 1, :], ps[:, TRB[s % 2], :], pt[:, s % 2, 0, :], ALU.subtract).then_inc(s_tl, 1)

            def add_null(b, e):
                dve.wait_ge(s_pn, b + 1)
                dve.tensor_tensor(rsum[:, :], sums[:, e, :], pn[:, e, :], ALU.add).then_inc(s_rs, 1)
                dve.wait_ge(s_rs, 2 * b + 1)
                dve.reciprocal(rsum[:, :], rsum[:, :]).then_inc(s_rs, 1)
                dve.wait_ge(s_pnv, b + 1)
                dve.wait_ge(s_pv, (b + 1) * UNITS)
                dve.tensor_tensor(o[:, :, :], ps[:, PVB:PVB + 2, :].rearrange("p b (h d) -> p (b h) d", d=XDH),
                                  pnv[:, :, :], ALU.add).then_inc(s_osum, 1)

            def normalise(b):
                dve.wait_ge(s_osum, b + 1)
                dve.wait_ge(s_rs, 2 * b + 2)
                dve.tensor_tensor(o[:, :, :], o[:, :, :], rsum[:, :].unsqueeze(2).broadcast_to([P, XHEADS, XDH]),
                                  ALU.mult).then_inc(s_o, 1)

            def before(i, u):
                if i == NORM_FROM:
                    norm.moments(dve)
                    for step in range(AHEAD_Z):
                        norm.step(dve, step)
                if NORM_FROM <= i < NORM_FROM + norm.UNITS + norm.LAG - AHEAD_Z:
                    norm.step(dve, i - NORM_FROM + AHEAD_Z)
                low(-1, u, 0)
                if u == FIRST[-1]:
                    dve.wait_ge(s_low, len(FIRST))
                    maxima(0, 0, 0)

            def body(g, j, half):
                for s in range(STEPS):
                    turned(g, s)
                    if s == STEPS - 2 and exists(g, s + 2):
                        dve.wait_ge(s_low, number(g, ("null", 0)) + 1)
                    if s % 2 == 0 and exists(g, s + 2):
                        maxima(*unit(g, j, s + 2))
                    units = side(g, s)
                    for u in units[:1]:
                        low(g, u, 1 - j)
                    ended = s % UNITS == 0 and exists(g, s - 1)
                    if ended:
                        add_null(g * GB + s // UNITS - 1, (s // UNITS - 1) % 2)
                    for u in units[1:2]:
                        low(g, u, 1 - j)
                    if ended:
                        normalise(g * GB + s // UNITS - 1)
                    for u in units[2:]:
                        low(g, u, 1 - j)

            over_groups(dve, before, body)
            add_null(NT - 1, 1)
            normalise(NT - 1)
            for u in LAST_END:
                low(NG, u, 0)
            dve.wait_ge(s_stats, NT)
            combine_stats(dve, chain, raw, S.mean[:, :], S.rstd[:, :], tmp[:, :], D)
            dve.tensor_scalar(S.rstd[:, :], S.rstd[:, :], 1e-6, None, ALU.add).then_inc(s_var, 1)
            dve.wait_ge(s_root, 1)
            chain.link(dve.reciprocal(S.rstd[:, :], S.rstd[:, :]))
            dve.wait_ge(s_xb, 1)
            for b in range(NT + 1):
                if b < NT:
                    dve.scalar_tensor_tensor(out=o2[:, b, :], in0=o2[:, b, :], scalar=S.mean[:, b:b + 1],
                                             in1=lns[:, :], op0=ALU.subtract, op1=ALU.mult).then_inc(s_t1, 1)
                if b > 0:
                    dve.wait_ge(s_t1, b)
                    dve.scalar_tensor_tensor(out=S.x[:, b - 1, :], in0=o2[:, b - 1, :], scalar=S.rstd[:, b - 1:b],
                                             in1=S.x[:, b - 1, :], op0=ALU.mult, op1=ALU.add).then_inc(s_res, 1)


def latent_stage(nc, S, A):
    U = LHEADS // 4
    LAT = LHEADS * LDH
    SCALE = LDH ** -0.5
    with Scope(nc, "la") as c:
        wraw = c.sb("wraw", [P, KD, D + 2 * LAT])
        w = c.sb("w", [P, 2, KD, 3, LAT], BF16)
        ow = c.sb("ow", [LAT, D])
        brow = c.sb("brow", [4, P])
        bcol = c.sb("bcol", [P, 4])
        vrow = c.sb("vrow", [P, LAT])
        ones = c.sb("ones", [P, LHEADS])
        own = c.sb("own", [P, LHEADS])
        qT = c.sb("qT", [P, 2, P])
        kT = c.sb("kT", [P, 2, P])
        km = c.sb("km", [P, 2, LHEADS, P])
        vf = c.sb("vf", [P, 2, LAT])
        v = c.sb("v", [P, 2, 2, LAT], BF16)
        mx = c.sb("mx", [P, 2, LHEADS])
        nmx = c.sb("nmx", [P, 2, LHEADS])
        sums = c.sb("sums", [P, 2, LHEADS])
        rsum = c.sb("rsum", [P, 2, LHEADS])
        pexp = c.sb("pexp", [P, 2, 4, P])
        pt = c.sb("pt", [P, 2, 2, 4 * P], BF16)
        ao = c.sb("ao", [P, 2, LHEADS, LDH])
        aoT = c.sb("aoT", [P, 2, P])
        (s_w, s_b, s_pool, s_split, s_bT, s_bcol, s_pj, s_k, s_v, s_vp, s_km, s_sc, s_max, s_mx, s_ex, s_t, s_th, s_tl,
         s_pv, s_rs, s_ao, s_aoT, s_aoc, s_mla, s_mh, s_ml) = (
            c.sem(n) for n in ("w", "b", "pool", "split", "bT", "bcol", "pj", "k", "v", "vp", "km", "sc", "max", "mx",
                               "ex", "t", "th", "tl", "pv", "rs", "ao", "aoT", "aoc", "mla", "mh", "ml"))
        ps = S.ps
        SCB, TRB, PJB, PVB, OUTB = (0, 1), (2, 3), 4, (5, 6), 7

        def exists(b, u=0):
            return not isinstance(b, int) or 0 <= b * U + u < NT * U

        def unit(b, j, u):
            return b + u // U, (j + u // U) % 2, u % U

        def over_entries(eng, body):
            body(0, 0)
            body(1, 1)
            with eng.Fori(1, NT // 2 - 1) as i:
                body(2 * i, 0)
                body(2 * i + 1, 1)
            body(NT - 2, 0)
            body(NT - 1, 1)

        block = c.block()

        @block.sync
        def _(sp):
            rows = lambda m: m.rearrange("(k p) c -> p k c", p=P)
            sp.dma_start(wraw[:, :, 0:D], rows(A["L1_ffn_q_w"])).then_inc(s_w, 16)
            sp.dma_start(wraw[:, :, D:D + LAT], rows(A["L1_ffn_k_w"])).then_inc(s_w, 16)
            sp.dma_start(wraw[:, :, D + LAT:], rows(A["L1_ffn_v_w"])).then_inc(s_w, 16)
            sp.dma_start(brow[0:1, :].rearrange("a (h r) -> a h r", r=LDH),
                         A["L1_ffn_q_b"].rearrange("(a h r) -> a h r", a=1, h=LHEADS)[:, :, 0:LDH]).then_inc(s_b, 16)
            sp.dma_start(brow[1:2, :], A["L1_ffn_k_b"].rearrange("(a n) -> a n", a=1)).then_inc(s_b, 16)
            sp.dma_start(brow[2:4, :], A["L1_ffn_o_b"].rearrange("(a n) -> a n", a=2)).then_inc(s_b, 16)
            sp.dma_start(vrow[:, :], A["L1_ffn_v_b"].partition_broadcast(P)).then_inc(s_b, 16)
            sp.dma_start(ow[:, :], A["L1_ffn_o_w"][0:LAT, :]).then_inc(s_b, 16)

        @block.gpsimd
        def _(pool):
            chain = Chain(pool, s_pool)
            chain.link(pool.memset(ones[:, :], 1.0))
            chain.link(pool.affine_select(out=own[:, :], in_=ones[:, :], compare_op=ALU.is_ge, fill=0.0,
                                          base=0, pattern=[[-LDH, LHEADS]], channel_multiplier=1))
            chain.link(pool.affine_select(out=own[:, :], in_=own[:, :], compare_op=ALU.is_ge, fill=0.0,
                                          base=LDH - 1, pattern=[[LDH, LHEADS]], channel_multiplier=-1))
            chain.link(pool.memset(km[:, :, :, :], 0.0))
            with pool.Fori(0, NT // 2) as i:
                for j in range(2):
                    pool.wait_ge(s_k, 2 * i + j + 1)
                    for u in range(U):
                        rows, hs = slice(32 * u, 32 * u + 32), slice(4 * u, 4 * u + 4)
                        pool.tensor_tensor(km[rows, j, hs, :], kT[rows, j, :].unsqueeze(1).broadcast_to([32, 4, P]),
                                           own[rows, hs].unsqueeze(2).broadcast_to([32, 4, P]), ALU.mult).then_inc(s_km, 1)

        @block.scalar
        def _(act):
            def exps(b, j, u):
                n = b * U + u
                act.wait_ge(s_mx, n + 1)
                wait_past_zero(act, s_t, n - 1)
                for i in range(4):
                    h = 4 * u + i
                    ex = act.activation(pexp[:, u % 2, i, :], ps[:, SCB[u % 2], i * P:(i + 1) * P], ACT.Exp,
                                        bias=nmx[:, j, h:h + 1], scale=SCALE, accum_out=sums[:, j, h:h + 1])
                ex.then_inc(s_ex, 1)

            def turned(b, j, u):
                act.wait_ge(s_t, b * U + u + 1)
                act.activation(pt[:, u % 2, 0, :], ps[:, TRB[u % 2], :], ACT.Copy).then_inc(s_th, 1)

            def output(b):
                act.wait_ge(s_mla, b + 1)
                for k in range(KD):
                    cp = act.activation(S.zt[:, 0, k, ts(b * P, P)], ps[:, OUTB, (1 + k) * P:(2 + k) * P], ACT.Identity,
                                        bias=bcol[:, 2 + k:3 + k])
                cp.then_inc(s_mh, 1)

            def body(b, j):
                for u in range(U):
                    if exists(b, u + 1):
                        exps(*unit(b, j, u + 1))
                    if u == 0 and exists(b - 2):
                        output(b - 2)
                    turned(b, j, u)

            act.wait_ge(s_bcol, 1)
            exps(0, 0, 0)
            over_entries(act, body)
            output(NT - 2)
            output(NT - 1)

        @block.tensor
        def _(pe):
            def project(b, j):
                wait_past_zero(pe, s_v, b)
                for which in range(3):
                    n = 0
                    for wp, ap in PASSES:
                        for k in range(KD):
                            wk, zk = w[:, wp, k, which, :], S.zt[:, ap, k, ts(b * P, P)]
                            lhs, rhs = (zk, wk) if which == 2 else (wk, zk)
                            mm = pe.matmul(ps[:, PJB, which * P:which * P + P], lhs, rhs, start=(n == 0), stop=(n == 3 * KD - 1))
                            n += 1
                mm.then_inc(s_pj, 1)

            def scores(b, j, u):
                pe.wait_ge(s_km, b * U + u + 1)
                wait_past_zero(pe, s_ex, b * U + u - 1)
                pe.matmul(ps[:, SCB[u % 2], :], qT[:, j, :], km[:, j, 4 * u:4 * u + 4, :].rearrange("p h k -> p (h k)"),
                          start=True, stop=True).then_inc(s_sc, 1)

            def turn(b, j, u):
                wait_past_zero(pe, s_tl, b * U + u - 1)
                pe.wait_ge(s_ex, b * U + u + 1)
                for i in range(4):
                    mm = pe.transpose(ps[:, TRB[u % 2], i * P:i * P + P], pexp[:, u % 2, i, :], S.ident[:, :])
                mm.then_inc(s_t, 1)

            def values(b, j, u):
                if u == 0:
                    wait_past_zero(pe, s_ao, b - 1)
                    pe.wait_ge(s_v, b + 1)
                pe.wait_ge(s_tl, b * U + u + 1)
                for i in range(4):
                    h = 4 * u + i
                    for p, (wp, ap) in enumerate(PASSES):
                        mm = pe.matmul(ps[:, PVB[j], h * LDH:(h + 1) * LDH], pt[:, u % 2, ap, i * P:i * P + P],
                                       v[:, j, wp, h * LDH:(h + 1) * LDH], start=(p == 0), stop=(p == 2))
                mm.then_inc(s_pv, 1)

            def turn_out(b, j):
                pe.wait_ge(s_ao, b + 1)
                wait_past_zero(pe, s_ml, b)
                pe.transpose(ps[:, OUTB, 0:P], ao[:, j, :, :].rearrange("p h d -> p (h d)"), S.ident[:, :]).then_inc(s_aoT, 1)

            def output(b, j):
                pe.wait_ge(s_aoc, b + 1)
                for k in range(KD):
                    mm = pe.matmul(ps[:, OUTB, (1 + k) * P:(2 + k) * P], ow[:, k * P:k * P + P], aoT[:, j, :],
                                   start=True, stop=True)
                mm.then_inc(s_mla, 1)

            def body(b, j):
                for u in range(U):
                    turn(b, j, u)
                    if exists(b, u + 2):
                        scores(*unit(b, j, u + 2))
                    if u > 0:
                        values(b, j, u - 1)
                    elif exists(b - 1):
                        values(b - 1, 1 - j, U - 1)
                    if u == 0 and exists(b + 1):
                        project(b + 1, 1 - j)
                    if u == 1 and exists(b - 1):
                        turn_out(b - 1, 1 - j)
                    if u == 3 and exists(b - 1):
                        output(b - 1, 1 - j)

            pe.wait_ge(s_b, 80)
            pe.transpose(ps[:, 0, 0:4], brow[:, :], S.ident[0:4, 0:4]).then_inc(s_bT, 1)
            pe.wait_ge(s_split, 6)
            project(0, 0)
            pe.wait_ge(s_bcol, 1)
            scores(0, 0, 0)
            scores(0, 0, 1)
            over_entries(pe, body)
            values(NT - 1, 1, U - 1)
            turn_out(NT - 1, 1)
            output(NT - 1, 1)

        @block.vector
        def _(dve):
            dve.wait_ge(s_w, 48)
            parts = [wraw[:, :, 0:D].rearrange("p k (h r) -> p k h r", r=2 * LDH)[:, :, :, 0:LDH],
                     wraw[:, :, D:D + LAT].rearrange("p k (h r) -> p k h r", r=LDH),
                     wraw[:, :, D + LAT:].rearrange("p k (h r) -> p k h r", r=LDH)]
            for i, part in enumerate(parts):
                for k in range(KD):
                    hi, lo = (w[:, a, k, i, :].rearrange("p (h r) -> p h r", r=LDH) for a in range(2))
                    dve.tensor_copy(hi, part[:, k, :, :]).then_inc(s_vp, 1)
                    dve.wait_ge(s_vp, KD * i + k + 1)
                    dve.tensor_tensor(lo, part[:, k, :, :], hi, ALU.subtract).then_inc(s_split, 1)
            dve.wait_ge(s_bT, 1)
            dve.tensor_copy(bcol[:, :], ps[:, 0, 0:4]).then_inc(s_bcol, 1)
            dve.wait_ge(s_bcol, 1)
            SPLITS = 3 * KD

            def projected_qk(b, j):
                dve.wait_ge(s_pj, b + 1)
                dve.tensor_scalar(kT[:, j, :], ps[:, PJB, P:2 * P], bcol[:, 1:2], None, ALU.add)
                dve.tensor_scalar(qT[:, j, :], ps[:, PJB, 0:P], bcol[:, 0:1], None, ALU.add).then_inc(s_k, 1)

            def projected_v(b, j):
                dve.tensor_tensor(vf[:, j, :], ps[:, PJB, 2 * P:3 * P], vrow[:, :], ALU.add).then_inc(s_vp, 1)
                dve.wait_ge(s_vp, 2 * b + 1 + SPLITS)
                dve.tensor_copy(v[:, j, 0, :], vf[:, j, :]).then_inc(s_vp, 1)
                dve.wait_ge(s_vp, 2 * b + 2 + SPLITS)
                dve.tensor_tensor(v[:, j, 1, :], vf[:, j, :], v[:, j, 0, :], ALU.subtract).then_inc(s_v, 1)

            def maxima(b, j, u):
                hs = slice(4 * u, 4 * u + 4)
                dve.wait_ge(s_sc, b * U + u + 1)
                dve.tensor_reduce(mx[:, j, hs], ps[:, SCB[u % 2], :].rearrange("p (h k) -> p h k", h=4), AX.X,
                                  ALU.max).then_inc(s_max, 1)
                dve.wait_ge(s_max, b * U + u + 1)
                dve.tensor_scalar(nmx[:, j, hs], mx[:, j, hs], -SCALE, None, ALU.mult).then_inc(s_mx, 1)

            def turned(b, j, u):
                dve.wait_ge(s_th, b * U + u + 1)
                dve.tensor_tensor(pt[:, u % 2, 1, :], ps[:, TRB[u % 2], :], pt[:, u % 2, 0, :], ALU.subtract).then_inc(s_tl, 1)

            def normalise(b, j):
                dve.reciprocal(rsum[:, j, :], sums[:, j, :]).then_inc(s_rs, 1)
                dve.wait_ge(s_rs, b + 1)
                dve.wait_ge(s_pv, b * U + U)
                dve.tensor_tensor(ao[:, j, :, :], ps[:, PVB[j], 0:LAT].rearrange("p (h d) -> p h d", d=LDH),
                                  rsum[:, j, :].unsqueeze(2).broadcast_to([P, LHEADS, LDH]), ALU.mult).then_inc(s_ao, 1)

            def copy_out(b, j):
                dve.wait_ge(s_aoT, b + 1)
                dve.tensor_copy(aoT[:, j, :], ps[:, OUTB, 0:P]).then_inc(s_aoc, 1)

            def output(b):
                dve.wait_ge(s_mh, b + 1)
                for k in range(KD):
                    q = dve.scalar_tensor_tensor(out=S.zt[:, 1, k, ts(b * P, P)], in0=ps[:, OUTB, (1 + k) * P:(2 + k) * P],
                                                 scalar=bcol[:, 2 + k:3 + k], in1=S.zt[:, 0, k, ts(b * P, P)],
                                                 op0=ALU.add, op1=ALU.subtract)
                q.then_inc(s_ml, 1)

            def body(b, j):
                for u in range(U):
                    if exists(b, u + 2):
                        maxima(*unit(b, j, u + 2))
                    if u == 2 and exists(b - 1):
                        copy_out(b - 1, 1 - j)
                    if u == 0 and exists(b - 2):
                        output(b - 2)
                    turned(b, j, u)
                    if u == 0 and exists(b - 1):
                        normalise(b - 1, 1 - j)
                    if u == 0 and exists(b + 1):
                        projected_qk(b + 1, 1 - j)
                    if u == 1 and exists(b + 1):
                        projected_v(b + 1, 1 - j)

            projected_qk(0, 0)
            projected_v(0, 0)
            maxima(0, 0, 0)
            maxima(0, 0, 1)
            over_entries(dve, body)
            normalise(NT - 1, 1)
            output(NT - 2)
            copy_out(NT - 1, 1)
            output(NT - 1)


def build(nc, A, out):
    with Scope(nc, "g") as g:
        S = Shared(nc, g)
        depool_stage(nc, S, A)
        with Scope(nc, "r1") as weights:
            cross = CrossWeights(nc, weights, A["L1_xattn_Wq"], A["L1_xattn_Wkv"], A["L1_xattn_Wout"])
            with Scope(nc, "r0") as experts:
                ring = Ring(nc, experts, [A["L0_ffn_W1"], A["L0_ffn_W0"], A["L0_ffn_W2"]])
                gate_stage(nc, S, "g0", A["L0_ffn_Wg"], A["L0_ffn_bg"], A["L0_ffn_b2"], 2, False,
                           prefetch=ring, norm_first=True)
                expert_stage(nc, S, "e0", ring, A["L0_ffn_b0"], A["L0_ffn_b1"], 1024, following=cross)
            cross_stage(nc, S, A, cross)
        with Scope(nc, "r2") as experts:
            ring = Ring(nc, experts, [A["L1_ffn_w1"], A["L1_ffn_w2"]])
            norm_stage(nc, S, "n2", prefetch=ring, residual=3)
            latent_stage(nc, S, A)
            gate_stage(nc, S, "g1", A["L1_ffn_router_w"], A["L1_ffn_router_b"], A["L1_ffn_b2"], 3, True, 0.3)
            expert_stage(nc, S, "e1", ring, None, A["L1_ffn_b1"], 512, out=out)


_INS = ["x", "ctx_2048", "mask_BxS2_if0", "g_xattn", "g_ffn", "L0_xattn_W_in", "L0_xattn_b_in", "L0_xattn_g_res",
        "L0_xattn_g_init", "L0_ffn_Wg", "L0_ffn_bg", "L0_ffn_W0", "L0_ffn_b0", "L0_ffn_W1", "L0_ffn_b1", "L0_ffn_W2",
        "L0_ffn_b2", "L1_xattn_Wq", "L1_xattn_Wkv", "L1_xattn_null_kv", "L1_xattn_Wout", "L1_xattn_ln_scale",
        "L1_xattn_ln_bias", "L1_ffn_q_w", "L1_ffn_q_b", "L1_ffn_k_w", "L1_ffn_k_b", "L1_ffn_v_w", "L1_ffn_v_b",
        "L1_ffn_o_w", "L1_ffn_o_b", "L1_ffn_router_w", "L1_ffn_router_b", "L1_ffn_w1", "L1_ffn_b1", "L1_ffn_w2",
        "L1_ffn_b2"]


def kernel(**inputs):
    import numpy as _np
    import concourse.bacc as _bacc
    from concourse import mybir as _mybir
    from concourse.bass_utils import run_bass_kernel_spmd as _run

    nc = _bacc.Bacc("TRN2", target_bir_lowering=False, num_devices=1)
    arrays, args = {}, {}
    for name in _INS:
        a = _np.ascontiguousarray(inputs[name])
        arrays[f"in_{name}_dram"] = a
        args[name] = nc.dram_tensor(f"in_{name}_dram", a.shape, _mybir.dt.from_np(a.dtype), kind="ExternalInput").ap()
    out = nc.dram_tensor("out_0_dram", (NT, P, D), F32, kind="ExternalOutput").ap()
    build(nc, args, out)
    r = _run(nc, [arrays], core_ids=[0])
    return r.results[0]["out_0_dram"]
```
